# Optimizing a Trainium2 kernel written in Bass

```python
import numpy as np
import jax
import jax.numpy as jnp

def _softmax(x, axis=-1):
    return jax.nn.softmax(x, axis=axis)

def _gelu(x):
    return jax.nn.gelu(x, approximate=True)

def _silu(x):
    return jax.nn.silu(x)

def _sigmoid(x):
    return jax.nn.sigmoid(x)

def _layernorm(x, axis=-1, eps=1e-05):
    m = jnp.mean(x, axis=axis, keepdims=True)
    v = jnp.var(x, axis=axis, keepdims=True)
    return (x - m) / jnp.sqrt(v + eps)

def _scatter_add(tgt, idx, src, axis=0):
    return tgt.at[idx].add(src)

def _segment_sum(src, seg, n):
    return jax.ops.segment_sum(src, seg, n)
kernel_name = 'mk_vit_tower_d2_tok_img1024_r4_36c0ed'

def setup_inputs(seed: int=0):
    np.random.seed(seed)
    _w = jnp.asarray

    def _rec_inputs():
        import jax
        import jax.numpy as jnp
        _rk = jax.random.key(seed)
        x = -0.000169711 + 1.00022 * jax.random.normal(jax.random.fold_in(_rk, 1), (64, 3, 84, 84), jnp.float32)
        return x
    x = _rec_inputs()

    def _L0_tok_setup():
        import jax, jax.numpy as jnp
        import numpy as np
        C = 256
        H8 = 8
        DH = C // H8
        PS = 14
        CS = 3
        IMG = 168
        B = 4

        def _ln(x, g, b):
            mu = jnp.mean(x, axis=-1, keepdims=True)
            xc = x - mu
            var = jnp.mean(xc * xc, axis=-1, keepdims=True)
            return xc * jax.lax.rsqrt(var + 1e-05) * g + b

        def _forward(pixel_values, conv_w, class_emb, la_ln_q_g, la_ln_q_b, la_wq, la_ln_kv_g, la_ln_kv_b, la_wkv, la_proj_w, la_proj_b, ga_ln_q_g, ga_ln_q_b, ga_wq, ga_ln_kv_g, ga_ln_kv_b, ga_wkv, ga_proj_w, ga_proj_b, mod_w, mod_b):
            b = pixel_values.shape[0]
            pe = jax.lax.conv_general_dilated(pixel_values, conv_w, (PS, PS), 'VALID', dimension_numbers=('NCHW', 'OIHW', 'NCHW'))
            HP = pe.shape[2]
            h = HP // CS
            hw, N = (h * h, CS * CS)
            scale = C ** (-0.5)
            grid = pe.reshape(b, C, h, CS, h, CS)
            red = grid.mean(axis=(3, 5)).reshape(b, C, hw).transpose(0, 2, 1)
            win = grid.transpose(0, 2, 4, 3, 5, 1).reshape(b, hw, N, C)
            q = _ln(red, la_ln_q_g, la_ln_q_b) @ la_wq
            q = q.reshape(b, hw, H8, DH).transpose(0, 2, 1, 3)
            kv = _ln(win, la_ln_kv_g, la_ln_kv_b) @ la_wkv
            kv = kv.reshape(b, hw, N, 2, H8, DH).transpose(3, 0, 4, 1, 2, 5)
            k_, v_ = (kv[0], kv[1])
            attn = jax.nn.softmax(jnp.einsum('bhnd,bhnkd->bhnk', q * scale, k_), axis=-1)
            agg = jnp.einsum('bhnk,bhnkd->bhnd', attn, v_)
            agg = agg.transpose(0, 2, 1, 3).reshape(b, hw, C)
            local_out = red + agg @ la_proj_w + la_proj_b
            cls = jnp.broadcast_to(class_emb, (b, 1, C))
            gq = (_ln(cls, ga_ln_q_g, ga_ln_q_b) @ ga_wq).reshape(b, H8, DH)
            gkv = _ln(local_out, ga_ln_kv_g, ga_ln_kv_b) @ ga_wkv
            gkv = gkv.reshape(b, hw, 2, H8, DH).transpose(2, 0, 3, 1, 4)
            gk, gv = (gkv[0], gkv[1])
            gattn = jax.nn.softmax(jnp.einsum('bhd,bhnd->bhn', gq * scale, gk), axis=-1)
            gagg = jnp.einsum('bhn,bhnd->bhd', gattn, gv).reshape(b, 1, C)
            cls_out = cls + gagg @ ga_proj_w + ga_proj_b
            patch_out = local_out @ mod_w + mod_b
            return jnp.concatenate([patch_out, cls_out], axis=1)
        key = jax.random.key(seed)
        ks = jax.random.split(key, 16)
        nrm = lambda k, shape: jax.random.normal(k, shape, jnp.float32) * 0.02
        return {'pixel_values': jax.random.normal(ks[0], (B, 3, IMG, IMG), jnp.float32), 'pixel_masks': jnp.ones((B, 1, IMG, IMG), jnp.float32), 'conv_w': nrm(ks[1], (C, 3, PS, PS)), 'class_emb': nrm(ks[2], (C,)), 'la_ln_q_g': jnp.ones((C,)), 'la_ln_q_b': jnp.zeros((C,)), 'la_wq': nrm(ks[3], (C, C)), 'la_ln_kv_g': jnp.ones((C,)), 'la_ln_kv_b': jnp.zeros((C,)), 'la_wkv': nrm(ks[4], (C, 2 * C)), 'la_proj_w': nrm(ks[5], (C, C)), 'la_proj_b': jnp.zeros((C,)), 'ga_ln_q_g': jnp.ones((C,)), 'ga_ln_q_b': jnp.zeros((C,)), 'ga_wq': nrm(ks[6], (C, C)), 'ga_ln_kv_g': jnp.ones((C,)), 'ga_ln_kv_b': jnp.zeros((C,)), 'ga_wkv': nrm(ks[7], (C, 2 * C)), 'ga_proj_w': nrm(ks[8], (C, C)), 'ga_proj_b': jnp.zeros((C,)), 'mod_w': nrm(ks[9], (C, C)), 'mod_b': jnp.zeros((C,))}
    _L0_tok_all = _L0_tok_setup()
    _L0_tok_in = {k: v for k, v in _L0_tok_all.items() if k in ('pixel_masks', 'conv_w', 'class_emb', 'la_ln_q_g', 'la_ln_q_b', 'la_wq', 'la_ln_kv_g', 'la_ln_kv_b', 'la_wkv', 'la_proj_w', 'la_proj_b', 'ga_ln_q_g', 'ga_ln_q_b', 'ga_wq', 'ga_ln_kv_g', 'ga_ln_kv_b', 'ga_wkv', 'ga_proj_w', 'ga_proj_b', 'mod_w', 'mod_b')}
    del _L0_tok_all

    def _L0_attn_setup():
        import math
        import jax, jax.numpy as jnp
        import numpy as np
        N_HEAD = 16

        def quant_weight(w):
            scale = jnp.maximum(jnp.mean(jnp.abs(w)), 1e-08)
            w_quant = jnp.clip(jnp.round(w / scale), -2.0, 2.0)
            return jax.lax.stop_gradient(w_quant * scale - w) + w
        key = jax.random.key(seed)
        k1, k2, k3 = jax.random.split(key, 3)
        C = 256
        x = jax.random.normal(k1, (2, 512, C), dtype=jnp.float32)
        w_attn = jax.random.normal(k2, (3 * C, C), dtype=jnp.float32) * (1.0 / math.sqrt(C))
        w_proj = jax.random.normal(k3, (C, C), dtype=jnp.float32) * (1.0 / math.sqrt(C))
        return {'x': x, 'w_attn': w_attn, 'w_proj': w_proj}
    _L0_attn_all = _L0_attn_setup()
    _L0_attn_in = {k: v for k, v in _L0_attn_all.items() if k in ('w_attn', 'w_proj')}
    del _L0_attn_all

    def _L0_ffn_setup():
        import jax, jax.numpy as jnp
        import numpy as np
        TOP_K = 2
        NUM_EXPERTS = 8
        key = jax.random.key(seed)
        ks = jax.random.split(key, 8)
        h, d, ds, E = (256, 128, 256, NUM_EXPERTS)
        s = 1.0 / np.sqrt(h)
        return {'x': jax.random.normal(ks[0], (2, 512, h), jnp.float32), 'router': jax.random.normal(ks[1], (h, E), jnp.float32) * s, 'experts_gate': jax.random.normal(ks[2], (E, h, d), jnp.float32) * s, 'experts_up': jax.random.normal(ks[3], (E, h, d), jnp.float32) * s, 'experts_down': jax.random.normal(ks[4], (E, d, h), jnp.float32) * (1.0 / np.sqrt(d)), 'shared_gate': jax.random.normal(ks[5], (h, ds), jnp.float32) * s, 'shared_up': jax.random.normal(ks[6], (h, ds), jnp.float32) * s, 'shared_down': jax.random.normal(ks[7], (ds, h), jnp.float32) * (1.0 / np.sqrt(ds))}
    _L0_ffn_all = _L0_ffn_setup()
    _L0_ffn_in = {k: v for k, v in _L0_ffn_all.items() if k in ('router', 'experts_gate', 'experts_up', 'experts_down', 'shared_gate', 'shared_up', 'shared_down')}
    del _L0_ffn_all

    def _L1_attn_setup():
        import math
        import jax, jax.numpy as jnp
        import numpy as np
        D_MODEL = 256
        N_HEADS = 16
        HEAD_DIM = D_MODEL // N_HEADS
        ROPE_THETA = 10000.0

        def _apply_rope(t, offset=0):
            B, H, T, Dh = t.shape
            inv_freq = 1.0 / ROPE_THETA ** (jnp.arange(0, Dh, 2, dtype=jnp.float32) / Dh)
            pos = jnp.arange(T, dtype=jnp.float32) + offset
            ang = pos[:, None] * inv_freq[None, :]
            cos = jnp.concatenate([jnp.cos(ang), jnp.cos(ang)], axis=-1)
            sin = jnp.concatenate([jnp.sin(ang), jnp.sin(ang)], axis=-1)
            t1, t2 = (t[..., :Dh // 2], t[..., Dh // 2:])
            rot = jnp.concatenate([-t2, t1], axis=-1)
            return t * cos + rot * sin

        def _forward(x, Wq, Wk, Wv, Wo):
            B, T, _ = x.shape
            scale = 1.0 / math.sqrt(HEAD_DIM)

            def split_heads(y):
                return y.reshape(B, T, N_HEADS, HEAD_DIM).transpose(0, 2, 1, 3)
            q = split_heads(x @ Wq.T)
            k = split_heads(x @ Wk.T)
            v = split_heads(x @ Wv.T)
            q = _apply_rope(q)
            k = _apply_rope(k)
            scores = jnp.einsum('bhtd,bhsd->bhts', q, k) * scale
            causal = jnp.triu(jnp.ones((T, T), dtype=bool), k=1)
            scores = jnp.where(causal[None, None], -jnp.inf, scores)
            attn = jax.nn.softmax(scores, axis=-1)
            attn = jnp.nan_to_num(attn, nan=0.0)
            out = jnp.einsum('bhts,bhsd->bhtd', attn, v)
            out = out.transpose(0, 2, 1, 3).reshape(B, T, N_HEADS * HEAD_DIM)
            return out @ Wo.T
        key = jax.random.key(seed)
        ks = jax.random.split(key, 5)
        B, T = (4, 512)
        w_scale = math.sqrt(2.0 / (D_MODEL + D_MODEL))
        return {'x': jax.random.normal(ks[0], (B, T, D_MODEL), dtype=jnp.float32), 'Wq': jax.random.normal(ks[1], (D_MODEL, D_MODEL), dtype=jnp.float32) * w_scale, 'Wk': jax.random.normal(ks[2], (D_MODEL, D_MODEL), dtype=jnp.float32) * w_scale, 'Wv': jax.random.normal(ks[3], (D_MODEL, D_MODEL), dtype=jnp.float32) * w_scale, 'Wo': jax.random.normal(ks[4], (D_MODEL, D_MODEL), dtype=jnp.float32) * w_scale}
    _L1_attn_all = _L1_attn_setup()
    _L1_attn_in = {k: v for k, v in _L1_attn_all.items() if k in ('Wq', 'Wk', 'Wv', 'Wo')}
    del _L1_attn_all

    def _L1_ffn_setup():
        import jax, jax.numpy as jnp
        import numpy as np
        HIDDEN = 256
        INNER = 1024

        def _weight_quant(w):
            scale = 1.0 / jnp.clip(jnp.mean(jnp.abs(w)), 1e-05)
            wq = jnp.clip(jnp.round(w * scale), -1.0, 1.0) / scale
            return w + jax.lax.stop_gradient(wq - w)

        def _act_quant(x):
            scale = 127.0 / jnp.clip(jnp.max(jnp.abs(x), axis=-1, keepdims=True), 1e-05)
            xq = jnp.clip(jnp.round(x * scale), -128.0, 127.0) / scale
            return x + jax.lax.stop_gradient(xq - x)

        def _bitlinear(x, w):
            return jnp.einsum('bsi,oi->bso', _act_quant(x), _weight_quant(w))
        key = jax.random.key(seed)
        k0, k1, k2, k3 = jax.random.split(key, 4)
        x = jax.random.normal(k0, (4, 512, HIDDEN), dtype=jnp.float32)
        w_gate = jax.random.normal(k1, (INNER, HIDDEN), dtype=jnp.float32) / np.sqrt(HIDDEN)
        w_up = jax.random.normal(k2, (INNER, HIDDEN), dtype=jnp.float32) / np.sqrt(HIDDEN)
        w_down = jax.random.normal(k3, (HIDDEN, INNER), dtype=jnp.float32) / np.sqrt(INNER)
        return {'x': x, 'w_gate': w_gate, 'w_up': w_up, 'w_down': w_down}
    _L1_ffn_all = _L1_ffn_setup()
    _L1_ffn_in = {k: v for k, v in _L1_ffn_all.items() if k in ('w_gate', 'w_up', 'w_down')}
    del _L1_ffn_all
    return {'x': x, 'L0_tok_pixel_masks': _L0_tok_in['pixel_masks'], 'L0_tok_conv_w': _L0_tok_in['conv_w'], 'L0_tok_class_emb': _L0_tok_in['class_emb'], 'L0_tok_la_ln_q_g': _L0_tok_in['la_ln_q_g'], 'L0_tok_la_ln_q_b': _L0_tok_in['la_ln_q_b'], 'L0_tok_la_wq': _L0_tok_in['la_wq'], 'L0_tok_la_ln_kv_g': _L0_tok_in['la_ln_kv_g'], 'L0_tok_la_ln_kv_b': _L0_tok_in['la_ln_kv_b'], 'L0_tok_la_wkv': _L0_tok_in['la_wkv'], 'L0_tok_la_proj_w': _L0_tok_in['la_proj_w'], 'L0_tok_la_proj_b': _L0_tok_in['la_proj_b'], 'L0_tok_ga_ln_q_g': _L0_tok_in['ga_ln_q_g'], 'L0_tok_ga_ln_q_b': _L0_tok_in['ga_ln_q_b'], 'L0_tok_ga_wq': _L0_tok_in['ga_wq'], 'L0_tok_ga_ln_kv_g': _L0_tok_in['ga_ln_kv_g'], 'L0_tok_ga_ln_kv_b': _L0_tok_in['ga_ln_kv_b'], 'L0_tok_ga_wkv': _L0_tok_in['ga_wkv'], 'L0_tok_ga_proj_w': _L0_tok_in['ga_proj_w'], 'L0_tok_ga_proj_b': _L0_tok_in['ga_proj_b'], 'L0_tok_mod_w': _L0_tok_in['mod_w'], 'L0_tok_mod_b': _L0_tok_in['mod_b'], 'L0_attn_w_attn': _L0_attn_in['w_attn'], 'L0_attn_w_proj': _L0_attn_in['w_proj'], 'L0_ffn_router': _L0_ffn_in['router'], 'L0_ffn_experts_gate': _L0_ffn_in['experts_gate'], 'L0_ffn_experts_up': _L0_ffn_in['experts_up'], 'L0_ffn_experts_down': _L0_ffn_in['experts_down'], 'L0_ffn_shared_gate': _L0_ffn_in['shared_gate'], 'L0_ffn_shared_up': _L0_ffn_in['shared_up'], 'L0_ffn_shared_down': _L0_ffn_in['shared_down'], 'L1_attn_Wq': _L1_attn_in['Wq'], 'L1_attn_Wk': _L1_attn_in['Wk'], 'L1_attn_Wv': _L1_attn_in['Wv'], 'L1_attn_Wo': _L1_attn_in['Wo'], 'L1_ffn_w_gate': _L1_ffn_in['w_gate'], 'L1_ffn_w_up': _L1_ffn_in['w_up'], 'L1_ffn_w_down': _L1_ffn_in['w_down']}

def reference(x, L0_tok_pixel_masks, L0_tok_conv_w, L0_tok_class_emb, L0_tok_la_ln_q_g, L0_tok_la_ln_q_b, L0_tok_la_wq, L0_tok_la_ln_kv_g, L0_tok_la_ln_kv_b, L0_tok_la_wkv, L0_tok_la_proj_w, L0_tok_la_proj_b, L0_tok_ga_ln_q_g, L0_tok_ga_ln_q_b, L0_tok_ga_wq, L0_tok_ga_ln_kv_g, L0_tok_ga_ln_kv_b, L0_tok_ga_wkv, L0_tok_ga_proj_w, L0_tok_ga_proj_b, L0_tok_mod_w, L0_tok_mod_b, L0_attn_w_attn, L0_attn_w_proj, L0_ffn_router, L0_ffn_experts_gate, L0_ffn_experts_up, L0_ffn_experts_down, L0_ffn_shared_gate, L0_ffn_shared_up, L0_ffn_shared_down, L1_attn_Wq, L1_attn_Wk, L1_attn_Wv, L1_attn_Wo, L1_ffn_w_gate, L1_ffn_w_up, L1_ffn_w_down):
    import jax
    import jax.numpy as jnp

    def _L0_tok_ref(pixel_values, pixel_masks, conv_w, class_emb, la_ln_q_g, la_ln_q_b, la_wq, la_ln_kv_g, la_ln_kv_b, la_wkv, la_proj_w, la_proj_b, ga_ln_q_g, ga_ln_q_b, ga_wq, ga_ln_kv_g, ga_ln_kv_b, ga_wkv, ga_proj_w, ga_proj_b, mod_w, mod_b):
        import jax, jax.numpy as jnp
        import numpy as np
        C = 256
        H8 = 8
        DH = C // H8
        PS = 14
        CS = 3
        IMG = 168
        B = 4

        def _ln(x, g, b):
            mu = jnp.mean(x, axis=-1, keepdims=True)
            xc = x - mu
            var = jnp.mean(xc * xc, axis=-1, keepdims=True)
            return xc * jax.lax.rsqrt(var + 1e-05) * g + b

        def _forward(pixel_values, conv_w, class_emb, la_ln_q_g, la_ln_q_b, la_wq, la_ln_kv_g, la_ln_kv_b, la_wkv, la_proj_w, la_proj_b, ga_ln_q_g, ga_ln_q_b, ga_wq, ga_ln_kv_g, ga_ln_kv_b, ga_wkv, ga_proj_w, ga_proj_b, mod_w, mod_b):
            b = pixel_values.shape[0]
            pe = jax.lax.conv_general_dilated(pixel_values, conv_w, (PS, PS), 'VALID', dimension_numbers=('NCHW', 'OIHW', 'NCHW'))
            HP = pe.shape[2]
            h = HP // CS
            hw, N = (h * h, CS * CS)
            scale = C ** (-0.5)
            grid = pe.reshape(b, C, h, CS, h, CS)
            red = grid.mean(axis=(3, 5)).reshape(b, C, hw).transpose(0, 2, 1)
            win = grid.transpose(0, 2, 4, 3, 5, 1).reshape(b, hw, N, C)
            q = _ln(red, la_ln_q_g, la_ln_q_b) @ la_wq
            q = q.reshape(b, hw, H8, DH).transpose(0, 2, 1, 3)
            kv = _ln(win, la_ln_kv_g, la_ln_kv_b) @ la_wkv
            kv = kv.reshape(b, hw, N, 2, H8, DH).transpose(3, 0, 4, 1, 2, 5)
            k_, v_ = (kv[0], kv[1])
            attn = jax.nn.softmax(jnp.einsum('bhnd,bhnkd->bhnk', q * scale, k_), axis=-1)
            agg = jnp.einsum('bhnk,bhnkd->bhnd', attn, v_)
            agg = agg.transpose(0, 2, 1, 3).reshape(b, hw, C)
            local_out = red + agg @ la_proj_w + la_proj_b
            cls = jnp.broadcast_to(class_emb, (b, 1, C))
            gq = (_ln(cls, ga_ln_q_g, ga_ln_q_b) @ ga_wq).reshape(b, H8, DH)
            gkv = _ln(local_out, ga_ln_kv_g, ga_ln_kv_b) @ ga_wkv
            gkv = gkv.reshape(b, hw, 2, H8, DH).transpose(2, 0, 3, 1, 4)
            gk, gv = (gkv[0], gkv[1])
            gattn = jax.nn.softmax(jnp.einsum('bhd,bhnd->bhn', gq * scale, gk), axis=-1)
            gagg = jnp.einsum('bhn,bhnd->bhd', gattn, gv).reshape(b, 1, C)
            cls_out = cls + gagg @ ga_proj_w + ga_proj_b
            patch_out = local_out @ mod_w + mod_b
            return jnp.concatenate([patch_out, cls_out], axis=1)
        del pixel_masks
        return _forward(pixel_values, conv_w, class_emb, la_ln_q_g, la_ln_q_b, la_wq, la_ln_kv_g, la_ln_kv_b, la_wkv, la_proj_w, la_proj_b, ga_ln_q_g, ga_ln_q_b, ga_wq, ga_ln_kv_g, ga_ln_kv_b, ga_wkv, ga_proj_w, ga_proj_b, mod_w, mod_b)

    def _L0_attn_ref(x, w_attn, w_proj):
        import math
        import jax, jax.numpy as jnp
        import numpy as np
        N_HEAD = 16

        def quant_weight(w):
            scale = jnp.maximum(jnp.mean(jnp.abs(w)), 1e-08)
            w_quant = jnp.clip(jnp.round(w / scale), -2.0, 2.0)
            return jax.lax.stop_gradient(w_quant * scale - w) + w
        B, T, C = x.shape
        H = N_HEAD
        D = C // H
        qkv = jnp.einsum('btc,oc->bto', x, quant_weight(w_attn))
        q, k, v = jnp.split(qkv, 3, axis=-1)
        q = q.reshape(B, T, H, D).transpose(0, 2, 1, 3)
        k = k.reshape(B, T, H, D).transpose(0, 2, 1, 3)
        v = v.reshape(B, T, H, D).transpose(0, 2, 1, 3)
        att = jnp.einsum('bhqd,bhkd->bhqk', q, k) * (1.0 / math.sqrt(D))
        causal = jnp.tril(jnp.ones((T, T), dtype=bool))
        att = jnp.where(causal, att, jnp.finfo(att.dtype).min)
        att = jax.nn.softmax(att, axis=-1)
        y = jnp.einsum('bhqk,bhkd->bhqd', att, v)
        y = y.transpose(0, 2, 1, 3).reshape(B, T, C)
        return jnp.einsum('btc,oc->bto', y, quant_weight(w_proj))

    def _L0_ffn_ref(x, router, experts_gate, experts_up, experts_down, shared_gate, shared_up, shared_down):
        import jax, jax.numpy as jnp
        import numpy as np
        TOP_K = 2
        NUM_EXPERTS = 8
        b, s, h = x.shape
        E = router.shape[1]
        shared_act = jax.nn.silu(jnp.einsum('bsh,hd->bsd', x, shared_gate))
        shared_up_out = jnp.einsum('bsh,hd->bsd', x, shared_up)
        shared_out = jnp.einsum('bsd,dh->bsh', shared_act * shared_up_out, shared_down)
        router_probs = jax.nn.softmax(jnp.einsum('bsh,he->bse', x, router), axis=-1)
        topk_probs, topk_idx = jax.lax.top_k(router_probs, TOP_K)
        coef = jnp.sum(jax.nn.one_hot(topk_idx, E, dtype=x.dtype) * topk_probs[..., None], axis=2)
        coef = coef.reshape(b * s, E)
        x_flat = x.reshape(b * s, h)
        gate = jnp.einsum('th,ehd->etd', x_flat, experts_gate)
        up = jnp.einsum('th,ehd->etd', x_flat, experts_up)
        expert_out = jnp.einsum('etd,edh->eth', jax.nn.silu(gate) * up, experts_down)
        routed = jnp.einsum('eth,te->th', expert_out, coef)
        return routed.reshape(b, s, h) + shared_out

    def _L1_attn_ref(x, Wq, Wk, Wv, Wo):
        import math
        import jax, jax.numpy as jnp
        import numpy as np
        D_MODEL = 256
        N_HEADS = 16
        HEAD_DIM = D_MODEL // N_HEADS
        ROPE_THETA = 10000.0

        def _apply_rope(t, offset=0):
            B, H, T, Dh = t.shape
            inv_freq = 1.0 / ROPE_THETA ** (jnp.arange(0, Dh, 2, dtype=jnp.float32) / Dh)
            pos = jnp.arange(T, dtype=jnp.float32) + offset
            ang = pos[:, None] * inv_freq[None, :]
            cos = jnp.concatenate([jnp.cos(ang), jnp.cos(ang)], axis=-1)
            sin = jnp.concatenate([jnp.sin(ang), jnp.sin(ang)], axis=-1)
            t1, t2 = (t[..., :Dh // 2], t[..., Dh // 2:])
            rot = jnp.concatenate([-t2, t1], axis=-1)
            return t * cos + rot * sin

        def _forward(x, Wq, Wk, Wv, Wo):
            B, T, _ = x.shape
            scale = 1.0 / math.sqrt(HEAD_DIM)

            def split_heads(y):
                return y.reshape(B, T, N_HEADS, HEAD_DIM).transpose(0, 2, 1, 3)
            q = split_heads(x @ Wq.T)
            k = split_heads(x @ Wk.T)
            v = split_heads(x @ Wv.T)
            q = _apply_rope(q)
            k = _apply_rope(k)
            scores = jnp.einsum('bhtd,bhsd->bhts', q, k) * scale
            causal = jnp.triu(jnp.ones((T, T), dtype=bool), k=1)
            scores = jnp.where(causal[None, None], -jnp.inf, scores)
            attn = jax.nn.softmax(scores, axis=-1)
            attn = jnp.nan_to_num(attn, nan=0.0)
            out = jnp.einsum('bhts,bhsd->bhtd', attn, v)
            out = out.transpose(0, 2, 1, 3).reshape(B, T, N_HEADS * HEAD_DIM)
            return out @ Wo.T
        return _forward(x, Wq, Wk, Wv, Wo)

    def _L1_ffn_ref(x, w_gate, w_up, w_down):
        import jax, jax.numpy as jnp
        import numpy as np
        HIDDEN = 256
        INNER = 1024

        def _weight_quant(w):
            scale = 1.0 / jnp.clip(jnp.mean(jnp.abs(w)), 1e-05)
            wq = jnp.clip(jnp.round(w * scale), -1.0, 1.0) / scale
            return w + jax.lax.stop_gradient(wq - w)

        def _act_quant(x):
            scale = 127.0 / jnp.clip(jnp.max(jnp.abs(x), axis=-1, keepdims=True), 1e-05)
            xq = jnp.clip(jnp.round(x * scale), -128.0, 127.0) / scale
            return x + jax.lax.stop_gradient(xq - x)

        def _bitlinear(x, w):
            return jnp.einsum('bsi,oi->bso', _act_quant(x), _weight_quant(w))
        gate = jax.nn.silu(_bitlinear(x, w_gate))
        up = _bitlinear(x, w_up)
        return _bitlinear(gate * up, w_down)
    h = _L0_tok_ref(x, L0_tok_pixel_masks, L0_tok_conv_w, L0_tok_class_emb, L0_tok_la_ln_q_g, L0_tok_la_ln_q_b, L0_tok_la_wq, L0_tok_la_ln_kv_g, L0_tok_la_ln_kv_b, L0_tok_la_wkv, L0_tok_la_proj_w, L0_tok_la_proj_b, L0_tok_ga_ln_q_g, L0_tok_ga_ln_q_b, L0_tok_ga_wq, L0_tok_ga_ln_kv_g, L0_tok_ga_ln_kv_b, L0_tok_ga_wkv, L0_tok_ga_proj_w, L0_tok_ga_proj_b, L0_tok_mod_w, L0_tok_mod_b)
    h = h + _L0_attn_ref(_layernorm(h, axis=-1), L0_attn_w_attn, L0_attn_w_proj)
    h = h + _L0_ffn_ref(_layernorm(h, axis=-1), L0_ffn_router, L0_ffn_experts_gate, L0_ffn_experts_up, L0_ffn_experts_down, L0_ffn_shared_gate, L0_ffn_shared_up, L0_ffn_shared_down)
    h = h + _L1_attn_ref(_layernorm(h, axis=-1), L1_attn_Wq, L1_attn_Wk, L1_attn_Wv, L1_attn_Wo)
    h = h + _L1_ffn_ref(_layernorm(h, axis=-1), L1_ffn_w_gate, L1_ffn_w_up, L1_ffn_w_down)
    return h

_drawn_inputs = setup_inputs


def setup_inputs(seed=0):
    import zlib

    import numpy as np

    out = dict(_drawn_inputs(seed))
    spreads = {'L0_tok_pixel_masks': (1.0, 0.2),
     'L0_tok_la_ln_q_g': (1.0, 0.6),
     'L0_tok_la_ln_q_b': (0.0, 0.8),
     'L0_tok_la_ln_kv_g': (1.0, 0.6),
     'L0_tok_la_ln_kv_b': (0.0, 0.1),
     'L0_tok_la_proj_b': (0.0, 0.1),
     'L0_tok_ga_ln_q_g': (1.0, 0.6),
     'L0_tok_ga_ln_q_b': (0.0, 2.0),
     'L0_tok_ga_ln_kv_g': (1.0, 0.583),
     'L0_tok_ga_ln_kv_b': (0.0, 0.308),
     'L0_tok_ga_proj_b': (0.0, 0.1),
     'L0_tok_mod_b': (0.0, 0.1)}
    factors = {'L0_tok_la_wq': 8.0, 'L0_tok_ga_wq': 8.0}
    for name, (base, spread) in spreads.items():
        noise = np.random.default_rng([zlib.crc32(name.encode()), seed]).standard_normal(out[name].shape)
        drawn = base * np.exp(spread * noise) if base else spread * noise
        out[name] = jnp.asarray(drawn.astype(out[name].dtype))
    for name, factor in factors.items():
        out[name] = (out[name] * factor).astype(out[name].dtype)
    return out
```

```python
from contextlib import ExitStack

import numpy as np

import concourse.bass as bass
from concourse import mybir

F32 = mybir.dt.float32
BF16 = mybir.dt.bfloat16
ALU = mybir.AluOpType
ACT = mybir.ActivationFunctionType
AX = mybir.AxisListType

P = 128
C = 256
KC = C // P
NB = 64
T = 5
NTOK = NB * T
CONV_K = 3 * 14 * 14
CONV_FULL = CONV_K // P
CONV_TAIL = CONV_K - CONV_FULL * P
TAIL_A = 64
NPATCH = 9
NT = 2 * NPATCH
LH, LD = 8, 32
HH = 8
HD = 16
E = 8
NM = E + 2
INNER = 1024
NI = INNER // P
EPS = 1e-5
MAGIC = 12582912.0
BLK = [0, 2, 1, 3, 4]
ROWS = [P, P, NB]
NEG = -3.0e38

C_ID, C_FOLD, C_IDX, C_COS, C_SIN, C_END = 0, 128, 192, 200, 264, 328
W_Q, W_KV, W_P, W_M, W_GQ, W_GKV, W_GP, W_END = 0, 256, 768, 1024, 1280, 1536, 2048, 2304
R_LAP, R_GAP, R_MOD, R_CLS = range(4)
G_LQ, G_LKV, G_GQ, G_GKV = 0, 2, 4, 6


def tokenizer_steps():
    s = [("clsT", 0), ("gq", 0)]
    s = [("conv", i) for i in range(3)] + s + [("conv", i) for i in range(3, 11)]
    s += [("qT", 0), ("conv", 11), ("q", 0), ("T", 0)]
    for i in range(12, 18):
        s += [("conv", i), ("T", i - 11), ("kv", i - 12)]
        if i == 14:
            s += [("sumA", 0)]
    s += [("T", 7), ("kv", 6), ("qT", 1), ("T", 8), ("kv", 7), ("q", 1), ("T", 9), ("kv", 8)]
    late = {12: ("aggT", 0), 13: ("proj", 0), 14: ("loT", 0), 15: ("mod", 0), 16: ("lnloT", 0)}
    for i in range(9, 18):
        if i < 17:
            s += [("T", i + 1)]
        s += [("kv", i)]
        if i in late:
            s += [late[i]]
    s += [("aggT", 1), ("proj", 1), ("loT", 1), ("mod", 1), ("lnloT", 1),
          ("gs", 0), ("gv", 0), ("pT", 0), ("fold", 0), ("cls", 0)]
    return s


LN_ORDER = (["cls"] + [("tile", i) for i in range(10)] + [("q", 0)] + [("tile", i) for i in range(10, 18)]
            + [("q", 1), ("lo", 0), ("lo", 1)] + [(n, j) for n in ("at0", "moe", "at1", "ffn") for j in range(3)])
LN = {k: i for i, k in enumerate(LN_ORDER)}
NLN = len(LN_ORDER)


def vit_tower(nc, xk, cw, cst, sel_in, fcols, frows, tokw, at0w, at0p, router, moe_gu, moe_d,
              at1w, at1p, ffg, ffu, ffd, out):
    with ExitStack() as ctx:
        def sb(name, shape, dt=F32):
            return ctx.enter_context(nc.sbuf_tensor(name, shape, dt))

        def sem(name):
            return ctx.enter_context(nc.semaphore(name))

        def bc(ap, axis, n):
            shape = list(ap.shape)
            shape.insert(axis, n)
            return ap.unsqueeze(axis).broadcast_to(shape)

        bank = [ctx.enter_context(nc.psum_tensor(f"bank{i}", [P, 512], F32)) for i in range(8)]

        cst_sb = sb("cst_sb", [P, C_END])
        ident = cst_sb[:, C_ID:C_ID + P]
        fold = cst_sb[:, C_FOLD:C_FOLD + NB]
        sel = sb("sel", [3 * E, E, P], BF16)
        identb = sb("identb", [P, P], BF16)
        ones = sb("ones", [P, P])
        cw_sb = sb("cw_sb", [P, CONV_FULL + 1, C])
        tw = sb("tw", [P, KC, W_END])
        fc = sb("fc", [P, 8, KC])
        fr = sb("fr", [P, 4, C])
        at0w_sb = sb("at0w_sb", [P, KC, 2, 3 * P])
        at0p_sb = sb("at0p_sb", [P, KC, C])
        router_sb = sb("router_sb", [P, KC, E])
        gu_sb = sb("gu_sb", [P, NM, 2, KC, P])

        x_sb = sb("x_sb", [P, CONV_FULL + 1, NT * P])
        pe = sb("pe", [P, NT, C])
        lnT = sb("lnT", [P, 3, KC, P])
        red = sb("red", [P, 2, C])
        xh = sb("xh", [P, 2, C])
        qlnT = sb("qlnT", [P, KC, P])
        q_sb = sb("q_sb", [P, 2, C])
        kv = sb("kv", [P, NT, 2 * C])
        prod = sb("prod", [P, NPATCH, C])
        sc = sb("sc", [P, NPATCH, LH])
        small = sb("small", [P, 4, 64])
        agg = sb("agg", [P, C])
        aggT = sb("aggT", [P, KC, P])
        lo = sb("lo", [P, 2, C])
        loT = sb("loT", [P, KC, P])
        lnloT = sb("lnloT", [P, KC, 2, P])
        clsT = sb("clsT", [P, KC, P])
        gq = sb("gq", [P, C])
        gprod = sb("gprod", [P, KC, C])
        G = sb("G", [P, KC, LH])
        gsc = sb("gsc", [LH, 4, NB])
        gsm = sb("gsm", [LH, 4, NB])
        gpt = sb("gpt", [P, 2, LH])
        pgv = sb("pgv", [P, 2, C])
        gfold = sb("gfold", [P, KC, NB])
        clsb = sb("clsb", [NB, C])

        def views(whole, *shapes):
            at, got = 0, []
            for shape in shapes:
                dt = F32
                if shape[-1] is BF16:
                    shape, dt = shape[:-1], BF16
                n = int(np.prod(shape)) // (2 if dt is BF16 else 1)
                part = whole[:, at:at + n]
                if dt is BF16:
                    part = part.bitcast(BF16)
                names = "abcd"[:len(shape)]
                dims = dict(zip(names[1:], shape[1:]))
                got.append(part.rearrange(f"p ({' '.join(names)}) -> p {' '.join(names)}", **dims))
                at += n
            assert at <= whole.shape[1]
            return got

        ffw_sb, at1w_sb, at1p_sb, dn_sb = views(
            x_sb[:, :, :].rearrange("p c n -> p (c n)"), (3, 2 * INNER), (KC, 2, 3 * P), (KC, C), (NM, C))
        qkv, aprod, y, yT, th, act_a, act_m, hm, hqT = views(
            kv[:, :, :].rearrange("p i n -> p (i n)"), (T, 3 * P), (T, P), (T, P), (KC, NTOK), (2, 512), (2, 512),
            (2, NTOK), (2, INNER), (NI, P, BF16))
        ffq_sb, xn, xT = views(pe[:, :, :].rearrange("p i n -> p (i n)"), (3, 2 * INNER, BF16), (3, C), (KC, NTOK))
        hq, xq, xqT, rot = views(prod[:, :, :].rearrange("p t n -> p (t n)"), (2, INNER, BF16), (3, C, BF16),
                                 (KC, NTOK, BF16), (2 * HH, HD))
        gateq = ffq_sb[:, 0, :].rearrange("p (c n) -> p c n", c=KC)
        upq = ffq_sb[:, 1, :].rearrange("p (c n) -> p c n", c=KC)
        downq = ffq_sb[:, 2, :].rearrange("p (c n) -> p c n", c=NI)

        h = sb("h", [P, 3, C])
        S = sb("S", [P, T, HH, T])
        S1 = sb("S1", [P, T, HH])
        lg = sb("lg", [P, 3, E])
        rt = sb("rt", [P, 6, 3, E])
        rs = sb("rs", [P, 4, 3])
        c3 = sb("c3", [P, 3, 3, E], BF16)
        c3T = sb("c3T", [3 * E, NTOK], BF16)
        junk = sb("junk", [P, 2 * INNER], BF16)
        wsum = sb("wsum", [P, 5])
        wsc = sb("wsc", [P, 5])
        winv = sb("winv", [P, 5])
        wf = sb("wf", [P, 4])
        fx = sb("fx", [P, 8, 3])
        stats = sb("stats", [P, NLN, 6])
        mv = sb("mv", [P, NLN, 2])
        veps = sb("veps", [P, NLN])
        rstd = sb("rstd", [P, NLN])
        nhalf = sb("nhalf", [P, 1])

        ld_cw, ld_cst, ld_sel, ld_fc, ld_fr = (sem(n) for n in ("ld_cw", "ld_cst", "ld_sel", "ld_fc", "ld_fr"))
        ld_x = [sem(f"ld_x{i}") for i in range(6)]
        ld_xt = [sem(f"ld_xt{i}") for i in range(2)]
        ld_tq, ld_tkv, ld_tp, ld_tg = (sem(n) for n in ("ld_tq", "ld_tkv", "ld_tp", "ld_tg"))
        ld_at0, ld_rt, ld_at1 = sem("ld_at0"), sem("ld_rt"), sem("ld_at1")
        ld_gu = [sem(f"ld_gu{i}") for i in range(3)]
        ld_dn = sem("ld_dn")
        ld_ff = sem("ld_ff")
        chain = sem("chain")
        pchain = sem("pchain")
        var_ready, rstd_ready = sem("var_ready"), sem("rstd_ready")
        consts_ready = sem("consts_ready")
        xh_ready = sem("xh_ready")
        norm_ready = sem("norm_ready")
        red_added = sem("red_added")
        pe_step = {k: sem("pe_" + k) for k in
                   ("conv", "T", "kv", "clsT", "gq", "qT", "q", "aggT", "proj", "loT", "mod",
                    "lnloT", "gv", "gs", "pT", "fold", "cls", "sumA")}
        ev = {k: sem("ev_" + k) for k in
              ("conv", "T", "kv", "clsT", "gq", "qT", "q", "aggT", "proj", "loT", "mod", "lnloT",
               "gs", "pgv", "pT", "fold", "cls", "sumA")}
        local_exp, local_arg = sem("local_exp"), sem("local_arg")
        agg_ready = sem("agg_ready")
        g_ready = sem("g_ready")
        gexp, garg = sem("gexp"), sem("garg")
        gp_ready = sem("gp_ready")
        abs_done = sem("abs_done")
        at0q_ready = sem("at0q_ready")
        xn_ready = sem("xn_ready")
        xnT_done, xT_ready = sem("xnT_done"), sem("xT_ready")
        qkv_done, qkv_ready = sem("qkv_done"), sem("qkv_ready")
        at_arg, at_exp = sem("at_arg"), sem("at_exp")
        rot_ready = sem("rot_ready")
        y_ready, yT_done, yT_ready, ao_done = sem("y_ready"), sem("yT_done"), sem("yT_ready"), sem("ao_done")
        h_ready = sem("h_ready")
        rt_done, rt_arg, rt_exp, c3_ready, c3T_done, c3T_ready = (
            sem(n) for n in ("rt_done", "rt_arg", "rt_exp", "c3_ready", "c3T_done", "c3T_ready"))
        lg_read = sem("lg_read")
        coef_done, coef_used = sem("coef_done"), sem("coef_used")
        gu_done, th_ready, gu_used, act_ready, dn_done = (
            sem(n) for n in ("gu_done", "th_ready", "gu_used", "act_ready", "dn_done"))
        sumB_done, scB_ready, ffq_ready = sem("sumB_done"), sem("scB_ready"), sem("ffq_ready")
        xq_ready, xqT_done, xqT_ready = sem("xq_ready"), sem("xqT_done"), sem("xqT_ready")
        fg_done, fth_ready, fg_used = sem("fg_done"), sem("fth_ready"), sem("fg_used")
        hq_ready, hqT_done, hqT_ready, fd_done = sem("hq_ready"), sem("hqT_done"), sem("hqT_ready"), sem("fd_done")
        tscale_ready = sem("tscale_ready")
        stored = sem("stored")

        STEPS = tokenizer_steps()
        block = ctx.enter_context(nc.Block())

        @block.sync
        def _(sp):
            xmain = xk[0:CONV_FULL * P, :].rearrange("(c p) n -> p c n", p=P)
            kt = CONV_FULL * P

            def load_x(g):
                cols = slice(g * 3 * P, (g + 1) * 3 * P)
                sp.dma_start(x_sb[:, 0:CONV_FULL, cols], xmain[:, :, cols]).then_inc(ld_x[g], 16)

            def load_tail(w):
                cols = slice(w * NPATCH * P, (w + 1) * NPATCH * P)
                sp.dma_start(x_sb[0:TAIL_A, CONV_FULL, cols], xk[kt:kt + TAIL_A, cols]).then_inc(ld_xt[w], 16)
                sp.dma_start(x_sb[TAIL_A:CONV_TAIL, CONV_FULL, cols],
                             xk[kt + TAIL_A:CONV_K, cols]).then_inc(ld_xt[w], 16)

            sp.dma_start(cw_sb[:, 0:CONV_FULL, :], cw[0:kt, :].rearrange("(c p) n -> p c n", p=P)).then_inc(ld_cw, 16)
            load_x(0)
            sp.dma_start(cw_sb[0:TAIL_A, CONV_FULL, :], cw[kt:kt + TAIL_A, :]).then_inc(ld_cw, 16)
            sp.dma_start(cw_sb[TAIL_A:CONV_TAIL, CONV_FULL, :], cw[kt + TAIL_A:CONV_K, :]).then_inc(ld_cw, 16)
            load_tail(0)
            load_x(1)
            sp.dma_start(fr[:, :, :], bc(frows, 0, P)).then_inc(ld_fr, 16)
            sp.dma_start(fc[:, :, :], fcols).then_inc(ld_fc, 16)
            sp.dma_start(cst_sb[:, :], cst).then_inc(ld_cst, 16)
            load_x(2)
            for g in (3, 4):
                load_x(g)
            load_tail(1)
            sp.dma_start(tw[:, :, W_Q:W_KV], tokw[:, :, W_Q:W_KV]).then_inc(ld_tq, 16)
            sp.dma_start(tw[:, :, W_KV:W_P], tokw[:, :, W_KV:W_P]).then_inc(ld_tkv, 16)
            sp.dma_start(tw[:, :, W_GQ:W_END], tokw[:, :, W_GQ:W_END]).then_inc(ld_tg, 16)
            load_x(5)
            sp.dma_start(at0w_sb[:, :, :, :], at0w).then_inc(ld_at0, 16)
            sp.dma_start(at0p_sb[:, :, :], at0p).then_inc(ld_at0, 16)
            sp.dma_start(tw[:, :, W_P:W_GQ], tokw[:, :, W_P:W_GQ]).then_inc(ld_tp, 16)
            sp.dma_start(router_sb[:, :, :], router).then_inc(ld_rt, 16)
            sp.dma_start(sel[:, :, :], sel_in).then_inc(ld_sel, 16)
            sp.dma_start(gu_sb[:, 8:10], moe_gu[:, 8:10]).then_inc(ld_gu[0], 16)
            sp.dma_start(gu_sb[:, 0:4], moe_gu[:, 0:4]).then_inc(ld_gu[1], 16)
            sp.dma_start(gu_sb[:, 4:8], moe_gu[:, 4:8]).then_inc(ld_gu[2], 16)
            sp.wait_ge(pe_step["conv"], NT)
            sp.dma_start(dn_sb[:, :, :], moe_d).then_inc(ld_dn, 16)
            for i, w in enumerate((ffg, ffu, ffd)):
                sp.dma_start(ffw_sb[:, i, :], w).then_inc(ld_ff, 16)
            sp.dma_start(at1w_sb[:, :, :, :], at1w).then_inc(ld_at1, 16)
            sp.dma_start(at1p_sb[:, :, :], at1p).then_inc(ld_at1, 16)
            for s in (0, 2, 1, 3, 4):
                j, half = BLK[s] // 2, BLK[s] % 2
                sp.wait_ge(h_ready, 9 + j + 1)
                sp.dma_start(out[:, s, :], h[half * NB:(half + 1) * NB, j, :]).then_inc(stored, 16)
            sp.wait_ge(stored, 16 * T)

        @block.tensor
        def _(te):
            def mm(o, l, r, c, n):
                return te.matmul(o, l, r, start=(c == 0), stop=(c == n - 1))

            def turn(o, src, np_):
                for c in range(KC):
                    last = te.transpose(o[:, c, 0:np_], src[0:np_, c * P:(c + 1) * P], ident[0:np_, 0:np_])
                return last

            def chunks(b, n=P):
                return bank[b][:, 0:KC * P].rearrange("p (c n) -> p c n", c=KC)

            def conv(i):
                if i % 3 == 0:
                    te.wait_ge(ld_x[i // 3], 16)
                if i % NPATCH == 0:
                    te.wait_ge(ld_xt[i // NPATCH], 32)
                if i == 0:
                    te.wait_ge(ld_cw, 48)
                if i >= 2:
                    te.wait_ge(ev["conv"], i - 1)
                cols = slice(i * P, (i + 1) * P)
                for c in range(CONV_FULL + 1):
                    k = P if c < CONV_FULL else CONV_TAIL
                    last = mm(bank[i % 2][:, 0:C], x_sb[0:k, c, cols], cw_sb[0:k, c, :], c, CONV_FULL + 1)
                last.then_inc(pe_step["conv"], 1)

            def tile_T(i):
                te.wait_ge(norm_ready, i + 1)
                if i >= 2:
                    te.wait_ge(ev["T"], i - 1)
                turn(chunks(2 + i % 2), pe[:, i, :], P).then_inc(pe_step["T"], 1)

            def tile_kv(i):
                if i == 0:
                    te.wait_ge(ld_tkv, 16)
                te.wait_ge(ev["T"], i + 1)
                if i >= 2:
                    te.wait_ge(ev["kv"], i - 1)
                for c in range(KC):
                    last = mm(bank[4 + i % 2][:, :], lnT[:, i % 3, c, :], tw[:, c, W_KV:W_P], c, KC)
                last.then_inc(pe_step["kv"], 1)

            def cls_T(_):
                te.wait_ge(ld_cst, 16)
                te.wait_ge(xh_ready, 1)
                turn(chunks(6), xh[:, 0, :], P).then_inc(pe_step["clsT"], 1)

            def cls_q(_):
                te.wait_ge(ld_tg, 16)
                te.wait_ge(ev["clsT"], 1)
                for c in range(KC):
                    last = mm(bank[7][:, 0:C], clsT[:, c, :], tw[:, c, W_GQ:W_GKV], c, KC)
                last.then_inc(pe_step["gq"], 1)

            def q_T(w):
                te.wait_ge(xh_ready, 2 + w)
                if w == 0:
                    te.wait_ge(ev["clsT"], 1)
                te.wait_ge(ev["qT"], w) if w else None
                turn(chunks(6), xh[:, w, :], P).then_inc(pe_step["qT"], 1)

            def q_mm(w):
                if w == 0:
                    te.wait_ge(ld_tq, 16)
                    te.wait_ge(ev["gq"], 1)
                    te.wait_ge(ev["qT"], 1)
                else:
                    te.wait_ge(ev["sumA"], 1)
                    te.wait_ge(ev["qT"], 2)
                for c in range(KC):
                    last = mm(bank[7][:, 0:C], qlnT[:, c, :], tw[:, c, W_Q:W_KV], c, KC)
                last.then_inc(pe_step["q"], 1)

            def sum_a(_):
                te.wait_ge(abs_done, 2)
                te.wait_ge(consts_ready, 3)
                te.wait_ge(ev["q"], 1)
                mm(bank[7][:, 0:2], ones[:, :], wsum[:, 0:2], 0, 1).then_inc(pe_step["sumA"], 1)

            def agg_T(w):
                te.wait_ge(agg_ready, w + 1)
                te.wait_ge(ev["qT"], 2) if w == 0 else te.wait_ge(ev["lnloT"], 1)
                turn(chunks(6), agg[:, :], P).then_inc(pe_step["aggT"], 1)

            def proj(w):
                if w == 0:
                    te.wait_ge(ld_tp, 16)
                te.wait_ge(ev["q"], 2) if w == 0 else te.wait_ge(ev["mod"], 1)
                te.wait_ge(ev["aggT"], w + 1)
                for c in range(KC):
                    last = mm(bank[7][:, 0:C], aggT[:, c, :], tw[:, c, W_P:W_M], c, KC)
                last.then_inc(pe_step["proj"], 1)

            def lo_T(w):
                te.wait_ge(ev["proj"], w + 1)
                te.wait_ge(ev["aggT"], w + 1)
                turn(chunks(6), lo[:, w, :], P).then_inc(pe_step["loT"], 1)

            def mod(w):
                te.wait_ge(ev["loT"], w + 1)
                te.wait_ge(ev["proj"], w + 1)
                for c in range(KC):
                    last = mm(bank[7][:, 0:C], loT[:, c, :], tw[:, c, W_M:W_GQ], c, KC)
                last.then_inc(pe_step["mod"], 1)

            def lnlo_T(w):
                te.wait_ge(xh_ready, 4 + w)
                te.wait_ge(ev["loT"], w + 1)
                turn(chunks(6), xh[:, w, :], P).then_inc(pe_step["lnloT"], 1)

            def g_scores(_):
                te.wait_ge(g_ready, 1)
                te.wait_ge(ev["lnloT"], 2)
                te.wait_ge(ev["kv"], NT)
                for c in range(KC):
                    last = mm(bank[5][0:LH, 0:2 * P], G[:, c, :], lnloT[:, c, :, :], c, KC)
                last.then_inc(pe_step["gs"], 1)

            def g_v(_):
                for w in range(2):
                    for c in range(KC):
                        last = mm(bank[4][:, w * C:(w + 1) * C], lnloT[:, c, w, :],
                                  tw[:, c, W_GKV + C:W_GP], c, KC)
                last.then_inc(pe_step["gv"], 1)

            def p_T(_):
                te.wait_ge(gp_ready, 1)
                te.wait_ge(ev["T"], NT)
                gs = gsc[:, :, :].rearrange("h (w a) b -> h w (a b)", w=2)
                for w in range(2):
                    last = te.transpose(bank[3][:, w * LH:(w + 1) * LH], gs[:, w, :], ident[0:LH, 0:LH])
                last.then_inc(pe_step["pT"], 1)

            def fold_halves(_):
                te.wait_ge(ev["pgv"], 1)
                te.wait_ge(ev["T"], NT)
                for c in range(KC):
                    for w in range(2):
                        last = mm(bank[2][:, c * NB:(c + 1) * NB], pgv[:, w, c * P:(c + 1) * P], fold, w, 2)
                last.then_inc(pe_step["fold"], 1)

            def cls_out(_):
                te.wait_ge(ev["fold"], 1)
                te.wait_ge(ev["conv"], NT)
                for c in range(KC):
                    last = mm(bank[1][0:NB, 0:C], gfold[:, c, :], tw[:, c, W_GP:W_END], c, KC)
                last.then_inc(pe_step["cls"], 1)

            run = {"conv": conv, "T": tile_T, "kv": tile_kv, "clsT": cls_T, "gq": cls_q, "qT": q_T,
                   "q": q_mm, "sumA": sum_a, "aggT": agg_T, "proj": proj, "loT": lo_T, "mod": mod,
                   "lnloT": lnlo_T, "gs": g_scores, "gv": g_v, "pT": p_T, "fold": fold_halves, "cls": cls_out}
            for kind, i in STEPS:
                run[kind](i)

            def tokens_T(n, j):
                te.wait_ge(xn_ready, 3 * n + j + 1)
                turn(chunks(j), xn[:, j, :], ROWS[j]).then_inc(xnT_done, 1)

            def attention(n, layer, w, wp):
                if layer == 0:
                    te.wait_ge(ev["cls"], 1)
                    te.wait_ge(ev["pgv"], 1)
                    te.wait_ge(ev["mod"], 2)
                    te.wait_ge(ev["lnloT"], 2)
                    te.wait_ge(ev["pT"], 1)
                    te.wait_ge(at0q_ready, 2)
                else:
                    te.wait_ge(ld_at1, 32)
                    te.wait_ge(h_ready, 6)
                for j in range(3):
                    tokens_T(n, j)
                for s in range(T):
                    te.wait_ge(xT_ready, 3 * n + BLK[s] // 2 + 1)
                    rows = slice(BLK[s] * NB, (BLK[s] + 1) * NB)
                    for hh in range(2):
                        for c in range(KC):
                            last = mm(bank[3 + s][hh * NB:(hh + 1) * NB, 0:3 * P], xT[:, c, rows],
                                      w[:, c, hh, :], c, KC)
                    last.then_inc(qkv_done, 1)
                te.wait_ge(xT_ready, 3 * n + 3)
                for g, ts in enumerate(((0, 1), (2, 3), (4,))):
                    te.wait_ge(y_ready, T * layer + ts[-1] + 1)
                    for i, t in enumerate(ts):
                        last = te.transpose(bank[g][:, i * P:(i + 1) * P], y[:, t, :], ident)
                    last.then_inc(yT_done, 1)
                te.wait_ge(qkv_ready, T * layer + T)
                for j in range(3):
                    te.wait_ge(yT_ready, 3 * layer + (2 if j < 2 else 3))
                    for c in range(KC):
                        last = mm(bank[3 + j][0:ROWS[j], 0:C], yT[:, c, j * P:j * P + ROWS[j]], wp[:, c, :], c, KC)
                    last.then_inc(ao_done, 1)

            attention(0, 0, at0w_sb, at0p_sb)

            te.wait_ge(yT_ready, 3)
            te.wait_ge(abs_done, 5)
            mm(bank[6][:, 0:3], ones[:, :], wsum[:, 2:5], 0, 1).then_inc(sumB_done, 1)
            for j in range(3):
                tokens_T(1, j)
            te.wait_ge(ld_rt, 16)
            te.wait_ge(h_ready, 3)
            for j in range(3):
                te.wait_ge(xT_ready, 3 + j + 1)
                for c in range(KC):
                    last = mm(bank[3][0:ROWS[j], j * E:(j + 1) * E], xT[:, c, j * P:j * P + ROWS[j]],
                              router_sb[:, c, :], c, KC)
            last.then_inc(rt_done, 1)

            def gate_up(i):
                m = MOE_ORDER[i]
                if i == 0:
                    te.wait_ge(ld_gu[0], 16)
                    te.wait_ge(scB_ready, 1)
                if i == 2:
                    te.wait_ge(ld_gu[1], 16)
                if i == 6:
                    te.wait_ge(ld_gu[2], 16)
                if i >= 2:
                    te.wait_ge(gu_used, i - 1)
                for gu in range(2):
                    for c in range(KC):
                        last = mm(bank[4 + 2 * gu + i % 2][:, 0:NTOK], gu_sb[:, m, gu, c, :], xT[:, c, :], c, KC)
                last.then_inc(gu_done, 1)

            def coef_rows(i):
                m = MOE_ORDER[i]
                if i == 2:
                    te.wait_ge(c3T_ready, 1)
                else:
                    te.wait_ge(coef_used, i - 2)
                te.matmul(bank[3][:, 0:NTOK], sel[:, m, :], c3T[:, :], start=True, stop=True).then_inc(coef_done, 1)

            def down(i):
                m = MOE_ORDER[i]
                if i == 0:
                    te.wait_ge(ld_dn, 16)
                te.wait_ge(act_ready, i + 1)
                for j in range(3):
                    last = mm(bank[j][0:ROWS[j], 0:C], act_m[:, i % 2, j * P:j * P + ROWS[j]], dn_sb[:, m, :], i, NM)
                last.then_inc(dn_done, 1)

            gate_up(0)
            gate_up(1)
            te.wait_ge(ld_sel, 16)
            te.wait_ge(consts_ready, 3)
            te.wait_ge(c3_ready, 1)
            bankb = bank[3][0:3 * E, 0:256].bitcast(BF16)
            for j in range(3):
                last = te.transpose(bankb[:, j * P:j * P + ROWS[j]],
                                    c3[0:ROWS[j], j, :, :].rearrange("p a e -> p (a e)"),
                                    identb[0:ROWS[j], 0:ROWS[j]])
            last.then_inc(c3T_done, 1)
            for i in range(2, NM):
                gate_up(i)
                coef_rows(i)
                down(i - 2)
            down(NM - 2)
            down(NM - 1)

            attention(2, 1, at1w_sb, at1p_sb)

            for j in range(3):
                te.wait_ge(xq_ready, j + 1)
                if j == 0:
                    te.wait_ge(yT_ready, 6)
                bankb = bank[j][:, 0:P].bitcast(BF16).rearrange("p (c n) -> p c n", c=KC)
                for c in range(KC):
                    last = te.transpose(bankb[:, c, 0:ROWS[j]], xq[0:ROWS[j], j, c * P:(c + 1) * P],
                                        identb[0:ROWS[j], 0:ROWS[j]])
                last.then_inc(xqT_done, 1)
            te.wait_ge(ffq_ready, 3)

            def ff_up(k):
                j, half = k // 2, k % 2
                if k == 0:
                    te.wait_ge(xqT_ready, 3)
                if k >= 2:
                    te.wait_ge(fg_used, k - 1)
                for gu, wq in enumerate((gateq, upq)):
                    for c in range(KC):
                        last = mm(bank[2 * gu + k % 2][0:ROWS[j], :], xqT[:, c, j * P:j * P + ROWS[j]],
                                  wq[:, c, half * 512:(half + 1) * 512], c, KC)
                last.then_inc(fg_done, 1)

            def ff_down(j):
                r = ROWS[j]
                te.wait_ge(hq_ready, j + 1)
                if j == 0:
                    te.wait_ge(h_ready, 9)
                else:
                    te.wait_ge(hqT_ready, j)
                bankb = bank[4][:, :].bitcast(BF16).rearrange("p (c n) -> p c n", c=NI)
                for c in range(NI):
                    last = te.transpose(bankb[:, c, 0:r], hq[0:r, j % 2, c * P:(c + 1) * P], identb[0:r, 0:r])
                last.then_inc(hqT_done, 1)
                te.wait_ge(hqT_ready, j + 1)
                for c in range(NI):
                    last = mm(bank[5 + j][0:r, 0:C], hqT[:, c, 0:r], downq[:, c, :], c, NI)
                last.then_inc(fd_done, 1)

            for k in range(4):
                ff_up(k)
            ff_down(0)
            ff_up(4)
            ff_up(5)
            ff_down(1)
            ff_down(2)

        @block.scalar
        def _(ac):
            def copy(o, i):
                return ac.activation(o, i, ACT.Copy)

            def chunks(b):
                return bank[b][:, 0:KC * P].rearrange("p (c n) -> p c n", c=KC)

            def affine(o, b, g):
                for c in range(KC):
                    last = ac.activation(o(c), chunks(b)[:, c, :], ACT.Identity,
                                         bias=fc[:, g + 1, c:c + 1], scale=fc[:, g, c:c + 1])
                return last

            def conv(i):
                ac.wait_ge(pe_step["conv"], i + 1)
                copy(pe[:, i, :], bank[i % 2][:, 0:C]).then_inc(ev["conv"], 1)

            def tile_T(i):
                ac.wait_ge(pe_step["T"], i + 1)
                if i >= 3:
                    ac.wait_ge(pe_step["kv"], i - 2)
                affine(lambda c: lnT[:, i % 3, c, :], 2 + i % 2, G_LKV).then_inc(ev["T"], 1)

            def tile_kv(i):
                ac.wait_ge(pe_step["kv"], i + 1)
                copy(kv[:, i, :], bank[4 + i % 2][:, :]).then_inc(ev["kv"], 1)

            def cls_T(_):
                ac.wait_ge(ld_fc, 16)
                ac.wait_ge(pe_step["clsT"], 1)
                affine(lambda c: clsT[:, c, :], 6, G_GQ).then_inc(ev["clsT"], 1)

            def cls_q(_):
                ac.wait_ge(pe_step["gq"], 1)
                copy(gq[:, :], bank[7][:, 0:C]).then_inc(ev["gq"], 1)

            def q_T(w):
                ac.wait_ge(pe_step["qT"], w + 1)
                if w:
                    ac.wait_ge(pe_step["q"], w)
                affine(lambda c: qlnT[:, c, :], 6, G_LQ).then_inc(ev["qT"], 1)

            def q_mm(w):
                ac.wait_ge(pe_step["q"], w + 1)
                ac.activation(q_sb[:, w, :], bank[7][:, 0:C], ACT.Copy, scale=float(C) ** -0.5).then_inc(ev["q"], 1)

            def exp_local(w):
                ac.wait_ge(local_arg, w + 1)
                ac.activation(sc[:, :, :], sc[:, :, :], ACT.Exp).then_inc(local_exp, 1)

            def agg_T(w):
                ac.wait_ge(pe_step["aggT"], w + 1)
                copy(aggT[:, :, :], chunks(6)).then_inc(ev["aggT"], 1)

            def lo_T(w):
                ac.wait_ge(pe_step["loT"], w + 1)
                copy(loT[:, :, :], chunks(6)).then_inc(ev["loT"], 1)

            def lnlo_T(w):
                ac.wait_ge(pe_step["lnloT"], w + 1)
                affine(lambda c: lnloT[:, c, w, :], 6, G_GKV).then_inc(ev["lnloT"], 1)

            def abs_sums(lots, first):
                for n, (i, src) in enumerate(lots):
                    if first + n:
                        ac.wait_ge(abs_done, first + n)
                    ac.activation(junk[:, 0:src.shape[1]], src, ACT.Abs, accum_out=wsum[:, i:i + 1]).then_inc(abs_done, 1)

            def sum_a(_):
                ac.wait_ge(ld_at0, 32)
                abs_sums([(0, at0w_sb[:, :, :, :].rearrange("p c a n -> p (c a n)")),
                          (1, at0p_sb[:, :, :].rearrange("p c n -> p (c n)"))], 0)

            def exp_global(_):
                ac.wait_ge(garg, 1)
                ac.activation(gsc[:, :, :], gsc[:, :, :], ACT.Exp, scale=float(C) ** -0.5).then_inc(gexp, 1)

            def fold_halves(_):
                ac.wait_ge(pe_step["fold"], 1)
                copy(gfold[:, :, :], bank[2][:, 0:KC * NB].rearrange("p (c n) -> p c n", c=KC)).then_inc(ev["fold"], 1)

            run = {"conv": conv, "T": tile_T, "kv": tile_kv, "clsT": cls_T, "gq": cls_q, "qT": q_T,
                   "q": q_mm, "sumA": sum_a, "aggT": agg_T, "loT": lo_T, "lnloT": lnlo_T, "fold": fold_halves}
            for kind, i in STEPS:
                if kind == "aggT":
                    exp_local(i)
                if kind == "pT":
                    exp_global(i)
                if kind in run:
                    run[kind](i)

            def tokens_T(n, j):
                ac.wait_ge(xnT_done, 3 * n + j + 1 - (3 if n == 3 else 0))
                r = ROWS[j]
                copy(xT[:, :, j * P:j * P + r], chunks(j)[:, :, 0:r]).then_inc(xT_ready, 1)

            def attention(n, layer):
                if n == 2:
                    ac.wait_ge(gu_done, NM)
                for j in range(3):
                    tokens_T(n, j)
                for s in range(T):
                    ac.wait_ge(qkv_done, T * layer + s + 1)
                    copy(qkv[:, s, :], bank[3 + s][:, 0:3 * P]).then_inc(qkv_ready, 1)
                if layer == 0:
                    ac.wait_ge(ld_ff, 48)
                    abs_sums([(2 + i, ffw_sb[:, i, :]) for i in range(3)], 2)
                ac.wait_ge(at_arg, layer + 1)
                ac.activation(S[:, :, :, :], S[:, :, :, :], ACT.Exp,
                              scale=wf[:, 0:1] if layer == 0 else HD ** -0.5).then_inc(at_exp, 1)
                for g in range(3):
                    ac.wait_ge(yT_done, 3 * layer + g + 1)
                    if g == 2:
                        o = yT[:, :, 4 * NB:5 * NB].rearrange("p (a) b -> p a b")
                        i = bank[g][:, 0:P].rearrange("p (a b) -> p a b", a=2)
                    else:
                        o = yT[:, :, 0:4 * NB].rearrange("p a (u v b) -> p u v a b", u=2, v=2)[:, :, g, :, :]
                        i = bank[g][:, 0:2 * P].rearrange("p (t a b) -> p t a b", t=2, a=2)
                    copy(o, i).then_inc(yT_ready, 1)

            attention(0, 0)

            for j in range(3):
                tokens_T(1, j)
            ac.wait_ge(rt_arg, 1)
            ac.activation(lg[:, :, :], lg[:, :, :], ACT.Exp).then_inc(rt_exp, 1)
            for i in range(NM):
                if i == 2:
                    ac.wait_ge(c3T_done, 1)
                    copy(c3T[:, :], bank[3][0:3 * E, 0:256].bitcast(BF16)[:, 0:NTOK]).then_inc(c3T_ready, 1)
                ac.wait_ge(gu_done, i + 1)
                if i >= 2:
                    ac.wait_ge(gu_used, i - 1)
                ac.activation(th[:, i % 2, 0:NTOK], bank[4 + i % 2][:, 0:NTOK], ACT.Tanh, scale=0.5).then_inc(th_ready, 1)

            attention(2, 1)

            for j in range(3):
                ac.wait_ge(xqT_done, j + 1)
                copy(xqT[:, :, j * P:j * P + ROWS[j]],
                     bank[j][:, 0:P].bitcast(BF16).rearrange("p (c n) -> p c n", c=KC)[:, :, 0:ROWS[j]]
                     ).then_inc(xqT_ready, 1)

            def ff_tanh(k):
                j = k // 2
                ac.wait_ge(fg_done, k + 1)
                ac.wait_ge(tscale_ready, j + 1)
                if k >= 2:
                    ac.wait_ge(fg_used, k - 1)
                r = ROWS[j]
                ac.activation(th[0:r, k % 2, :], bank[k % 2][0:r, :], ACT.Tanh,
                              scale=fx[0:r, 3, j:j + 1]).then_inc(fth_ready, 1)

            def ff_T(j):
                r = ROWS[j]
                ac.wait_ge(hqT_done, j + 1)
                if j:
                    ac.wait_ge(fd_done, j)
                copy(hqT[:, :, 0:r], bank[4][:, :].bitcast(BF16).rearrange("p (c n) -> p c n", c=NI)[:, :, 0:r]
                     ).then_inc(hqT_ready, 1)

            for k in range(4):
                ff_tanh(k)
            ff_T(0)
            ff_tanh(4)
            ff_tanh(5)
            ff_T(1)
            ff_T(2)

        @block.gpsimd
        def _(po):
            links = [0]

            def link(ins):
                links[0] += 1
                ins.then_inc(pchain, 1)
                po.wait_ge(pchain, links[0])

            po.memset(nhalf[:, :], -0.5).then_inc(consts_ready, 1)
            po.memset(ones[:, :], 1.0).then_inc(consts_ready, 1)
            po.memset(S[:, :, :, :], NEG).then_inc(consts_ready, 0 + 1)
            po.wait_ge(consts_ready, 3)

            def root(key, r=P):
                i = LN[key]
                po.wait_ge(var_ready, i + 1)
                link(po.tensor_scalar(veps[0:r, i:i + 1], mv[0:r, i, 1:2], EPS, None, ALU.add))
                po.tensor_tensor(rstd[0:r, i:i + 1], veps[0:r, i:i + 1], nhalf[0:r, :], ALU.pow).then_inc(rstd_ready, 1)

            def add_patch(i):
                w, t = i // NPATCH, i % NPATCH
                if t == 0:
                    return
                po.wait_ge(ev["conv"], i + 1)
                if t > 1:
                    po.wait_ge(red_added, 8 * w + t - 1)
                po.tensor_tensor(red[:, w, :], pe[:, i, :], pe[:, i - 1, :] if t == 1 else red[:, w, :],
                                 ALU.add).then_inc(red_added, 1)

            def quantise(src, dst, i, lim):
                link(po.tensor_scalar(src, src, winv[:, i:i + 1], MAGIC, ALU.mult, ALU.add))
                link(po.tensor_scalar(src, src, MAGIC - lim, MAGIC + lim, ALU.max, ALU.min))
                return po.tensor_scalar(dst, src, -MAGIC, None, ALU.add)

            root("cls")
            for i in range(NT):
                add_patch(i)
                root(("tile", i))
                if i == 9:
                    root(("q", 0))
            root(("q", 1))
            po.wait_ge(ev["sumA"], 1)
            a0 = at0w_sb[:, :, :, :].rearrange("p c a n -> p (c a n)")
            quantise(a0, a0, 0, 2.0).then_inc(at0q_ready, 1)
            a0 = at0p_sb[:, :, :].rearrange("p c n -> p (c n)")
            quantise(a0, a0, 1, 2.0).then_inc(at0q_ready, 1)
            root(("lo", 0))
            root(("lo", 1))
            for j in range(3):
                root(("at0", j), ROWS[j])
            for j in range(3):
                root(("moe", j), ROWS[j])
            po.wait_ge(scB_ready, 1)
            for i in range(3):
                quantise(ffw_sb[:, i, :], ffq_sb[:, i, :], 2 + i, 1.0).then_inc(ffq_ready, 1)
            for j in range(3):
                root(("at1", j), ROWS[j])
            for j in range(3):
                root(("ffn", j), ROWS[j])

        @block.vector
        def _(ve):
            links = [0]

            def link(ins):
                links[0] += 1
                ins.then_inc(chain, 1)
                ve.wait_ge(chain, links[0])

            def chunks(b):
                return bank[b][:, 0:KC * P].rearrange("p (c n) -> p c n", c=KC)

            def ln_stats(key, src, r=P):
                i = LN[key]
                link(ve.bn_stats(stats[0:r, i, :], src))
                ve.bn_aggr(mv[0:r, i, :], stats[0:r, i, :]).then_inc(var_ready, 1)

            def ln_norm(key, dst, src, r=P):
                i = LN[key]
                ve.wait_ge(rstd_ready, i + 1)
                return ve.tensor_scalar(dst, src, mv[0:r, i, 0:1], rstd[0:r, i:i + 1], ALU.subtract, ALU.mult)

            ve.wait_ge(ld_fr, 16)
            ln_stats("cls", fr[:, R_CLS, :])
            ln_norm("cls", xh[:, 0, :], fr[:, R_CLS, :]).then_inc(xh_ready, 1)
            ve.tensor_tensor(clsb[:, :], fr[0:NB, R_CLS, :], fr[0:NB, R_GAP, :], ALU.add)

            def stats_tile(i):
                ve.wait_ge(ev["conv"], i + 1)
                ln_stats(("tile", i), pe[:, i, :])

            def norm_tile(i):
                w, t = i // NPATCH, i % NPATCH
                ve.wait_ge(red_added, 8 * w + max(t, 1))
                ln_norm(("tile", i), pe[:, i, :], pe[:, i, :]).then_inc(norm_ready, 1)

            def query(w):
                ve.wait_ge(red_added, 8 * w + 8)
                link(ve.tensor_scalar(red[:, w, :], red[:, w, :], 1.0 / NPATCH, None, ALU.mult))
                ln_stats(("q", w), red[:, w, :])
                if w == 0:
                    ve.wait_ge(pe_step["clsT"], 1)
                ln_norm(("q", w), xh[:, w, :], red[:, w, :]).then_inc(xh_ready, 1)

            def class_query():
                ve.wait_ge(ev["gq"], 1)
                link(ve.tensor_tensor(gprod[:, :, :], tw[:, :, W_GKV:W_GKV + C], bc(gq[:, :], 1, KC), ALU.mult))
                ve.tensor_reduce(G[:, :, :], gprod[:, :, :].rearrange("p c (h d) -> p c h d", d=LD), AX.X,
                                 ALU.add).then_inc(g_ready, 1)

            def window_scores(g):
                w, t0 = g // 3, 3 * (g % 3)
                ve.wait_ge(ev["kv"], 3 * g + 3)
                ve.wait_ge(ev["q"], w + 1)
                link(ve.tensor_tensor(prod[:, t0:t0 + 3, :], kv[:, 3 * g:3 * g + 3, 0:C],
                                      bc(q_sb[:, w, :], 1, 3), ALU.mult))
                link(ve.tensor_reduce(sc[:, t0:t0 + 3, :],
                                      prod[:, t0:t0 + 3, :].rearrange("p t (h d) -> p t h d", d=LD), AX.X, ALU.add))

            def window_softmax(w):
                m, z = small[:, 0, 0:LH], small[:, 1, 0:LH]
                by_head = sc[:, :, :].rearrange("p t h -> p h t")
                link(ve.tensor_reduce(m, by_head, AX.X, ALU.max))
                ve.tensor_tensor(sc[:, :, :], sc[:, :, :], bc(m, 1, NPATCH), ALU.subtract).then_inc(local_arg, 1)
                ve.wait_ge(local_exp, w + 1)
                link(ve.tensor_reduce(z, by_head, AX.X, ALU.add))
                link(ve.reciprocal(z, z))
                link(ve.tensor_tensor(sc[:, :, :], sc[:, :, :], bc(z, 1, NPATCH), ALU.mult))

            def window_values(w):
                link(ve.tensor_tensor(prod[:, :, :].rearrange("p t (h d) -> p t h d", d=LD),
                                      kv[:, NPATCH * w:NPATCH * (w + 1), C:2 * C].rearrange("p t (h d) -> p t h d", d=LD),
                                      bc(sc[:, :, :], 3, LD), ALU.mult))
                if w:
                    ve.wait_ge(pe_step["aggT"], w)
                ve.tensor_reduce(agg[:, :], prod[:, :, :].rearrange("p t f -> p f t"), AX.X, ALU.add
                                 ).then_inc(agg_ready, 1)
                ve.wait_ge(agg_ready, w + 1)

            def local_out(w):
                link(ve.tensor_tensor(red[:, w, :], red[:, w, :], fr[:, R_LAP, :], ALU.add))
                ve.wait_ge(pe_step["proj"], w + 1)
                ve.tensor_tensor(lo[:, w, :], bank[7][:, 0:C], red[:, w, :], ALU.add).then_inc(ev["proj"], 1)
                ve.wait_ge(ev["proj"], w + 1)
                ln_stats(("lo", w), lo[:, w, :])
                ve.wait_ge(pe_step["qT"], w + 1)
                ln_norm(("lo", w), xh[:, w, :], lo[:, w, :]).then_inc(xh_ready, 1)
                ve.wait_ge(pe_step["mod"], w + 1)
                ve.tensor_tensor(h[:, w, :], bank[7][:, 0:C], fr[:, R_MOD, :], ALU.add).then_inc(ev["mod"], 1)

            def scales_a():
                ve.wait_ge(pe_step["sumA"], 1)
                for i, w in enumerate((at0w_sb.shape, at0p_sb.shape)):
                    n = float(np.prod(w))
                    last = ve.tensor_scalar(wsc[:, i:i + 1], bank[7][:, i:i + 1], 1.0 / n, 1e-8, ALU.mult, ALU.max)
                link(last)
                link(ve.reciprocal(winv[:, 0:2], wsc[:, 0:2]))
                link(ve.tensor_scalar(wf[:, 0:1], wsc[:, 0:1], wsc[:, 0:1], HD ** -0.5, ALU.mult, ALU.mult))
                ve.tensor_tensor(wf[:, 1:2], wsc[:, 0:1], wsc[:, 1:2], ALU.mult).then_inc(ev["sumA"], 1)

            for i in range(NT):
                stats_tile(i)
                if i >= 2:
                    norm_tile(i - 2)
                if i == 9:
                    query(0)
                if i == 10:
                    class_query()
                if i == 16:
                    scales_a()
                    window_scores(0)
            norm_tile(NT - 2)
            norm_tile(NT - 1)
            query(1)
            window_scores(1)
            window_scores(2)
            window_softmax(0)
            window_values(0)
            window_scores(3)
            window_scores(4)
            local_out(0)
            window_scores(5)
            window_softmax(1)
            window_values(1)
            local_out(1)

            by_image = gsc[:, :, :].rearrange("h s b -> h b s")
            ve.wait_ge(pe_step["gs"], 1)
            link(ve.tensor_copy(gsc[:, :, :], bank[5][0:LH, 0:2 * P].rearrange("h (s b) -> h s b", s=4)))
            link(ve.tensor_reduce(gsm[:, 0, :], by_image, AX.X, ALU.max))
            ve.tensor_tensor(gsc[:, :, :], gsc[:, :, :], bc(gsm[:, 0, :], 1, 4), ALU.subtract).then_inc(garg, 1)
            ve.wait_ge(gexp, 1)
            link(ve.tensor_reduce(gsm[:, 1, :], by_image, AX.X, ALU.add))
            link(ve.reciprocal(gsm[:, 2, :], gsm[:, 1, :]))
            ve.tensor_tensor(gsc[:, :, :], gsc[:, :, :], bc(gsm[:, 2, :], 1, 4), ALU.mult).then_inc(gp_ready, 1)
            ve.wait_ge(pe_step["pT"], 1)
            ve.tensor_copy(gpt[:, :, :], bank[3][:, 0:2 * LH].rearrange("p (w h) -> p w h", w=2)).then_inc(ev["pT"], 1)
            ve.wait_ge(ev["pT"], 1)
            ve.wait_ge(pe_step["gv"], 1)
            ve.tensor_tensor(pgv[:, :, :].rearrange("p w (h d) -> p w h d", d=LD),
                             bank[4][:, :].rearrange("p (w h d) -> p w h d", w=2, d=LD),
                             bc(gpt[:, :, :], 3, LD), ALU.mult).then_inc(ev["pgv"], 1)
            ve.wait_ge(ld_cst, 16)
            link(ve.tensor_copy(identb[:, :], ident))

            def norm_rows(n, name, tiles, dst):
                for j in tiles:
                    ln_stats((name, j), h[0:ROWS[j], j, :], ROWS[j])
                for j in tiles:
                    ln_norm((name, j), dst[0:ROWS[j], j, :], h[0:ROWS[j], j, :], ROWS[j]).then_inc(xn_ready, 1)

            ve.wait_ge(ev["mod"], 2)
            norm_rows(0, "at0", (0, 1), xn)
            ve.wait_ge(pe_step["cls"], 1)
            ve.tensor_tensor(h[0:NB, 2, :], bank[1][0:NB, 0:C], clsb[:, :], ALU.add).then_inc(ev["cls"], 1)
            ve.wait_ge(ev["cls"], 1)
            norm_rows(0, "at0", (2,), xn)

            def rotate(s):
                v = qkv[:, s, 0:2 * P].rearrange("p (g d) -> p g d", d=HD)
                cos = cst_sb[:, C_COS + HD * (s - 1):C_COS + HD * s]
                sin = cst_sb[:, C_SIN + HD * (s - 1):C_SIN + HD * s]
                half = HD // 2
                ve.tensor_tensor(rot[:, :, 0:half], v[:, :, half:HD], bc(sin[:, 0:half], 1, 2 * HH), ALU.mult)
                link(ve.tensor_tensor(rot[:, :, half:HD], v[:, :, 0:half], bc(sin[:, half:HD], 1, 2 * HH), ALU.mult))
                link(ve.tensor_tensor(v, v, bc(cos, 1, 2 * HH), ALU.mult))
                link(ve.tensor_tensor(v, v, rot[:, :, :], ALU.add))

            def attention(layer):
                for t in range(T):
                    ve.wait_ge(qkv_ready, T * layer + t + 1)
                    if layer == 1 and t:
                        rotate(t)
                    link(ve.tensor_tensor(aprod[:, 0:t + 1, :], qkv[:, 0:t + 1, P:2 * P],
                                          bc(qkv[:, t, 0:P], 1, t + 1), ALU.mult))
                    link(ve.tensor_reduce(S[:, t, :, 0:t + 1].rearrange("p h s -> p s h"),
                                          aprod[:, 0:t + 1, :].rearrange("p s (h d) -> p s h d", d=HD),
                                          AX.X, ALU.add))
                rows = S[:, :, :, :].rearrange("p t h s -> p (t h) s")
                m = S1[:, :, :].rearrange("p t h -> p (t h)")
                link(ve.tensor_reduce(m, rows, AX.X, ALU.max))
                ve.tensor_tensor(rows, rows, bc(m, 2, T), ALU.subtract).then_inc(at_arg, 1)
                ve.wait_ge(at_exp, layer + 1)
                link(ve.tensor_reduce(m, rows, AX.X, ALU.add))
                link(ve.reciprocal(m, m))
                link(ve.tensor_tensor(rows, rows, bc(m, 2, T), ALU.mult))
                for t in range(T):
                    v = qkv[:, 0:t + 1, 2 * P:3 * P].rearrange("p s (h d) -> p s h d", d=HD)
                    pr = bc(S[:, t, :, 0:t + 1].rearrange("p h s -> p s h"), 3, HD)
                    if layer == 1 and t == 0:
                        ve.wait_ge(yT_done, 3)
                    link(ve.tensor_tensor(aprod[:, 0:t + 1, :].rearrange("p s (h d) -> p s h d", d=HD), v, pr, ALU.mult))
                    ve.tensor_reduce(y[:, t, :], aprod[:, 0:t + 1, :].rearrange("p s f -> p f s"), AX.X, ALU.add
                                     ).then_inc(y_ready, 1)
                    ve.wait_ge(y_ready, T * layer + t + 1)
                if layer == 0:
                    link(ve.memset(S[:, :, :, :], NEG))
                for j in range(3):
                    r = ROWS[j]
                    ve.wait_ge(ao_done, 3 * layer + j + 1)
                    ve.scalar_tensor_tensor(h[0:r, j, :], bank[3 + j][0:r, 0:C], wf[0:r, 1:2] if layer == 0 else 1.0,
                                            h[0:r, j, :], ALU.mult, ALU.add).then_inc(h_ready, 1)
                    ve.wait_ge(h_ready, 6 * layer + j + 1)
                    ln_stats(("ffn" if layer else "moe", j), h[0:r, j, :], r)

            ve.wait_ge(consts_ready, 3)
            attention(0)

            for j in range(3):
                r = ROWS[j]
                if j == 0:
                    ve.wait_ge(xnT_done, 3)
                ln_norm(("moe", j), xn[0:r, j, :], h[0:r, j, :], r).then_inc(xn_ready, 1)
            ve.wait_ge(sumB_done, 1)
            link(ve.tensor_scalar(wsc[:, 2:5], bank[6][:, 0:3], 1.0 / (C * INNER), 1e-5, ALU.mult, ALU.max))
            ve.reciprocal(winv[:, 2:5], wsc[:, 2:5]).then_inc(scB_ready, 1)

            idx = bc(cst_sb[:, C_IDX:C_IDX + E], 1, 3)
            prob, left, is_max, rank, pick = (rt[:, i] for i in range(5))
            m, z, best = rs[:, 0], rs[:, 1], rs[:, 2]
            link(ve.memset(lg[:, :, :], 0.0))
            ve.wait_ge(rt_done, 1)
            ve.tensor_copy(lg[:, 0:2, :], bank[3][:, 0:2 * E].rearrange("p (j e) -> p j e", j=2))
            link(ve.tensor_copy(lg[0:NB, 2, :], bank[3][0:NB, 2 * E:3 * E]))
            link(ve.tensor_reduce(m, lg[:, :, :], AX.X, ALU.max))
            ve.tensor_tensor(lg[:, :, :], lg[:, :, :], bc(m, 2, E), ALU.subtract).then_inc(rt_arg, 1)
            ve.wait_ge(rt_exp, 1)
            link(ve.tensor_reduce(z, lg[:, :, :], AX.X, ALU.add))
            link(ve.reciprocal(z, z))
            link(ve.tensor_tensor(prob, lg[:, :, :], bc(z, 2, E), ALU.mult))
            src = prob
            for k in range(2):
                link(ve.tensor_reduce(m, src, AX.X, ALU.max))
                link(ve.tensor_tensor(is_max, src, bc(m, 2, E), ALU.is_ge))
                link(ve.tensor_tensor(rank, is_max, idx, ALU.mult))
                link(ve.tensor_reduce(best, rank, AX.X, ALU.max))
                if k == 0:
                    link(ve.tensor_tensor(pick, idx, bc(best, 2, E), ALU.is_equal))
                    link(ve.scalar_tensor_tensor(left.rearrange("p j e -> p (j e)"), pick.rearrange("p j e -> p (j e)"),
                                                 -2.0, prob.rearrange("p j e -> p (j e)"), ALU.mult, ALU.add))
                    src = left
                else:
                    link(ve.tensor_tensor(rank, idx, bc(best, 2, E), ALU.is_equal))
                    link(ve.tensor_tensor(pick, pick, rank, ALU.add))
            link(ve.tensor_tensor(prob, prob, pick, ALU.mult))
            for k in range(3):
                if k < 2:
                    link(ve.tensor_copy(c3[:, :, k, :], prob))
                    link(ve.tensor_tensor(prob, prob, c3[:, :, k, :], ALU.subtract))
                else:
                    ve.tensor_copy(c3[:, :, k, :], prob).then_inc(c3_ready, 1)
            for i in range(NM):
                a = act_a[:, i % 2, 0:NTOK]
                ve.wait_ge(th_ready, i + 1)
                link(ve.scalar_tensor_tensor(a, th[:, i % 2, 0:NTOK], 1.0, bank[4 + i % 2][:, 0:NTOK], ALU.add, ALU.mult))
                ve.scalar_tensor_tensor(a, a, 0.5, bank[6 + i % 2][:, 0:NTOK], ALU.mult, ALU.mult).then_inc(gu_used, 1)
                ve.wait_ge(gu_used, i + 1)
                if i >= 2:
                    ve.wait_ge(dn_done, i - 1)
                    ve.wait_ge(coef_done, i - 1)
                    ve.tensor_tensor(act_m[:, i % 2, :], a, bank[3][:, 0:NTOK], ALU.mult).then_inc(act_ready, 1)
                    ve.wait_ge(act_ready, i + 1)
                    ve.tensor_copy(rs[:, 3, 0:1], rs[:, 2, 0:1]).then_inc(coef_used, 1)
                else:
                    ve.tensor_copy(act_m[:, i % 2, :], a).then_inc(act_ready, 1)
            ve.wait_ge(dn_done, NM)
            for j in range(3):
                r = ROWS[j]
                ve.tensor_tensor(h[0:r, j, :], bank[j][0:r, 0:C], h[0:r, j, :], ALU.add).then_inc(h_ready, 1)
                ve.wait_ge(h_ready, 3 + j + 1)
                ln_stats(("at1", j), h[0:r, j, :], r)
            for j in range(3):
                r = ROWS[j]
                ln_norm(("at1", j), xn[0:r, j, :], h[0:r, j, :], r).then_inc(xn_ready, 1)

            attention(1)

            amax, sx, f1, fh, ah, ah2, sh, fo = (fx[:, i] for i in range(8))
            for j in range(3):
                r = ROWS[j]
                if j == 0:
                    ve.wait_ge(xnT_done, 9)
                link(ln_norm(("ffn", j), xn[0:r, j, :], h[0:r, j, :], r))
                link(ve.tensor_reduce(amax[0:r, j:j + 1], xn[0:r, j, :], AX.X, ALU.max, apply_absolute_value=True))
                link(ve.tensor_scalar(amax[0:r, j:j + 1], amax[0:r, j:j + 1], 1e-5, None, ALU.max))
                link(ve.reciprocal(sx[0:r, j:j + 1], amax[0:r, j:j + 1]))
                link(ve.tensor_scalar(sx[0:r, j:j + 1], sx[0:r, j:j + 1], 127.0, None, ALU.mult))
                link(ve.tensor_scalar(xn[0:r, j, :], xn[0:r, j, :], sx[0:r, j:j + 1], MAGIC, ALU.mult, ALU.add))
                ve.tensor_scalar(xq[0:r, j, :], xn[0:r, j, :], -MAGIC, None, ALU.add).then_inc(xq_ready, 1)
                link(ve.tensor_scalar(f1[0:r, j:j + 1], amax[0:r, j:j + 1], 1.0 / 127.0, wsc[0:r, 2:3], ALU.mult, ALU.mult))
                ve.tensor_scalar(fh[0:r, j:j + 1], f1[0:r, j:j + 1], 0.5, None, ALU.mult).then_inc(tscale_ready, 1)
                ve.wait_ge(tscale_ready, j + 1)
                link(ve.tensor_scalar(fo[0:r, j:j + 1], amax[0:r, j:j + 1], 1.0 / 127.0, wsc[0:r, 3:4], ALU.mult, ALU.mult))
                link(ve.tensor_tensor(fo[0:r, j:j + 1], fo[0:r, j:j + 1], fh[0:r, j:j + 1], ALU.mult))

            def ff_act(k):
                j, half = k // 2, k % 2
                r = ROWS[j]
                ve.wait_ge(fth_ready, k + 1)
                if half == 0 and j == 2:
                    pass
                a = act_a[0:r, k % 2, :]
                link(ve.scalar_tensor_tensor(a, th[0:r, k % 2, :], 1.0, bank[k % 2][0:r, :], ALU.add, ALU.mult))
                o = hm[0:r, j % 2, half * 512:(half + 1) * 512]
                ve.tensor_tensor(o, a, bank[2 + k % 2][0:r, :], ALU.mult).then_inc(fg_used, 1)
                ve.wait_ge(fg_used, k + 1)

            def ff_quant(j):
                r = ROWS[j]
                col = slice(j, j + 1)
                link(ve.tensor_reduce(ah[0:r, col], hm[0:r, j % 2, :], AX.X, ALU.max, apply_absolute_value=True))
                link(ve.tensor_scalar(ah2[0:r, col], ah[0:r, col], fo[0:r, col], 1e-5, ALU.mult, ALU.max))
                link(ve.reciprocal(sh[0:r, col], ah2[0:r, col]))
                link(ve.tensor_scalar(sh[0:r, col], sh[0:r, col], 127.0, fo[0:r, col], ALU.mult, ALU.mult))
                link(ve.tensor_scalar(hm[0:r, j % 2, :], hm[0:r, j % 2, :], sh[0:r, col], MAGIC, ALU.mult, ALU.add))
                if j == 2:
                    ve.wait_ge(hqT_done, 1)
                ve.tensor_scalar(hq[0:r, j % 2, :], hm[0:r, j % 2, :], -MAGIC, None, ALU.add).then_inc(hq_ready, 1)
                link(ve.tensor_scalar(ah[0:r, col], ah2[0:r, col], 1.0 / 127.0, wsc[0:r, 4:5], ALU.mult, ALU.mult))

            def ff_out(j):
                r = ROWS[j]
                ve.wait_ge(fd_done, j + 1)
                ve.scalar_tensor_tensor(h[0:r, j, :], bank[5 + j][0:r, 0:C], ah[0:r, j:j + 1], h[0:r, j, :],
                                        ALU.mult, ALU.add).then_inc(h_ready, 1)

            ff_act(0)
            ff_act(1)
            ff_quant(0)
            ff_act(2)
            ff_act(3)
            ff_quant(1)
            ff_out(0)
            ff_act(4)
            ff_act(5)
            ff_quant(2)
            ff_out(1)
            ff_out(2)


MOE_ORDER = [8, 9] + list(range(E))


def kernel(**inputs):
    import ml_dtypes
    import concourse.bacc as _bacc
    from concourse.bass_utils import run_bass_kernel_spmd as _run

    a = {k: np.asarray(v) for k, v in inputs.items()}

    def rows(w):
        return w.reshape(w.shape[0] // P, P, w.shape[1]).transpose(1, 0, 2)

    xk = a["x"].reshape(NB, 3, 2, 3, 14, 2, 3, 14).transpose(1, 4, 7, 5, 3, 6, 2, 0).reshape(CONV_K, NT * P)
    cw = a["L0_tok_conv_w"].reshape(C, CONV_K).T
    t = lambda n: a["L0_tok_" + n]
    tokw = rows(np.concatenate([t("la_wq"), t("la_wkv"), t("la_proj_w"), t("mod_w"), t("ga_wq"), t("ga_wkv"),
                                t("ga_proj_w")], axis=1))
    fcols = np.stack([t(n) for n in ("la_ln_q_g", "la_ln_q_b", "la_ln_kv_g", "la_ln_kv_b", "ga_ln_q_g", "ga_ln_q_b",
                                     "ga_ln_kv_g", "ga_ln_kv_b")]).reshape(8, KC, P).transpose(2, 0, 1)
    frows = np.stack([t("la_proj_b"), t("ga_proj_b"), t("mod_b"), t("class_emb")])

    def halves(w):
        return rows(w.T.reshape(C, 3, 2, P).transpose(0, 2, 1, 3).reshape(C, 6 * P)).reshape(P, KC, 2, 3 * P)

    at1 = np.concatenate([a["L1_attn_Wq"], a["L1_attn_Wk"], a["L1_attn_Wv"]])
    eg, eu = (a["L0_ffn_experts_" + n].transpose(1, 0, 2) for n in ("gate", "up"))
    sg, su = (a["L0_ffn_shared_" + n].reshape(C, 2, P) for n in ("gate", "up"))
    gu = np.stack([np.concatenate([eg, sg], axis=1), np.concatenate([eu, su], axis=1)], axis=2)
    moe_gu = gu.reshape(KC, P, NM, 2, P).transpose(1, 2, 3, 0, 4)
    moe_d = np.concatenate([a["L0_ffn_experts_down"], a["L0_ffn_shared_down"].reshape(2, P, C)]).transpose(1, 0, 2)

    cst = np.zeros((P, C_END), np.float32)
    cst[:, C_ID:C_ID + P] = np.eye(P)
    cst[:, C_FOLD:C_FOLD + NB] = np.tile(np.eye(NB), (2, 1))
    cst[:, C_IDX:C_IDX + E] = np.arange(E, 0, -1)
    freq = (1.0 / np.float32(10000.0) ** (np.arange(0, HD, 2, dtype=np.float32) / HD)).astype(np.float32)
    ang = np.arange(1, T, dtype=np.float32)[:, None] * freq[None, :]
    cst[:, C_COS:C_SIN] = np.concatenate([np.cos(ang), np.cos(ang)], axis=1).reshape(1, -1)
    cst[:, C_SIN:C_END] = np.concatenate([-np.sin(ang), np.sin(ang)], axis=1).reshape(1, -1)
    sel = np.zeros((3 * E, E, P), ml_dtypes.bfloat16)
    for k in range(3 * E):
        sel[k, k % E, :] = 1

    ins = {"xk": xk, "cw": cw, "cst": cst, "sel": sel, "fcols": fcols, "frows": frows, "tokw": tokw,
           "at0w": halves(a["L0_attn_w_attn"]), "at0p": rows(a["L0_attn_w_proj"].T), "router": rows(a["L0_ffn_router"]),
           "moe_gu": moe_gu, "moe_d": moe_d, "at1w": halves(at1), "at1p": rows(a["L1_attn_Wo"].T),
           "ffg": rows(a["L1_ffn_w_gate"].T).reshape(P, -1), "ffu": rows(a["L1_ffn_w_up"].T).reshape(P, -1),
           "ffd": rows(a["L1_ffn_w_down"].T).reshape(P, -1)}
    nc = _bacc.Bacc("TRN2", target_bir_lowering=False, num_devices=1)
    arrays, args = {}, []
    for name, v in ins.items():
        v = np.ascontiguousarray(v)
        arrays[f"in_{name}"] = v
        args.append(nc.dram_tensor(f"in_{name}", v.shape, mybir.dt.from_np(v.dtype), kind="ExternalInput").ap())
    out = nc.dram_tensor("out_0", (NB, T, C), F32, kind="ExternalOutput").ap()
    vit_tower(nc, *args, out)
    r = _run(nc, [arrays], core_ids=[0])
    return r.results[0]["out_0"]
```

```python
from contextlib import ExitStack

import numpy as np

import concourse.bass as bass
from concourse import mybir

F32 = mybir.dt.float32
BF16 = mybir.dt.bfloat16
ALU = mybir.AluOpType
ACT = mybir.ActivationFunctionType
AX = mybir.AxisListType

P = 128
C = 256
KC = C // P
NB = 64
T = 5
NTOK = NB * T
CONV_K = 3 * 14 * 14
CK = 5
CP = 120
NPATCH = 9
X_LOADS = [0, 1, 3, 6, 9, 12, 15, 18]
NT = 2 * NPATCH
LH, LD = 8, 32
HH = 8
HD = 16
E = 8
NM = E + 2
INNER = 1024
NI = INNER // P
EPS = 1e-5
MAGIC = 12582912.0
BLK = [0, 2, 1, 3, 4]
ROWS = [P, P, NB]
NEG = -3.0e38

C_ID, C_FOLD, C_IDX, C_COS, C_SIN, C_END = 0, 128, 192, 200, 264, 328
W_Q, W_KV, W_P, W_M, W_GQ, W_GKV, W_GP, W_END = 0, 256, 768, 1024, 1280, 1536, 2048, 2304
R_LAP, R_GAP, R_MOD, R_CLS = range(4)
G_LQ, G_LKV, G_GQ, G_GKV = 0, 2, 4, 6


def tokenizer_steps():
    s = [("conv", i) for i in range(NPATCH + 1)]
    s += [("T", 0), ("abs0", 0), ("conv", 10), ("T", 1), ("kv", 0), ("sumA", 0), ("T", 2), ("kv", 1)]
    beside = {11: [("qT", 0)], 12: [("q", 0)], 14: [("exp", 0)], 15: [("clsT", 0)],
              16: [("gq", 0)], 17: [("aggT", 0)]}
    t = 3
    for i in range(11, NT):
        s += [("conv", i)] + beside.get(i, [])
        for _ in range(3 if i < 14 else 1):
            if t < 12:
                s += [("T", t)] + ([("kv", t - 1)] if t <= NPATCH else [])
                t += 1
    beside = {9: [("proj", 0)], 12: [("qT", 1)], 13: [("q", 1)], 14: [("loT", 0)], 15: [("mod", 0)],
              16: [("lnloT", 0)]}
    for i in range(9, NT):
        if i + 3 < NT:
            s += [("T", i + 3)]
        s += [("K", i)] + beside.get(i, [])
    beside = {10: [("exp", 1)]}
    for i in range(9, NT):
        s += [("V", i)] + beside.get(i, [])
    s += [("xT", 0), ("qkv", 0), ("aggT", 1), ("proj", 1), ("qkv", 2), ("loT", 1), ("mod", 1), ("lnloT", 1),
          ("gs", 0), ("xT", 1), ("gexp", 0), ("gv", 0), ("qkv", 1), ("pT", 0), ("qkv", 3), ("fold", 0), ("cls", 0),
          ("exp4", 0), ("xT", 2), ("qkv", 4)]
    return s


LN_ORDER = ([("tile", i) for i in range(9)] + [("q", 0)] + [("tile", i) for i in range(9, 14)] + [("cls", 0)]
            + [("tile", i) for i in range(14, 18)] + [("q", 1), ("lo", 0), ("at0", 0), ("lo", 1), ("at0", 1), ("at0", 2)]
            + [(n, j) for n in ("moe", "at1", "ffn") for j in range(3)])
LN = {k: i for i, k in enumerate(LN_ORDER)}
NLN = len(LN_ORDER)


MOE_ORDER = [8, 9] + list(range(E))

XT_BANK = [(0, 0, 0), (0, 1, 2)]
QKV_BANK = [(3, 7, 2, 6, 3), (3, 4, 5, 6, 7)]
YT_BANK = [(0, 1, 2), (0, 1, 2)]
AO_BANK = [(4, 5, 7), (3, 4, 5)]


def vit_tower(nc, xk, cw, cst, sel_in, fcols, frows, tokw, at0w, at0p, router, moe_gu, moe_d,
              at1w, at1p, ffg, ffu, ffd, out):
    with ExitStack() as ctx:
        def sb(name, shape, dt=F32):
            return ctx.enter_context(nc.sbuf_tensor(name, shape, dt))

        def sem(name):
            return ctx.enter_context(nc.semaphore(name))

        def bc(ap, axis, n):
            shape = list(ap.shape)
            shape.insert(axis, n)
            return ap.unsqueeze(axis).broadcast_to(shape)

        bank = [ctx.enter_context(nc.psum_tensor(f"bank{i}", [P, 512], F32)) for i in range(8)]

        cst_sb = sb("cst_sb", [P, C_END])
        ident = cst_sb[:, C_ID:C_ID + P]
        fold = cst_sb[:, C_FOLD:C_FOLD + NB]
        sel = sb("sel", [3 * E, E, P], BF16)
        identb = sb("identb", [P, P], BF16)
        ones = sb("ones", [P, P])
        cw_sb = sb("cw_sb", [CP, CK, C])
        tw = sb("tw", [P, KC, W_END])
        fc = sb("fc", [P, 8, KC])
        fr = sb("fr", [P, 4, C])
        at0w_sb = sb("at0w_sb", [P, KC, 2, 3 * P])
        at0p_sb = sb("at0p_sb", [P, KC, C])
        at0w_flat = at0w_sb[:, :, :, :].rearrange("p c a n -> p (c a n)")
        at0p_flat = at0p_sb[:, :, :].rearrange("p c n -> p (c n)")
        router_sb = sb("router_sb", [P, KC, E])
        gu_sb = sb("gu_sb", [P, NM, 2, KC, P])

        x_sb = sb("x_sb", [P, CK, NT * P])
        pe = sb("pe", [P, NT, C])
        lnT = sb("lnT", [P, NPATCH, KC, P])
        red = sb("red", [P, 2, C])
        xh = sb("xh", [P, 3, C])
        qlnT = sb("qlnT", [P, KC, P])
        q_sb = sb("q_sb", [P, 2, C])
        kvb = sb("kvb", [P, 6 + NPATCH, C])
        hm = sb("hm", [P, 2, INNER])
        act_m = sb("act_m", [P, 2, NTOK])
        hqT = sb("hqT", [P, NI, P], BF16)
        prod = sb("prod", [P, NPATCH, C])
        sc = sb("sc", [P, NPATCH, LH])
        small = sb("small", [P, 4, 64])
        agg = sb("agg", [P, C])
        aggT = sb("aggT", [P, KC, P])
        lo = sb("lo", [P, 2, C])
        loT = sb("loT", [P, KC, P])
        lnloT = sb("lnloT", [P, KC, 2, P])
        clsT = sb("clsT", [P, KC, P])
        gq = sb("gq", [P, C])
        gprod = sb("gprod", [P, KC, C])
        G = sb("G", [P, KC, LH])
        gsc = sb("gsc", [LH, 4, NB])
        gsm = sb("gsm", [LH, 4, NB])
        gpt = sb("gpt", [P, 2, LH])
        pgv = sb("pgv", [P, 2, C])
        gfold = sb("gfold", [P, KC, NB])
        clsb = sb("clsb", [NB, C])

        def views(whole, *shapes):
            at, got = 0, []
            for shape in shapes:
                dt = F32
                if shape[-1] is BF16:
                    shape, dt = shape[:-1], BF16
                n = int(np.prod(shape)) // (2 if dt is BF16 else 1)
                part = whole[:, at:at + n]
                if dt is BF16:
                    part = part.bitcast(BF16)
                names = "abcd"[:len(shape)]
                dims = dict(zip(names[1:], shape[1:]))
                got.append(part.rearrange(f"p ({' '.join(names)}) -> p {' '.join(names)}", **dims))
                at += n
            assert at <= whole.shape[1]
            return got

        ffw_sb, at1w_sb, at1p_sb, dn_sb = views(
            x_sb[:, :, :].rearrange("p c n -> p (c n)"), (3, 2 * INNER), (KC, 2, 3 * P), (KC, C), (NM, C))
        qkv, aprod, y, yT = views(kvb[:, :, :].rearrange("p i n -> p (i n)"), (T, 3 * P), (T, P), (T, P), (KC, NTOK))
        th, act_a = views(lnT[:, :, :, :].rearrange("p i c n -> p (i c n)"), (2, 512), (2, 512))
        ffq_sb, xn, xT = views(pe[:, :, :].rearrange("p i n -> p (i n)"), (3, 2 * INNER, BF16), (3, C), (KC, NTOK))
        xqT, rot = views(prod[:, :, :].rearrange("p t n -> p (t n)"), (KC, NTOK, BF16), (2, 2 * HH, HD))
        gateq = ffq_sb[:, 0, :].rearrange("p (c n) -> p c n", c=KC)
        upq = ffq_sb[:, 1, :].rearrange("p (c n) -> p c n", c=KC)
        downq = ffq_sb[:, 2, :].rearrange("p (c n) -> p c n", c=NI)

        h = sb("h", [P, 3, C])
        S = sb("S", [P, T, HH, T])
        S1 = sb("S1", [P, T, HH])
        lg = sb("lg", [P, 3, E])
        rt = sb("rt", [P, 6, 3, E])
        rs = sb("rs", [P, 4, 3])
        c3 = sb("c3", [P, 3, 3, E], BF16)
        c3T = sb("c3T", [3 * E, NTOK], BF16)
        junk = sb("junk", [P, 2 * INNER], BF16)
        wsum = sb("wsum", [P, 5])
        wsc = sb("wsc", [P, 5])
        winv = sb("winv", [P, 5])
        wf = sb("wf", [P, 4])
        fx = sb("fx", [P, 8, 3])
        hmx = sb("hmx", [P, 2, 3])
        stats = sb("stats", [P, NLN, 6])
        mv = sb("mv", [P, NLN, 2])
        veps = sb("veps", [P, NLN])
        rstd = sb("rstd", [P, NLN])
        nhalf = sb("nhalf", [P, 1])
        magic = sb("magic", [P, 2])

        ld_cst, ld_sel, ld_fc, ld_fr = (sem(n) for n in ("ld_cst", "ld_sel", "ld_fc", "ld_fr"))
        ld_x = [sem(f"ld_x{i}") for i in range(7)]
        ld_cw = [sem(f"ld_cw{i}") for i in range(2)]
        ld_tq, ld_tkv, ld_tp, ld_tg = (sem(n) for n in ("ld_tq", "ld_tkv", "ld_tp", "ld_tg"))
        ld_at0, ld_rt, ld_at1 = sem("ld_at0"), sem("ld_rt"), sem("ld_at1")
        ld_gu = [sem(f"ld_gu{i}") for i in range(3)]
        ld_dn = sem("ld_dn")
        ld_ff = sem("ld_ff")
        chain = sem("chain")
        pchain = sem("pchain")
        var_ready, rstd_ready = sem("var_ready"), sem("rstd_ready")
        consts_ready = sem("consts_ready")
        xh_ready = sem("xh_ready")
        norm_ready = sem("norm_ready")
        red_added = sem("red_added")
        pe_step = {k: sem("pe_" + k) for k in
                   ("conv", "T", "kv", "K", "V", "clsT", "gq", "qT", "q", "aggT", "proj", "loT", "mod",
                    "lnloT", "gv", "gs", "pT", "fold", "cls", "sumA")}
        ev = {k: sem("ev_" + k) for k in
              ("conv", "T", "kv", "clsT", "gq", "qT", "q", "aggT", "proj", "loT", "mod", "lnloT",
               "gs", "pgv", "pT", "fold", "cls", "sumA")}
        local_exp, local_arg = sem("local_exp"), sem("local_arg")
        scored = sem("scored")
        agg_ready = sem("agg_ready")
        g_ready = sem("g_ready")
        gexp, garg = sem("gexp"), sem("garg")
        gp_ready = sem("gp_ready")
        abs_done = sem("abs_done")
        intA = sem("intA")
        scaledB, intB = sem("scaledB"), sem("intB")
        xn_ready = sem("xn_ready")
        xnT_done, xT_ready = sem("xnT_done"), sem("xT_ready")
        qkv_done, qkv_ready = sem("qkv_done"), sem("qkv_ready")
        at_arg, at_exp = sem("at_arg"), sem("at_exp")
        rot_ready, rot_used = sem("rot_ready"), sem("rot_used")
        y_ready, yT_done, yT_ready, ao_done = sem("y_ready"), sem("yT_done"), sem("yT_ready"), sem("ao_done")
        h_ready = sem("h_ready")
        rt_done, rt_arg, rt_exp, c3_ready, c3T_done, c3T_ready = (
            sem(n) for n in ("rt_done", "rt_arg", "rt_exp", "c3_ready", "c3T_done", "c3T_ready"))
        lg_read = sem("lg_read")
        coef_done = sem("coef_done")
        acc_done = sem("acc_done")
        gu_done, th_ready, gu_used, act_ready, dn_done = (
            sem(n) for n in ("gu_done", "th_ready", "gu_used", "act_ready", "dn_done"))
        scB_ready = sem("scB_ready")
        xq_ready, xqT_done, xqT_ready = sem("xq_ready"), sem("xqT_done"), sem("xqT_ready")
        hs_ready = sem("hs_ready")
        fg_done, fth_ready, fg_used = sem("fg_done"), sem("fth_ready"), sem("fg_used")
        hq_ready, hqT_done, hqT_ready, fd_done = sem("hq_ready"), sem("hqT_done"), sem("hqT_ready"), sem("fd_done")
        tscale_ready = sem("tscale_ready")
        stored = sem("stored")

        STEPS = tokenizer_steps()
        block = ctx.enter_context(nc.Block())

        @block.sync
        def _(sp):
            xmain = xk.rearrange("(c p) n -> p c n", p=CP)
            cmain = cw.rearrange("(c p) n -> p c n", p=CP)

            def load_x(g):
                cols = slice(X_LOADS[g] * P, X_LOADS[g + 1] * P)
                sp.dma_start(x_sb[0:CP, :, cols], xmain[:, :, cols]).then_inc(ld_x[g], 16)

            load_x(0)
            sp.dma_start(cw_sb[:, 0:2, :], cmain[:, 0:2, :]).then_inc(ld_cw[0], 16)
            sp.dma_start(cw_sb[:, 2:CK, :], cmain[:, 2:CK, :]).then_inc(ld_cw[1], 16)
            load_x(1)
            load_x(2)
            sp.dma_start(fc[:, :, :], fcols).then_inc(ld_fc, 16)
            sp.dma_start(cst_sb[:, :], cst).then_inc(ld_cst, 16)
            load_x(3)
            sp.dma_start(tw[:, :, W_Q:W_KV], tokw[:, :, W_Q:W_KV]).then_inc(ld_tq, 16)
            sp.dma_start(tw[:, :, W_KV:W_P], tokw[:, :, W_KV:W_P]).then_inc(ld_tkv, 16)
            load_x(4)
            sp.dma_start(at0w_sb[:, :, :, :], at0w).then_inc(ld_at0, 16)
            sp.dma_start(at0p_sb[:, :, :], at0p).then_inc(ld_at0, 16)
            load_x(5)
            sp.dma_start(fr[:, :, :], bc(frows, 0, P)).then_inc(ld_fr, 16)
            load_x(6)
            sp.dma_start(tw[:, :, W_GQ:W_END], tokw[:, :, W_GQ:W_END]).then_inc(ld_tg, 16)
            sp.dma_start(tw[:, :, W_P:W_GQ], tokw[:, :, W_P:W_GQ]).then_inc(ld_tp, 16)
            sp.dma_start(router_sb[:, :, :], router).then_inc(ld_rt, 16)
            sp.dma_start(sel[:, :, :], sel_in).then_inc(ld_sel, 16)
            sp.dma_start(gu_sb[:, 8:10], moe_gu[:, 8:10]).then_inc(ld_gu[0], 16)
            sp.dma_start(gu_sb[:, 0:4], moe_gu[:, 0:4]).then_inc(ld_gu[1], 16)
            sp.dma_start(gu_sb[:, 4:8], moe_gu[:, 4:8]).then_inc(ld_gu[2], 16)
            sp.wait_ge(pe_step["conv"], NT)
            sp.dma_start(dn_sb[:, :, :], moe_d).then_inc(ld_dn, 16)
            for i, w in enumerate((ffg, ffu, ffd)):
                sp.dma_start(ffw_sb[:, i, :], w).then_inc(ld_ff, 16)
            sp.dma_start(at1w_sb[:, :, :, :], at1w).then_inc(ld_at1, 16)
            sp.dma_start(at1p_sb[:, :, :], at1p).then_inc(ld_at1, 16)
            for s in (0, 2, 1, 3, 4):
                j, half = BLK[s] // 2, BLK[s] % 2
                sp.wait_ge(h_ready, 9 + j + 1)
                sp.dma_start(out[:, s, :], h[half * NB:(half + 1) * NB, j, :]).then_inc(stored, 16)
            sp.wait_ge(stored, 16 * T)

        @block.tensor
        def _(te):
            def mm(o, l, r, c, n):
                return te.matmul(o, l, r, start=(c == 0), stop=(c == n - 1))

            def turn(o, src, np_):
                for c in range(KC):
                    last = te.transpose(o[:, c, 0:np_], src[0:np_, c * P:(c + 1) * P], ident[0:np_, 0:np_])
                return last

            def chunks(b, n=P):
                return bank[b][:, 0:KC * P].rearrange("p (c n) -> p c n", c=KC)

            def conv(i):
                if i in X_LOADS:
                    te.wait_ge(ld_x[X_LOADS.index(i)], 16)
                if i >= 2:
                    te.wait_ge(ev["conv"], i - 1)
                cols = slice(i * P, (i + 1) * P)
                for c in range(CK):
                    if i == 0 and c in (0, 2):
                        te.wait_ge(ld_cw[c // 2], 16)
                    last = mm(bank[i % 2][:, 0:C], x_sb[0:CP, c, cols], cw_sb[:, c, :], c, CK)
                last.then_inc(pe_step["conv"], 1)

            def tile_T(i):
                te.wait_ge(norm_ready, i + 1)
                if i >= 2:
                    te.wait_ge(ev["T"], i - 1)
                if i == 0:
                    te.wait_ge(ld_cst, 16)
                turn(chunks(2 + i % 2), pe[:, i, :], P).then_inc(pe_step["T"], 1)

            def key_value(u, i, c0, c1):
                if u == 0:
                    te.wait_ge(ld_tkv, 16)
                te.wait_ge(ev["T"], i + 1)
                if u >= 2:
                    te.wait_ge(ev["kv"], u - 1)
                for c in range(KC):
                    last = mm(bank[4 + u % 2][:, 0:c1 - c0], lnT[:, i % NPATCH, c, :], tw[:, c, W_KV + c0:W_KV + c1], c, KC)
                return last

            def tile_kv(i):
                key_value(i, i, 0, 2 * C).then_inc(pe_step["kv"], 1)

            def tile_k(i):
                key_value(i, i, 0, C).then_inc(pe_step["K"], 1)

            def tile_v(i):
                key_value(i + NPATCH, i, C, 2 * C).then_inc(pe_step["V"], 1)

            def cls_T(_):
                te.wait_ge(ld_cst, 16)
                te.wait_ge(xh_ready, 2)
                te.wait_ge(ev["qT"], 1)
                turn(chunks(6), xh[:, 2, :], P).then_inc(pe_step["clsT"], 1)

            def cls_q(_):
                te.wait_ge(ld_tg, 16)
                te.wait_ge(ev["clsT"], 1)
                te.wait_ge(ev["q"], 1)
                for c in range(KC):
                    last = mm(bank[7][:, 0:C], clsT[:, c, :], tw[:, c, W_GQ:W_GKV], c, KC)
                last.then_inc(pe_step["gq"], 1)

            def q_T(w):
                te.wait_ge(xh_ready, 1 + 2 * w)
                if w:
                    te.wait_ge(ev["aggT"], 1)
                turn(chunks(6), xh[:, w, :], P).then_inc(pe_step["qT"], 1)

            def q_mm(w):
                if w == 0:
                    te.wait_ge(ld_tq, 16)
                te.wait_ge(ev["proj"] if w else ev["sumA"], 1)
                te.wait_ge(ev["qT"], w + 1)
                for c in range(KC):
                    last = mm(bank[7][:, 0:C], qlnT[:, c, :], tw[:, c, W_Q:W_KV], c, KC)
                last.then_inc(pe_step["q"], 1)

            def sum_a(_):
                te.wait_ge(abs_done, 2)
                te.wait_ge(consts_ready, 5)
                mm(bank[7][:, 0:2], ones[:, :], wsum[:, 0:2], 0, 1).then_inc(pe_step["sumA"], 1)

            def agg_T(w):
                te.wait_ge(agg_ready, w + 1)
                te.wait_ge(ev["lnloT"] if w else ev["clsT"], 1)
                turn(chunks(6), agg[:, :], P).then_inc(pe_step["aggT"], 1)

            def proj(w):
                if w == 0:
                    te.wait_ge(ld_tp, 16)
                te.wait_ge(ev["mod"] if w else ev["gq"], 1)
                te.wait_ge(ev["aggT"], w + 1)
                for c in range(KC):
                    last = mm(bank[7][:, 0:C], aggT[:, c, :], tw[:, c, W_P:W_M], c, KC)
                last.then_inc(pe_step["proj"], 1)

            def lo_T(w):
                te.wait_ge(ev["proj"], w + 1)
                te.wait_ge(ev["aggT"] if w else ev["qT"], 2)
                turn(chunks(6), lo[:, w, :], P).then_inc(pe_step["loT"], 1)

            def mod(w):
                te.wait_ge(ev["loT"], w + 1)
                te.wait_ge(ev["proj"] if w else ev["q"], 2)
                for c in range(KC):
                    last = mm(bank[7][:, 0:C], loT[:, c, :], tw[:, c, W_M:W_GQ], c, KC)
                last.then_inc(pe_step["mod"], 1)

            def lnlo_T(w):
                te.wait_ge(xh_ready, 4 + w)
                te.wait_ge(ev["loT"], w + 1)
                turn(chunks(6), xh[:, w, :], P).then_inc(pe_step["lnloT"], 1)

            def g_scores(_):
                te.wait_ge(g_ready, 1)
                te.wait_ge(ev["lnloT"], 2)
                te.wait_ge(ev["conv"], NT)
                for c in range(KC):
                    last = mm(bank[1][0:LH, 0:2 * P], G[:, c, :], lnloT[:, c, :, :], c, KC)
                last.then_inc(pe_step["gs"], 1)

            def g_v(_):
                te.wait_ge(ev["kv"], 3 * NPATCH)
                for w in range(2):
                    for c in range(KC):
                        last = mm(bank[4][:, w * C:(w + 1) * C], lnloT[:, c, w, :],
                                  tw[:, c, W_GKV + C:W_GP], c, KC)
                last.then_inc(pe_step["gv"], 1)

            def p_T(_):
                te.wait_ge(gp_ready, 1)
                gs = gsc[:, :, :].rearrange("h (w a) b -> h w (a b)", w=2)
                for w in range(2):
                    last = te.transpose(bank[1][:, w * LH:(w + 1) * LH], gs[:, w, :], ident[0:LH, 0:LH])
                last.then_inc(pe_step["pT"], 1)

            def fold_halves(_):
                te.wait_ge(ev["pgv"], 1)
                for c in range(KC):
                    for w in range(2):
                        last = mm(bank[5][:, c * NB:(c + 1) * NB], pgv[:, w, c * P:(c + 1) * P], fold, w, 2)
                last.then_inc(pe_step["fold"], 1)

            def cls_out(_):
                te.wait_ge(ev["fold"], 1)
                for c in range(KC):
                    last = mm(bank[5][0:NB, C:2 * C], gfold[:, c, :], tw[:, c, W_GP:W_END], c, KC)
                last.then_inc(pe_step["cls"], 1)

            def tokens_T(n, j, b):
                te.wait_ge(xn_ready, 3 * n + j + 1)
                turn(chunks(b), xn[:, j, :], ROWS[j]).then_inc(xnT_done, 1)

            def token_qkv(layer, s, w):
                te.wait_ge(xT_ready, 6 * layer + BLK[s] // 2 + 1)
                rows = slice(BLK[s] * NB, (BLK[s] + 1) * NB)
                for hh in range(2):
                    for c in range(KC):
                        last = mm(bank[QKV_BANK[layer][s]][hh * NB:(hh + 1) * NB, 0:3 * P], xT[:, c, rows],
                                  w[:, c, hh, :], c, KC)
                last.then_inc(qkv_done, 1)

            def first_T(j):
                if j == 0:
                    te.wait_ge(ev["conv"], NT)
                else:
                    te.wait_ge(xT_ready, j)
                tokens_T(0, j, XT_BANK[0][j])

            def first_qkv(s):
                if s == 0:
                    te.wait_ge(intA, 2)
                    te.wait_ge(ev["T"], NT)
                if s == 1:
                    te.wait_ge(ev["mod"], 2)
                if s == 3:
                    te.wait_ge(ev["lnloT"], 2)
                if s == 4:
                    te.wait_ge(qkv_ready, 1)
                token_qkv(0, s, at0w_sb)

            def attention_out(layer, wp):
                def y_T(g, ts):
                    te.wait_ge(y_ready, T * layer + ts[-1] + 1)
                    for i, t in enumerate(ts):
                        last = te.transpose(bank[YT_BANK[layer][g]][:, i * P:(i + 1) * P], y[:, t, :], ident)
                    last.then_inc(yT_done, 1)

                def project(j):
                    te.wait_ge(yT_ready, 3 * layer + (2 if j < 2 else 3))
                    for c in range(KC):
                        last = mm(bank[AO_BANK[layer][j]][0:ROWS[j], 0:C], yT[:, c, j * P:j * P + ROWS[j]],
                                  wp[:, c, :], c, KC)
                    last.then_inc(ao_done, 1)

                te.wait_ge(xT_ready, 6 * layer + 3)
                y_T(0, (0, 1))
                y_T(1, (2, 3))
                te.wait_ge(qkv_ready, T * layer + T)
                project(0)
                project(1)
                y_T(2, (4,))
                project(2)

            run = {"conv": conv, "T": tile_T, "kv": tile_kv, "K": tile_k, "V": tile_v, "clsT": cls_T, "gq": cls_q,
                   "qT": q_T, "q": q_mm, "sumA": sum_a, "aggT": agg_T, "proj": proj, "loT": lo_T, "mod": mod,
                   "lnloT": lnlo_T, "gs": g_scores, "gv": g_v, "pT": p_T, "fold": fold_halves, "cls": cls_out,
                   "xT": first_T, "qkv": first_qkv}
            for kind, i in STEPS:
                if kind in run:
                    run[kind](i)
            attention_out(0, at0p_sb)

            te.wait_ge(yT_ready, 3)
            for j in range(3):
                tokens_T(1, j, j)
            te.wait_ge(ld_rt, 16)
            te.wait_ge(h_ready, 3)
            for j in range(3):
                te.wait_ge(xT_ready, 3 + j + 1)
                for c in range(KC):
                    last = mm(bank[3][0:ROWS[j], j * E:(j + 1) * E], xT[:, c, j * P:j * P + ROWS[j]],
                              router_sb[:, c, :], c, KC)
            last.then_inc(rt_done, 1)

            def gate_up(i):
                m = MOE_ORDER[i]
                if i == 0:
                    te.wait_ge(ld_gu[0], 16)
                if i == 2:
                    te.wait_ge(ld_gu[1], 16)
                if i == 6:
                    te.wait_ge(ld_gu[2], 16)
                if i >= 2:
                    te.wait_ge(gu_used, i - 1)
                for gu in range(2):
                    for c in range(KC):
                        last = mm(bank[4 + 2 * gu + i % 2][:, 0:NTOK], gu_sb[:, m, gu, c, :], xT[:, c, :], c, KC)
                last.then_inc(gu_done, 1)

            def coef_rows(i):
                m = MOE_ORDER[i]
                if i == 2:
                    te.wait_ge(c3T_ready, 1)
                else:
                    te.wait_ge(act_ready, i)
                last = mm(bank[3][:, 0:NTOK], sel[:, m, :], c3T[:, :], 0, 1)
                if i == 4:
                    te.wait_ge(abs_done, 5)
                    last = mm(bank[3][:, 384:387], ones[:, :], wsum[:, 2:5], 0, 1)
                last.then_inc(coef_done, 1)

            def down(i):
                m = MOE_ORDER[i]
                if i == 0:
                    te.wait_ge(ld_dn, 16)
                te.wait_ge(act_ready, i + 1)
                for j in range(3):
                    last = mm(bank[j][0:ROWS[j], 0:C], act_m[:, i % 2, j * P:j * P + ROWS[j]], dn_sb[:, m, :], i, NM)
                    if i == NM - 1:
                        last.then_inc(acc_done, 1)
                if i < NM - 1:
                    last.then_inc(dn_done, 1)

            gate_up(0)
            gate_up(1)
            te.wait_ge(ld_sel, 16)
            te.wait_ge(consts_ready, 5)
            te.wait_ge(c3_ready, 1)
            bankb = bank[3][0:3 * E, 0:256].bitcast(BF16)
            for j in range(3):
                last = te.transpose(bankb[:, j * P:j * P + ROWS[j]],
                                    c3[0:ROWS[j], j, :, :].rearrange("p a e -> p (a e)"),
                                    identb[0:ROWS[j], 0:ROWS[j]])
            last.then_inc(c3T_done, 1)
            for i in range(2, NM):
                gate_up(i)
                coef_rows(i)
                down(i - 2)
            down(NM - 2)
            down(NM - 1)

            te.wait_ge(ld_at1, 32)
            for j in range(3):
                te.wait_ge(h_ready, 3 + j + 1)
                tokens_T(2, j, XT_BANK[1][j])
            for s in range(T):
                token_qkv(1, s, at1w_sb)
            attention_out(1, at1p_sb)

            def grid_T(j):
                te.wait_ge(xq_ready, j + 1)
                if j == 2:
                    te.wait_ge(xqT_ready, 1)
                turn(chunks(6 + j % 2), xn[:, j, :], ROWS[j]).then_inc(xqT_done, 1)

            def ff_up(k):
                j, half = k // 2, k % 2
                te.wait_ge(xqT_ready, j + 1)
                if k >= 2:
                    te.wait_ge(fg_used, k - 1)
                for gu, wq in enumerate((gateq, upq)):
                    for c in range(KC):
                        last = mm(bank[2 * gu + k % 2][0:ROWS[j], :], xqT[:, c, j * P:j * P + ROWS[j]],
                                  wq[:, c, half * 512:(half + 1) * 512], c, KC)
                last.then_inc(fg_done, 1)

            def ff_down(j):
                r = ROWS[j]
                te.wait_ge(hs_ready, j + 1)
                for half in range(2):
                    if j:
                        te.wait_ge(hqT_ready, 2 * j - 1 + half)
                    for c in range(NI // 2):
                        k = half * NI // 2 + c
                        last = te.transpose(bank[4 + half][:, c * P:c * P + r], hm[0:r, j % 2, k * P:(k + 1) * P],
                                            ident[0:r, 0:r])
                    last.then_inc(hqT_done, 1)
                if j == 0:
                    te.wait_ge(xqT_ready, 3)
                if j == 2:
                    te.wait_ge(h_ready, 10)
                for c in range(NI):
                    if c % (NI // 2) == 0:
                        te.wait_ge(hqT_ready, 2 * j + 1 + c // (NI // 2))
                    last = mm(bank[6 + j % 2][0:r, 0:C], hqT[:, c, 0:r], downq[:, c, :], c, NI)
                last.then_inc(fd_done, 1)

            te.wait_ge(intB, 3)
            te.wait_ge(h_ready, 9)
            grid_T(0)
            ff_up(0)
            grid_T(1)
            ff_up(1)
            grid_T(2)
            ff_up(2)
            ff_up(3)
            ff_down(0)
            ff_up(4)
            ff_up(5)
            ff_down(1)
            ff_down(2)

        @block.scalar
        def _(ac):
            def copy(o, i):
                return ac.activation(o, i, ACT.Copy)

            def chunks(b):
                return bank[b][:, 0:KC * P].rearrange("p (c n) -> p c n", c=KC)

            def affine(o, b, g):
                for c in range(KC):
                    last = ac.activation(o(c), chunks(b)[:, c, :], ACT.Identity,
                                         bias=fc[:, g + 1, c:c + 1], scale=fc[:, g, c:c + 1])
                return last

            def conv(i):
                ac.wait_ge(pe_step["conv"], i + 1)
                copy(pe[:, i, :], bank[i % 2][:, 0:C]).then_inc(ev["conv"], 1)

            def tile_T(i):
                ac.wait_ge(pe_step["T"], i + 1)
                if i == 0:
                    ac.wait_ge(ld_fc, 16)
                if i >= NPATCH:
                    ac.wait_ge(pe_step["kv"], i - NPATCH + 1)
                affine(lambda c: lnT[:, i % NPATCH, c, :], 2 + i % 2, G_LKV).then_inc(ev["T"], 1)

            def tile_kv(i):
                ac.wait_ge(pe_step["kv"], i + 1)
                if i >= 6:
                    ac.wait_ge(scored, i // 3 - 1)
                k, v = i % 6, 6 + i
                copy(kvb[:, k:v + 1:v - k, :], bank[4 + i % 2][:, :].rearrange("p (a n) -> p a n", a=2)
                     ).then_inc(ev["kv"], 1)

            def tile_k(i):
                ac.wait_ge(pe_step["K"], i - NPATCH + 1)
                ac.wait_ge(scored, i // 3 - 1)
                copy(kvb[:, i % 6, :], bank[4 + i % 2][:, 0:C]).then_inc(ev["kv"], 1)

            def tile_v(i):
                ac.wait_ge(pe_step["V"], i - NPATCH + 1)
                ac.wait_ge(agg_ready, 1)
                copy(kvb[:, 6 + i - NPATCH, :], bank[4 + (i + NPATCH) % 2][:, 0:C]).then_inc(ev["kv"], 1)

            def cls_T(_):
                ac.wait_ge(pe_step["clsT"], 1)
                affine(lambda c: clsT[:, c, :], 6, G_GQ).then_inc(ev["clsT"], 1)

            def cls_q(_):
                ac.wait_ge(pe_step["gq"], 1)
                copy(gq[:, :], bank[7][:, 0:C]).then_inc(ev["gq"], 1)

            def q_T(w):
                if w == 0:
                    ac.wait_ge(ld_fc, 16)
                ac.wait_ge(pe_step["qT"], w + 1)
                if w:
                    ac.wait_ge(pe_step["q"], w)
                affine(lambda c: qlnT[:, c, :], 6, G_LQ).then_inc(ev["qT"], 1)

            def q_mm(w):
                ac.wait_ge(pe_step["q"], w + 1)
                ac.activation(q_sb[:, w, :], bank[7][:, 0:C], ACT.Copy, scale=float(C) ** -0.5).then_inc(ev["q"], 1)

            def exp_local(w):
                ac.wait_ge(local_arg, w + 1)
                ac.activation(sc[:, :, :], sc[:, :, :], ACT.Exp).then_inc(local_exp, 1)

            def agg_T(w):
                ac.wait_ge(pe_step["aggT"], w + 1)
                copy(aggT[:, :, :], chunks(6)).then_inc(ev["aggT"], 1)

            def lo_T(w):
                ac.wait_ge(pe_step["loT"], w + 1)
                copy(loT[:, :, :], chunks(6)).then_inc(ev["loT"], 1)

            def lnlo_T(w):
                ac.wait_ge(pe_step["lnloT"], w + 1)
                affine(lambda c: lnloT[:, c, w, :], 6, G_GKV).then_inc(ev["lnloT"], 1)

            def abs_sums(lots, first):
                for n, (i, src) in enumerate(lots):
                    if first + n:
                        ac.wait_ge(abs_done, first + n)
                    ac.activation(junk[:, 0:src.shape[1]], src, ACT.Abs, accum_out=wsum[:, i:i + 1]).then_inc(abs_done, 1)

            def abs_a(_):
                ac.wait_ge(ld_at0, 32)
                abs_sums([(0, at0w_flat), (1, at0p_flat)], 0)

            def exp_global(_):
                ac.wait_ge(garg, 1)
                ac.activation(gsc[:, :, :], gsc[:, :, :], ACT.Exp, scale=float(C) ** -0.5).then_inc(gexp, 1)

            def fold_halves(_):
                ac.wait_ge(pe_step["fold"], 1)
                copy(gfold[:, :, :], bank[5][:, 0:KC * NB].rearrange("p (c n) -> p c n", c=KC)).then_inc(ev["fold"], 1)

            def tokens_T(n, j, b):
                ac.wait_ge(xnT_done, 3 * n + j + 1)
                r = ROWS[j]
                copy(xT[:, :, j * P:j * P + r], chunks(b)[:, :, 0:r]).then_inc(xT_ready, 1)

            def token_qkv(layer, n, s):
                ac.wait_ge(qkv_done, T * layer + n + 1)
                copy(qkv[:, s, :], bank[QKV_BANK[layer][s]][:, 0:3 * P]).then_inc(qkv_ready, 1)

            def exp_scores(layer, k):
                part = S[:, 0:4, :, :] if k == 0 else S[:, 4, :, :]
                ac.wait_ge(at_arg, 2 * layer + k + 1)
                ac.activation(part, part, ACT.Exp, scale=wf[:, 0:1] if layer == 0 else HD ** -0.5).then_inc(at_exp, 1)

            def y_T(layer, g):
                ac.wait_ge(yT_done, 3 * layer + g + 1)
                if g == 2:
                    o = yT[:, :, 4 * NB:5 * NB]
                    i = bank[YT_BANK[layer][g]][:, 0:P].rearrange("p (a b) -> p a b", a=2)
                else:
                    o = yT[:, :, 0:4 * NB].rearrange("p a (u v b) -> p u v a b", u=2, v=2)[:, :, g, :, :]
                    i = bank[YT_BANK[layer][g]][:, 0:2 * P].rearrange("p (t a b) -> p t a b", t=2, a=2)
                copy(o, i).then_inc(yT_ready, 1)

            run = {"conv": conv, "T": tile_T, "kv": tile_kv, "K": tile_k, "V": tile_v, "clsT": cls_T, "gq": cls_q,
                   "qT": q_T, "q": q_mm, "abs0": abs_a, "aggT": agg_T, "loT": lo_T,
                   "lnloT": lnlo_T, "gexp": exp_global, "exp": exp_local, "fold": fold_halves, "exp4": lambda _: exp_scores(0, 0),
                   "xT": lambda j: tokens_T(0, j, XT_BANK[0][j]),
                   "qkv": lambda s: token_qkv(0, [i for k, i in STEPS if k == "qkv"].index(s), s)}
            for kind, i in STEPS:
                if kind in run:
                    run[kind](i)

            ac.wait_ge(ld_ff, 48)
            abs_sums([(2, ffw_sb[:, 0, :])], 2)
            y_T(0, 0)
            y_T(0, 1)
            exp_scores(0, 1)
            y_T(0, 2)

            for j in range(3):
                tokens_T(1, j, j)
            ac.wait_ge(rt_arg, 1)
            ac.activation(lg[:, :, :], lg[:, :, :], ACT.Exp).then_inc(rt_exp, 1)
            for i in range(NM):
                if i == 2:
                    ac.wait_ge(c3T_done, 1)
                    copy(c3T[:, :], bank[3][0:3 * E, 0:256].bitcast(BF16)[:, 0:NTOK]).then_inc(c3T_ready, 1)
                ac.wait_ge(gu_done, i + 1)
                if i >= 2:
                    ac.wait_ge(gu_used, i - 1)
                ac.activation(th[:, i % 2, 0:NTOK], bank[4 + i % 2][:, 0:NTOK], ACT.Tanh, scale=0.5).then_inc(th_ready, 1)
                if i < 2:
                    abs_sums([(3 + i, ffw_sb[:, 1 + i, :])], 3 + i)
                elif 4 <= i < 7:
                    k = i - 4
                    if k == 0:
                        ac.wait_ge(scB_ready, 1)
                    ac.activation(ffw_sb[:, k, :], ffw_sb[:, k, :], ACT.Copy,
                                  scale=winv[:, 2 + k:3 + k]).then_inc(scaledB, 1)

            for j in range(3):
                tokens_T(2, j, XT_BANK[1][j])
            for s in range(T):
                token_qkv(1, s, s)
            exp_scores(1, 0)
            exp_scores(1, 1)
            ac.activation(junk[:, 0:1], magic[:, 0:1], ACT.Silu).then_inc(abs_done, 1)
            for g in range(3):
                y_T(1, g)

            def grid_T(j):
                ac.wait_ge(xqT_done, j + 1)
                ac.activation(xqT[:, :, j * P:j * P + ROWS[j]], chunks(6 + j % 2)[:, :, 0:ROWS[j]], ACT.Identity,
                              bias=magic[:, 1:2]).then_inc(xqT_ready, 1)

            def ff_tanh(k):
                j = k // 2
                ac.wait_ge(fg_done, k + 1)
                ac.wait_ge(tscale_ready, j + 1)
                if k >= 2:
                    ac.wait_ge(fg_used, k - 1)
                r = ROWS[j]
                ac.activation(th[0:r, k % 2, :], bank[k % 2][0:r, :], ACT.Silu,
                              scale=fx[0:r, 3, j:j + 1]).then_inc(fth_ready, 1)

            def ff_grid(j):
                r = ROWS[j]
                ac.wait_ge(hq_ready, j + 1)
                ac.activation(hm[0:r, j % 2, :], hm[0:r, j % 2, :], ACT.Identity, bias=magic[0:r, 0:1],
                              scale=fx[0:r, 6, j:j + 1]).then_inc(hs_ready, 1)

            def ff_T(j):
                r = ROWS[j]
                for half in range(2):
                    ac.wait_ge(hqT_done, 2 * j + half + 1)
                    if j:
                        ac.wait_ge(fd_done, j)
                    ac.activation(hqT[:, half * NI // 2:(half + 1) * NI // 2, 0:r],
                                  bank[4 + half][:, :].rearrange("p (c n) -> p c n", c=NI // 2)[:, :, 0:r],
                                  ACT.Identity, bias=magic[:, 1:2]).then_inc(hqT_ready, 1)

            grid_T(0)
            ff_tanh(0)
            grid_T(1)
            ff_tanh(1)
            grid_T(2)
            ff_tanh(2)
            ff_grid(0)
            ff_tanh(3)
            ff_T(0)
            ff_tanh(4)
            ff_grid(1)
            ff_tanh(5)
            ff_T(1)
            ff_grid(2)
            ff_T(2)

        @block.gpsimd
        def _(po):
            links = [0]

            def link(ins):
                links[0] += 1
                ins.then_inc(pchain, 1)
                po.wait_ge(pchain, links[0])

            po.memset(nhalf[:, :], -0.5).then_inc(consts_ready, 1)
            po.memset(ones[:, :], 1.0).then_inc(consts_ready, 1)
            po.memset(magic[:, 0:1], MAGIC).then_inc(consts_ready, 1)
            po.memset(magic[:, 1:2], -MAGIC).then_inc(consts_ready, 1)
            po.memset(S[:, :, :, :], NEG).then_inc(consts_ready, 1)
            po.wait_ge(consts_ready, 5)

            def root(key):
                r = ROWS[key[1]] if key[0] in ("at0", "moe", "at1", "ffn") else P
                i = LN[key]
                po.wait_ge(var_ready, i + 1)
                link(po.tensor_scalar(veps[0:r, i:i + 1], mv[0:r, i, 1:2], EPS, None, ALU.add))
                po.tensor_tensor(rstd[0:r, i:i + 1], veps[0:r, i:i + 1], nhalf[0:r, :], ALU.pow).then_inc(rstd_ready, 1)

            def add_patch(i):
                w, t = i // NPATCH, i % NPATCH
                if t == 0:
                    return
                po.wait_ge(ev["conv"], i + 1)
                if t > 1:
                    po.wait_ge(red_added, 8 * w + t - 1)
                po.tensor_tensor(red[:, w, :], pe[:, i, :], pe[:, i - 1, :] if t == 1 else red[:, w, :],
                                 ALU.add).then_inc(red_added, 1)

            for key in LN_ORDER:
                if key == ("at1", 0):
                    break
                if key[0] == "tile" and key[1] < NT - 2:
                    add_patch(key[1])
                if key in (("tile", NT - 3), ("tile", NT - 2)):
                    add_patch(key[1] + 1)
                root(key)
            for j in range(3):
                root(("at1", j))

            def swap_halves(s):
                half = HD // 2
                v = qkv[:, s, 0:2 * P].rearrange("p (g d) -> p g d", d=HD)
                sin = cst_sb[:, C_SIN + HD * (s - 1):C_SIN + HD * s]
                if s > 2:
                    po.wait_ge(rot_used, s - 2)
                po.wait_ge(qkv_ready, T + s + 1)
                po.tensor_tensor(rot[:, s % 2, :, 0:half], v[:, :, half:HD], bc(sin[:, 0:half], 1, 2 * HH),
                                 ALU.mult).then_inc(rot_ready, 1)
                po.tensor_tensor(rot[:, s % 2, :, half:HD], v[:, :, 0:half], bc(sin[:, half:HD], 1, 2 * HH),
                                 ALU.mult).then_inc(rot_ready, 1)

            for s in range(1, T):
                swap_halves(s)
            for j in range(3):
                root(("ffn", j))

        @block.vector
        def _(ve):
            links = [0]

            def link(ins):
                links[0] += 1
                ins.then_inc(chain, 1)
                ve.wait_ge(chain, links[0])

            def chunks(b):
                return bank[b][:, 0:KC * P].rearrange("p (c n) -> p c n", c=KC)

            def ln_stats(key, src, r=P):
                i = LN[key]
                link(ve.bn_stats(stats[0:r, i, :], src))
                ve.bn_aggr(mv[0:r, i, :], stats[0:r, i, :]).then_inc(var_ready, 1)

            def ln_norm(key, dst, src, r=P):
                i = LN[key]
                ve.wait_ge(rstd_ready, i + 1)
                return ve.tensor_scalar(dst, src, mv[0:r, i, 0:1], rstd[0:r, i:i + 1], ALU.subtract, ALU.mult)

            def class_row():
                ve.wait_ge(ld_fr, 16)
                ln_stats(("cls", 0), fr[:, R_CLS, :])
                ve.tensor_tensor(clsb[:, :], fr[0:NB, R_CLS, :], fr[0:NB, R_GAP, :], ALU.add)
                ln_norm(("cls", 0), xh[:, 2, :], fr[:, R_CLS, :]).then_inc(xh_ready, 1)

            def stats_tile(i):
                ve.wait_ge(ev["conv"], i + 1)
                ln_stats(("tile", i), pe[:, i, :])

            def norm_tile(i):
                w, t = i // NPATCH, i % NPATCH
                ve.wait_ge(red_added, 8 * w + max(t, 1))
                ln_norm(("tile", i), pe[:, i, :], pe[:, i, :]).then_inc(norm_ready, 1)

            def query_stats(w):
                ve.wait_ge(red_added, 8 * w + 8)
                link(ve.tensor_scalar(red[:, w, :], red[:, w, :], 1.0 / NPATCH, None, ALU.mult))
                ln_stats(("q", w), red[:, w, :])

            def query_norm(w):
                ln_norm(("q", w), xh[:, w, :], red[:, w, :]).then_inc(xh_ready, 1)

            def class_query():
                ve.wait_ge(ev["gq"], 1)
                link(ve.tensor_tensor(gprod[:, :, :], tw[:, :, W_GKV:W_GKV + C], bc(gq[:, :], 1, KC), ALU.mult))
                ve.tensor_reduce(G[:, :, :], gprod[:, :, :].rearrange("p c (h d) -> p c h d", d=LD), AX.X,
                                 ALU.add).then_inc(g_ready, 1)

            def window_scores(g):
                w, t0 = g // 3, 3 * (g % 3)
                ve.wait_ge(ev["kv"], 3 * g + 3)
                ve.wait_ge(ev["q"], w + 1)
                k0 = 3 * (g % 2)
                link(ve.tensor_tensor(prod[:, t0:t0 + 3, :], kvb[:, k0:k0 + 3, :], bc(q_sb[:, w, :], 1, 3), ALU.mult
                                      ))
                ve.tensor_reduce(sc[:, t0:t0 + 3, :], prod[:, t0:t0 + 3, :].rearrange("p t (h d) -> p t h d", d=LD),
                                 AX.X, ALU.add).then_inc(scored, 1)
                ve.wait_ge(scored, g + 1)

            def window_softmax(w):
                m, z = small[:, 0, 0:LH], small[:, 1, 0:LH]
                by_head = sc[:, :, :].rearrange("p t h -> p h t")
                link(ve.tensor_reduce(m, by_head, AX.X, ALU.max))
                ve.tensor_tensor(sc[:, :, :], sc[:, :, :], bc(m, 1, NPATCH), ALU.subtract).then_inc(local_arg, 1)
                ve.wait_ge(local_exp, w + 1)
                link(ve.tensor_reduce(z, by_head, AX.X, ALU.add))
                link(ve.reciprocal(z, z))
                link(ve.tensor_tensor(sc[:, :, :], sc[:, :, :], bc(z, 1, NPATCH), ALU.mult))

            def weigh(t0, t1):
                return ve.tensor_tensor(prod[:, t0:t1, :].rearrange("p t (h d) -> p t h d", d=LD),
                                        kvb[:, 6 + t0:6 + t1, :].rearrange("p t (h d) -> p t h d", d=LD),
                                        bc(sc[:, t0:t1, :], 3, LD), ALU.mult)

            def window_values_first():
                ve.tensor_reduce(agg[:, :], prod[:, :, :].rearrange("p t f -> p f t"), AX.X, ALU.add
                                 ).then_inc(agg_ready, 1)
                ve.wait_ge(agg_ready, 1)

            def window_values_second():
                ve.wait_ge(ev["kv"], 2 * NPATCH + 3)
                weigh(0, 3)
                ve.wait_ge(ev["kv"], 2 * NPATCH + 6)
                link(weigh(3, 6))
                ve.wait_ge(pe_step["aggT"], 1)
                link(ve.tensor_reduce(agg[:, :], prod[:, 0:6, :].rearrange("p t f -> p f t"), AX.X, ALU.add))
                for t in range(6, NPATCH):
                    ve.wait_ge(ev["kv"], 2 * NPATCH + t + 1)
                    link(weigh(t, t + 1))
                    last = ve.tensor_tensor(agg[:, :], agg[:, :], prod[:, t, :], ALU.add)
                    if t < NPATCH - 1:
                        link(last)
                last.then_inc(agg_ready, 1)

            def local_add(w):
                link(ve.tensor_tensor(red[:, w, :], red[:, w, :], fr[:, R_LAP, :], ALU.add))
                ve.wait_ge(pe_step["proj"], w + 1)
                ve.tensor_tensor(lo[:, w, :], bank[7][:, 0:C], red[:, w, :], ALU.add).then_inc(ev["proj"], 1)
                ve.wait_ge(ev["proj"], w + 1)
                ln_stats(("lo", w), lo[:, w, :])

            def local_norm(w):
                ve.wait_ge(pe_step["qT"], w + 1)
                ln_norm(("lo", w), xh[:, w, :], lo[:, w, :]).then_inc(xh_ready, 1)

            def trunk_rows(w):
                ve.wait_ge(pe_step["mod"], w + 1)
                ve.tensor_tensor(h[:, w, :], bank[7][:, 0:C], fr[:, R_MOD, :], ALU.add).then_inc(ev["mod"], 1)
                ve.wait_ge(ev["mod"], w + 1)
                ln_stats(("at0", w), h[:, w, :])

            def trunk_norm(w):
                if w == 0:
                    ve.wait_ge(pe_step["T"], NT)
                ln_norm(("at0", w), xn[:, w, :], h[:, w, :]).then_inc(xn_ready, 1)

            def scales_a():
                ve.wait_ge(pe_step["sumA"], 1)
                for i, w in enumerate((at0w_sb.shape, at0p_sb.shape)):
                    n = float(np.prod(w))
                    last = ve.tensor_scalar(wsc[:, i:i + 1], bank[7][:, i:i + 1], 1.0 / n, 1e-8, ALU.mult, ALU.max)
                link(last)
                link(ve.reciprocal(winv[:, 0:2], wsc[:, 0:2]))
                link(ve.tensor_scalar(wf[:, 0:1], wsc[:, 0:1], wsc[:, 0:1], HD ** -0.5, ALU.mult, ALU.mult))
                ve.tensor_tensor(wf[:, 1:2], wsc[:, 0:1], wsc[:, 1:2], ALU.mult).then_inc(ev["sumA"], 1)

            def clipped_integers(o, w, top):
                link(ve.tensor_scalar(w, w, MAGIC, MAGIC + top, ALU.add, ALU.min))
                return ve.tensor_scalar(o, w, MAGIC - top, MAGIC, ALU.max, ALU.subtract)

            def integers_a():
                for i, w in enumerate((at0w_flat, at0p_flat)):
                    link(ve.tensor_scalar(w, w, winv[:, i:i + 1], MAGIC, ALU.mult, ALU.add))
                    link(ve.tensor_scalar(w, w, MAGIC - 2.0, MAGIC + 2.0, ALU.max, ALU.min))
                    ve.tensor_scalar(w, w, MAGIC, None, ALU.subtract).then_inc(intA, 1)

            for i in range(NT):
                stats_tile(i)
                if i >= 2:
                    norm_tile(i - 2)
                if i == 8:
                    query_stats(0)
                    query_norm(0)
                if i == 10:
                    scales_a()
                if i == 11:
                    integers_a()
                if i == 12:
                    window_scores(0)
                    window_scores(1)
                if i == 13:
                    class_row()
                    window_scores(2)
                    window_softmax(0)
                    link(weigh(0, NPATCH))
                if i == 14:
                    window_values_first()
            norm_tile(NT - 2)
            query_stats(1)
            norm_tile(NT - 1)
            query_norm(1)
            local_add(0)
            local_norm(0)
            window_scores(3)
            window_scores(4)
            trunk_rows(0)
            window_scores(5)
            trunk_norm(0)
            window_softmax(1)
            window_values_second()
            class_query()
            local_add(1)
            local_norm(1)
            trunk_rows(1)
            trunk_norm(1)

            def rotate(s):
                v = qkv[:, s, 0:2 * P].rearrange("p (g d) -> p g d", d=HD)
                cos = cst_sb[:, C_COS + HD * (s - 1):C_COS + HD * s]
                ve.wait_ge(rot_ready, 2 * s)
                link(ve.tensor_tensor(v, v, bc(cos, 1, 2 * HH), ALU.mult))
                ve.tensor_tensor(v, v, rot[:, s % 2, :, :], ALU.add).then_inc(rot_used, 1)
                ve.wait_ge(rot_used, s)

            def score(layer, n, t):
                ve.wait_ge(qkv_ready, T * layer + n)
                if layer == 1 and t:
                    rotate(t)
                link(ve.tensor_tensor(aprod[:, 0:t + 1, :], qkv[:, 0:t + 1, P:2 * P],
                                      bc(qkv[:, t, 0:P], 1, t + 1), ALU.mult))
                link(ve.tensor_reduce(S[:, t, :, 0:t + 1].rearrange("p h s -> p s h"),
                                      aprod[:, 0:t + 1, :].rearrange("p s (h d) -> p s h d", d=HD), AX.X, ALU.add))

            def softmax_part(k):
                t0, t1 = ((0, 4), (4, 5))[k]
                return (S[:, t0:t1, :, :].rearrange("p t h s -> p (t h) s"),
                        S1[:, t0:t1, :].rearrange("p t h -> p (t h)"))

            def softmax_shift(k):
                rows, m = softmax_part(k)
                link(ve.tensor_reduce(m, rows, AX.X, ALU.max))
                ve.tensor_tensor(rows, rows, bc(m, 2, T), ALU.subtract).then_inc(at_arg, 1)

            def softmax_divide(layer, k):
                rows, m = softmax_part(k)
                ve.wait_ge(at_exp, 2 * layer + k + 1)
                link(ve.tensor_reduce(m, rows, AX.X, ALU.add))
                link(ve.reciprocal(m, m))
                link(ve.tensor_tensor(rows, rows, bc(m, 2, T), ALU.mult))

            def values(layer, t):
                v = qkv[:, 0:t + 1, 2 * P:3 * P].rearrange("p s (h d) -> p s h d", d=HD)
                pr = bc(S[:, t, :, 0:t + 1].rearrange("p h s -> p s h"), 3, HD)
                link(ve.tensor_tensor(aprod[:, 0:t + 1, :].rearrange("p s (h d) -> p s h d", d=HD), v, pr, ALU.mult))
                ve.tensor_reduce(y[:, t, :], aprod[:, 0:t + 1, :].rearrange("p s f -> p f s"), AX.X, ALU.add
                                 ).then_inc(y_ready, 1)
                ve.wait_ge(y_ready, T * layer + t + 1)

            def add_attention(layer):
                for j in range(3):
                    r = ROWS[j]
                    ve.wait_ge(ao_done, 3 * layer + j + 1)
                    ve.scalar_tensor_tensor(h[0:r, j, :], bank[AO_BANK[layer][j]][0:r, 0:C],
                                            wf[0:r, 1:2] if layer == 0 else 1.0,
                                            h[0:r, j, :], ALU.mult, ALU.add).then_inc(h_ready, 1)
                    ve.wait_ge(h_ready, 6 * layer + j + 1)
                    ln_stats(("ffn" if layer else "moe", j), h[0:r, j, :], r)

            by_image = gsc[:, :, :].rearrange("h s b -> h b s")
            ve.wait_ge(consts_ready, 5)
            ve.wait_ge(ld_cst, 16)
            link(ve.tensor_copy(identb[:, :], ident))
            ve.wait_ge(pe_step["gs"], 1)
            link(ve.tensor_copy(gsc[:, :, :], bank[1][0:LH, 0:2 * P].rearrange("h (s b) -> h s b", s=4)))
            link(ve.tensor_reduce(gsm[:, 0, :], by_image, AX.X, ALU.max))
            ve.tensor_tensor(gsc[:, :, :], gsc[:, :, :], bc(gsm[:, 0, :], 1, 4), ALU.subtract).then_inc(garg, 1)
            score(0, 1, 0)
            ve.wait_ge(gexp, 1)
            link(ve.tensor_reduce(gsm[:, 1, :], by_image, AX.X, ALU.add))
            link(ve.reciprocal(gsm[:, 2, :], gsm[:, 1, :]))
            ve.tensor_tensor(gsc[:, :, :], gsc[:, :, :], bc(gsm[:, 2, :], 1, 4), ALU.mult).then_inc(gp_ready, 1)
            score(0, 3, 1)
            ve.wait_ge(pe_step["pT"], 1)
            ve.tensor_copy(gpt[:, :, :], bank[1][:, 0:2 * LH].rearrange("p (w h) -> p w h", w=2)).then_inc(ev["pT"], 1)
            ve.wait_ge(ev["pT"], 1)
            ve.wait_ge(pe_step["gv"], 1)
            ve.tensor_tensor(pgv[:, :, :].rearrange("p w (h d) -> p w h d", d=LD),
                             bank[4][:, :].rearrange("p (w h d) -> p w h d", w=2, d=LD),
                             bc(gpt[:, :, :], 3, LD), ALU.mult).then_inc(ev["pgv"], 1)
            score(0, 3, 2)
            score(0, 4, 3)
            softmax_shift(0)
            ve.wait_ge(pe_step["cls"], 1)
            ve.tensor_tensor(h[0:NB, 2, :], bank[5][0:NB, C:2 * C], clsb[:, :], ALU.add).then_inc(ev["cls"], 1)
            ve.wait_ge(ev["cls"], 1)
            ln_stats(("at0", 2), h[0:NB, 2, :], NB)
            softmax_divide(0, 0)
            ln_norm(("at0", 2), xn[0:NB, 2, :], h[0:NB, 2, :], NB).then_inc(xn_ready, 1)
            for t in range(4):
                values(0, t)
            score(0, 5, 4)
            softmax_shift(1)
            softmax_divide(0, 1)
            values(0, 4)
            link(ve.memset(S[:, :, :, :], NEG))
            add_attention(0)

            for j in range(3):
                r = ROWS[j]
                if j == 0:
                    ve.wait_ge(xnT_done, 3)
                ln_norm(("moe", j), xn[0:r, j, :], h[0:r, j, :], r).then_inc(xn_ready, 1)
            idx = bc(cst_sb[:, C_IDX:C_IDX + E], 1, 3)
            prob, left, is_max, rank, pick = (rt[:, i] for i in range(5))
            m, z, best = rs[:, 0], rs[:, 1], rs[:, 2]
            link(ve.memset(lg[:, :, :], 0.0))
            ve.wait_ge(rt_done, 1)
            ve.tensor_copy(lg[:, 0:2, :], bank[3][:, 0:2 * E].rearrange("p (j e) -> p j e", j=2))
            link(ve.tensor_copy(lg[0:NB, 2, :], bank[3][0:NB, 2 * E:3 * E]))
            link(ve.tensor_reduce(m, lg[:, :, :], AX.X, ALU.max))
            ve.tensor_tensor(lg[:, :, :], lg[:, :, :], bc(m, 2, E), ALU.subtract).then_inc(rt_arg, 1)
            ve.wait_ge(rt_exp, 1)
            link(ve.tensor_reduce(z, lg[:, :, :], AX.X, ALU.add))
            link(ve.reciprocal(z, z))
            link(ve.tensor_tensor(prob, lg[:, :, :], bc(z, 2, E), ALU.mult))
            src = prob
            for k in range(2):
                link(ve.tensor_reduce(m, src, AX.X, ALU.max))
                link(ve.tensor_tensor(is_max, src, bc(m, 2, E), ALU.is_ge))
                link(ve.tensor_tensor(rank, is_max, idx, ALU.mult))
                link(ve.tensor_reduce(best, rank, AX.X, ALU.max))
                if k == 0:
                    link(ve.tensor_tensor(pick, idx, bc(best, 2, E), ALU.is_equal))
                    link(ve.scalar_tensor_tensor(left.rearrange("p j e -> p (j e)"), pick.rearrange("p j e -> p (j e)"),
                                                 -2.0, prob.rearrange("p j e -> p (j e)"), ALU.mult, ALU.add))
                    src = left
                else:
                    link(ve.tensor_tensor(rank, idx, bc(best, 2, E), ALU.is_equal))
                    link(ve.tensor_tensor(pick, pick, rank, ALU.add))
            link(ve.tensor_tensor(prob, prob, pick, ALU.mult))
            for k in range(3):
                if k < 2:
                    link(ve.tensor_copy(c3[:, :, k, :], prob))
                    link(ve.tensor_tensor(prob, prob, c3[:, :, k, :], ALU.subtract))
                else:
                    ve.tensor_copy(c3[:, :, k, :], prob).then_inc(c3_ready, 1)
            for i in range(NM):
                a = act_a[:, i % 2, 0:NTOK]
                ve.wait_ge(th_ready, i + 1)
                link(ve.scalar_tensor_tensor(a, th[:, i % 2, 0:NTOK], 1.0, bank[4 + i % 2][:, 0:NTOK], ALU.add, ALU.mult))
                ve.scalar_tensor_tensor(a, a, 0.5, bank[6 + i % 2][:, 0:NTOK], ALU.mult, ALU.mult).then_inc(gu_used, 1)
                ve.wait_ge(gu_used, i + 1)
                if i >= 2:
                    ve.wait_ge(dn_done, i - 1)
                    ve.wait_ge(coef_done, i - 1)
                    if i == 4:
                        link(ve.tensor_scalar(wsc[:, 2:5], bank[3][:, 384:387], 1.0 / (C * INNER), 1e-5,
                                              ALU.mult, ALU.max))
                        ve.reciprocal(winv[:, 2:5], wsc[:, 2:5]).then_inc(scB_ready, 1)
                    ve.tensor_tensor(act_m[:, i % 2, :], a, bank[3][:, 0:NTOK], ALU.mult).then_inc(act_ready, 1)
                else:
                    ve.tensor_copy(act_m[:, i % 2, :], a).then_inc(act_ready, 1)
                if 6 <= i < 9:
                    k = i - 6
                    ve.wait_ge(scaledB, k + 1)
                    clipped_integers(ffq_sb[:, k, :], ffw_sb[:, k, :], 1.0).then_inc(intB, 1)
            for j in range(3):
                r = ROWS[j]
                ve.wait_ge(acc_done, j + 1)
                ve.tensor_tensor(h[0:r, j, :], bank[j][0:r, 0:C], h[0:r, j, :], ALU.add).then_inc(h_ready, 1)
                ve.wait_ge(h_ready, 3 + j + 1)
                ln_stats(("at1", j), h[0:r, j, :], r)
            for j in range(3):
                r = ROWS[j]
                ln_norm(("at1", j), xn[0:r, j, :], h[0:r, j, :], r).then_inc(xn_ready, 1)

            for t in range(4):
                score(1, t + 1, t)
            softmax_shift(0)
            score(1, 5, 4)
            softmax_shift(1)
            softmax_divide(1, 0)
            for t in range(4):
                values(1, t)
            softmax_divide(1, 1)
            values(1, 4)
            add_attention(1)

            amax, sx, unit, gscale, least, hsize, sh, fo = (fx[:, i] for i in range(8))

            def grid_tokens(j0, j1):
                cols = slice(j0, j1)
                for j in range(j0, j1):
                    r = ROWS[j]
                    ln_norm(("ffn", j), xn[0:r, j, :], h[0:r, j, :], r).then_inc(xn_ready, 1)
                for j in range(j0, j1):
                    r = ROWS[j]
                    ve.wait_ge(xn_ready, 9 + j + 1)
                    last = ve.tensor_reduce(amax[0:r, j:j + 1], xn[0:r, j, :], AX.X, ALU.max, apply_absolute_value=True)
                link(last)
                link(ve.tensor_scalar(amax[:, cols], amax[:, cols], 1.0 / 127.0, 1e-5 / 127.0, ALU.mult, ALU.max))
                link(ve.reciprocal(sx[:, cols], amax[:, cols]))
                for j in range(j0, j1):
                    r = ROWS[j]
                    ve.tensor_scalar(xn[0:r, j, :], xn[0:r, j, :], sx[0:r, j:j + 1], MAGIC, ALU.mult, ALU.add
                                     ).then_inc(xq_ready, 1)
                for j in range(j0, j1):
                    ve.tensor_scalar(gscale[:, j:j + 1], amax[:, j:j + 1], wsc[:, 2:3], None, ALU.mult
                                     ).then_inc(tscale_ready, 1)
                    last = ve.tensor_scalar(unit[:, j:j + 1], amax[:, j:j + 1], wsc[:, 3:4], None, ALU.mult)
                link(last)
                link(ve.reciprocal(least[:, cols], unit[:, cols]))
                link(ve.tensor_scalar(least[:, cols], least[:, cols], 1e-5 / 127.0, None, ALU.mult))

            def ff_act(k):
                j, half = k // 2, k % 2
                r = ROWS[j]
                ve.wait_ge(fth_ready, k + 1)
                if j == 2:
                    ve.wait_ge(hqT_done, 2)
                o = hm[0:r, j % 2, half * 512:(half + 1) * 512]
                ve.tensor_tensor(o, th[0:r, k % 2, :], bank[2 + k % 2][0:r, :], ALU.mult).then_inc(fg_used, 1)
                ve.wait_ge(fg_used, k + 1)
                link(ve.tensor_reduce(hmx[0:r, half, j:j + 1], o, AX.X, ALU.max, apply_absolute_value=True))
                if half == 0:
                    link(ve.tensor_scalar(hmx[0:r, 0, j:j + 1], hmx[0:r, 0, j:j + 1], 1.0 / 127.0, least[0:r, j:j + 1],
                                          ALU.mult, ALU.max))

            def ff_scale(j):
                r = ROWS[j]
                col = slice(j, j + 1)
                link(ve.scalar_tensor_tensor(hsize[0:r, col], hmx[0:r, 1, col], 1.0 / 127.0, hmx[0:r, 0, col],
                                             ALU.mult, ALU.max))
                ve.reciprocal(sh[0:r, col], hsize[0:r, col]).then_inc(hq_ready, 1)
                link(ve.tensor_scalar(fo[0:r, col], hsize[0:r, col], unit[0:r, col], wsc[0:r, 4:5], ALU.mult, ALU.mult))

            def ff_out(j):
                r = ROWS[j]
                ve.wait_ge(fd_done, j + 1)
                ve.scalar_tensor_tensor(h[0:r, j, :], bank[6 + j % 2][0:r, 0:C], fo[0:r, j:j + 1], h[0:r, j, :],
                                        ALU.mult, ALU.add).then_inc(h_ready, 1)

            link(ve.memset(amax, 1.0))
            grid_tokens(0, 1)
            grid_tokens(1, 3)
            ff_act(0)
            ff_act(1)
            ff_scale(0)
            ff_act(2)
            ff_act(3)
            ff_scale(1)
            ff_out(0)
            ff_act(4)
            ff_act(5)
            ff_scale(2)
            ff_out(1)
            ff_out(2)


def kernel(**inputs):
    import ml_dtypes
    import concourse.bacc as _bacc
    from concourse.bass_utils import run_bass_kernel_spmd as _run

    a = {k: np.asarray(v) for k, v in inputs.items()}

    def rows(w):
        return w.reshape(w.shape[0] // P, P, w.shape[1]).transpose(1, 0, 2)

    xk = a["x"].reshape(NB, 3, 2, 3, 14, 2, 3, 14).transpose(1, 4, 7, 5, 3, 6, 2, 0).reshape(CONV_K, NT * P)
    cw = a["L0_tok_conv_w"].reshape(C, CONV_K).T
    xk, cw = (np.concatenate([m, np.zeros((CK * CP - CONV_K, m.shape[1]), m.dtype)]) for m in (xk, cw))
    t = lambda n: a["L0_tok_" + n]
    tokw = rows(np.concatenate([t("la_wq"), t("la_wkv"), t("la_proj_w"), t("mod_w"), t("ga_wq"), t("ga_wkv"),
                                t("ga_proj_w")], axis=1))
    fcols = np.stack([t(n) for n in ("la_ln_q_g", "la_ln_q_b", "la_ln_kv_g", "la_ln_kv_b", "ga_ln_q_g", "ga_ln_q_b",
                                     "ga_ln_kv_g", "ga_ln_kv_b")]).reshape(8, KC, P).transpose(2, 0, 1)
    frows = np.stack([t("la_proj_b"), t("ga_proj_b"), t("mod_b"), t("class_emb")])

    def halves(w):
        return rows(w.T.reshape(C, 3, 2, P).transpose(0, 2, 1, 3).reshape(C, 6 * P)).reshape(P, KC, 2, 3 * P)

    at1 = np.concatenate([a["L1_attn_Wq"], a["L1_attn_Wk"], a["L1_attn_Wv"]])
    eg, eu = (a["L0_ffn_experts_" + n].transpose(1, 0, 2) for n in ("gate", "up"))
    sg, su = (a["L0_ffn_shared_" + n].reshape(C, 2, P) for n in ("gate", "up"))
    gu = np.stack([np.concatenate([eg, sg], axis=1), np.concatenate([eu, su], axis=1)], axis=2)
    moe_gu = gu.reshape(KC, P, NM, 2, P).transpose(1, 2, 3, 0, 4)
    moe_d = np.concatenate([a["L0_ffn_experts_down"], a["L0_ffn_shared_down"].reshape(2, P, C)]).transpose(1, 0, 2)

    cst = np.zeros((P, C_END), np.float32)
    cst[:, C_ID:C_ID + P] = np.eye(P)
    cst[:, C_FOLD:C_FOLD + NB] = np.tile(np.eye(NB), (2, 1))
    cst[:, C_IDX:C_IDX + E] = np.arange(E, 0, -1)
    freq = (1.0 / np.float32(10000.0) ** (np.arange(0, HD, 2, dtype=np.float32) / HD)).astype(np.float32)
    ang = np.arange(1, T, dtype=np.float32)[:, None] * freq[None, :]
    cst[:, C_COS:C_SIN] = np.concatenate([np.cos(ang), np.cos(ang)], axis=1).reshape(1, -1)
    cst[:, C_SIN:C_END] = np.concatenate([-np.sin(ang), np.sin(ang)], axis=1).reshape(1, -1)
    sel = np.zeros((3 * E, E, P), ml_dtypes.bfloat16)
    for k in range(3 * E):
        sel[k, k % E, :] = 1

    ins = {"xk": xk, "cw": cw, "cst": cst, "sel": sel, "fcols": fcols, "frows": frows, "tokw": tokw,
           "at0w": halves(a["L0_attn_w_attn"]), "at0p": rows(a["L0_attn_w_proj"].T), "router": rows(a["L0_ffn_router"]),
           "moe_gu": moe_gu, "moe_d": moe_d, "at1w": halves(at1), "at1p": rows(a["L1_attn_Wo"].T),
           "ffg": rows(a["L1_ffn_w_gate"].T).reshape(P, -1), "ffu": rows(a["L1_ffn_w_up"].T).reshape(P, -1),
           "ffd": rows(a["L1_ffn_w_down"].T).reshape(P, -1)}
    nc = _bacc.Bacc("TRN2", target_bir_lowering=False, num_devices=1)
    arrays, args = {}, []
    for name, v in ins.items():
        v = np.ascontiguousarray(v)
        arrays[f"in_{name}"] = v
        args.append(nc.dram_tensor(f"in_{name}", v.shape, mybir.dt.from_np(v.dtype), kind="ExternalInput").ap())
    out = nc.dram_tensor("out_0", (NB, T, C), F32, kind="ExternalOutput").ap()
    vit_tower(nc, *args, out)
    r = _run(nc, [arrays], core_ids=[0])
    return r.results[0]["out_0"]
```

```python
from contextlib import ExitStack

import numpy as np

import concourse.bass as bass
from concourse import mybir

F32 = mybir.dt.float32
BF16 = mybir.dt.bfloat16
ALU = mybir.AluOpType
ACT = mybir.ActivationFunctionType
AX = mybir.AxisListType

P = 128
C = 256
KC = C // P
NB = 64
T = 5
NTOK = NB * T
CONV_K = 3 * 14 * 14
CK = 5
CP = 120
NPATCH = 9
X_LOADS = [0, 1, 3, 6, 9, 12, 15, 18]
NT = 2 * NPATCH
LH, LD = 8, 32
HH = 8
HD = 16
E = 8
NM = E + 2
INNER = 1024
NI = INNER // P
EPS = 1e-5
MAGIC = 12582912.0
BLK = [0, 2, 1, 3, 4]
ROWS = [P, P, NB]
NEG = -3.0e38

C_ID, C_FOLD, C_IDX, C_COS, C_SIN, C_END = 0, 128, 192, 200, 264, 328
W_Q, W_KV, W_P, W_M, W_GQ, W_GKV, W_GP, W_END = 0, 256, 768, 1024, 1280, 1536, 2048, 2304
R_LAP, R_GAP, R_MOD, R_CLS = range(4)
G_LQ, G_LKV, G_GQ, G_GKV = 0, 2, 4, 6


def tokenizer_steps():
    s = [("conv", i) for i in range(NPATCH + 1)]
    s += [("T", 0), ("abs0", 0), ("conv", 10), ("T", 1), ("kv", 0), ("sumA", 0), ("T", 2), ("kv", 1)]
    beside = {11: [("qT", 0)], 12: [("q", 0)], 14: [("exp", 0)], 15: [("clsT", 0)],
              16: [("gq", 0)], 17: [("aggT", 0)]}
    t = 3
    for i in range(11, NT):
        s += [("conv", i)] + beside.get(i, [])
        for _ in range(3 if i < 14 else 1):
            if t < 12:
                s += [("T", t)] + ([("kv", t - 1)] if t <= NPATCH else [])
                t += 1
    beside = {9: [("proj", 0)], 12: [("qT", 1)], 13: [("q", 1)], 14: [("loT", 0)], 15: [("mod", 0)],
              16: [("lnloT", 0)]}
    for i in range(9, NT):
        if i + 3 < NT:
            s += [("T", i + 3)]
        s += [("K", i)] + beside.get(i, [])
    beside = {10: [("exp", 1)]}
    for i in range(9, NT):
        s += [("V", i)] + beside.get(i, [])
    s += [("xT", 0), ("qkv", 0), ("aggT", 1), ("proj", 1), ("loT", 1), ("mod", 1), ("lnloT", 1),
          ("qkv", 2), ("gs", 0), ("xT", 1), ("gexp", 0), ("qkv", 1), ("qkv", 3), ("gv", 0), ("exp4", 0), ("absB", 0),
          ("yT", 0), ("yT", 1), ("absB", 1), ("pT", 0), ("ao", 0), ("ao", 1), ("fold", 0), ("cls", 0)]
    return s


LN_ORDER = ([("tile", i) for i in range(9)] + [("q", 0)] + [("tile", i) for i in range(9, 14)] + [("cls", 0)]
            + [("tile", i) for i in range(14, 18)] + [("q", 1), ("lo", 0), ("at0", 0), ("lo", 1), ("at0", 1)]
            + [("moe", 0), ("moe", 1), ("at0", 2), ("moe", 2)] + [(n, j) for n in ("at1", "ffn") for j in range(3)])
LN = {k: i for i, k in enumerate(LN_ORDER)}
NLN = len(LN_ORDER)
TRUNK_NORMS = ("at0", "moe", "at1", "ffn")
XN = {k: i for i, k in enumerate(k for k in LN_ORDER if k[0] in TRUNK_NORMS)}


POOL_INTS = 1
NAB = 2 * P
MOE_ORDER = [8, 9] + list(range(E))

FIRST_QKV = (0, 2, 1, 3, 4)
XT_BANK = {"at0": (0, 0, 0), "moe": (0, 1, 2), "at1": (0, 1, 3)}
QKV_BANK = [(3, 7, 2, 6, 2), (6, 7, 0, 1, 2)]
YT_BANK = [(0, 1, 2), (4, 5, 4)]
AO_BANK = [(7, 6, 2), (6, 7, 5)]


def vit_tower(nc, xk, cw, cst, sel_in, fcols, frows, tokw, at0w, at0p, router, moe_gu, moe_d,
              at1w, at1p, ffg, ffu, ffd, out):
    with ExitStack() as ctx:
        def sb(name, shape, dt=F32):
            return ctx.enter_context(nc.sbuf_tensor(name, shape, dt))

        def sem(name):
            return ctx.enter_context(nc.semaphore(name))

        def bc(ap, axis, n):
            shape = list(ap.shape)
            shape.insert(axis, n)
            return ap.unsqueeze(axis).broadcast_to(shape)

        bank = [ctx.enter_context(nc.psum_tensor(f"bank{i}", [P, 512], F32)) for i in range(8)]

        cst_sb = sb("cst_sb", [P, C_END])
        ident = cst_sb[:, C_ID:C_ID + P]
        fold = cst_sb[:, C_FOLD:C_FOLD + NB]
        sel = sb("sel", [3 * E, E, P], BF16)
        identb = sb("identb", [P, P], BF16)
        ones = sb("ones", [P, P])
        cw_sb = sb("cw_sb", [CP, CK, C])
        tw = sb("tw", [P, KC, W_END])
        fc = sb("fc", [P, 8, KC])
        fr = sb("fr", [P, 4, C])
        at0w_sb = sb("at0w_sb", [P, KC, 2, 3 * P])
        at0p_sb = sb("at0p_sb", [P, KC, C])
        at0w_flat = at0w_sb[:, :, :, :].rearrange("p c a n -> p (c a n)")
        at0p_flat = at0p_sb[:, :, :].rearrange("p c n -> p (c n)")
        router_sb = sb("router_sb", [P, KC, E])
        gu_sb = sb("gu_sb", [P, NM, 2, KC, P])

        x_sb = sb("x_sb", [P, CK, NT * P])
        pe = sb("pe", [P, NT, C])
        lnT = sb("lnT", [P, NPATCH, KC, P])
        red = sb("red", [P, 2, C])
        xh = sb("xh", [P, 3, C])
        qlnT = sb("qlnT", [P, KC, P])
        q_sb = sb("q_sb", [P, 2, C])
        kvb = sb("kvb", [P, 6 + NPATCH, C])
        hm = sb("hm", [P, 2, INNER])
        act_m = sb("act_m", [P, 2, NAB + P])
        hqT = sb("hqT", [P, NI, P], BF16)
        prod = sb("prod", [P, NPATCH + 1, C])
        sc = sb("sc", [P, NPATCH, LH])
        msum = sb("msum", [P, 2, LH])
        agg = sb("agg", [P, C])
        aggT = sb("aggT", [P, KC, P])
        lo = sb("lo", [P, 2, C])
        loT = sb("loT", [P, KC, P])
        lnloT = sb("lnloT", [P, KC, 2, P])
        clsT = sb("clsT", [P, KC, P])
        gq = sb("gq", [P, C])
        gprod = sb("gprod", [P, KC, C])
        G = sb("G", [P, KC, LH])
        gsc = sb("gsc", [LH, 4, NB])
        gsm = sb("gsm", [LH, 3, NB])
        gpt = sb("gpt", [P, 2, LH])
        pgv = sb("pgv", [P, 2, C])
        gfold = sb("gfold", [P, KC, NB])
        clsb = sb("clsb", [NB, C])

        def views(whole, *shapes):
            at, got = 0, []
            for shape in shapes:
                dt = F32
                if shape[-1] is BF16:
                    shape, dt = shape[:-1], BF16
                n = int(np.prod(shape)) // (2 if dt is BF16 else 1)
                part = whole[:, at:at + n]
                if dt is BF16:
                    part = part.bitcast(BF16)
                names = "abcd"[:len(shape)]
                dims = dict(zip(names[1:], shape[1:]))
                got.append(part.rearrange(f"p ({' '.join(names)}) -> p {' '.join(names)}", **dims))
                at += n
            assert at <= whole.shape[1]
            return got

        ffw_sb, at1w_sb, at1p_sb, dn_sb = views(
            x_sb[:, :, :].rearrange("p c n -> p (c n)"), (3, 2 * INNER), (KC, 2, 3 * P), (KC, C), (NM, C))
        qkv, aprod, y, yT = views(kvb[:, :, :].rearrange("p i n -> p (i n)"), (T, 3 * P), (T, P), (T, P), (KC, NTOK))
        th, act_a = views(lnT[:, :, :, :].rearrange("p i c n -> p (i c n)"), (2, 512), (2, 512))
        ffq_sb, xn, xT = views(pe[:, :, :].rearrange("p i n -> p (i n)"), (3, 2 * INNER, BF16), (3, C), (KC, NTOK))
        xqT, rot = views(prod[:, :, :].rearrange("p t n -> p (t n)"), (KC, NTOK, BF16), (2, 2 * HH, HD))
        gateq = ffq_sb[:, 0, :].rearrange("p (c n) -> p c n", c=KC)
        upq = ffq_sb[:, 1, :].rearrange("p (c n) -> p c n", c=KC)
        downq = ffq_sb[:, 2, :].rearrange("p (c n) -> p c n", c=NI)

        h = sb("h", [P, 3, C])
        S = sb("S", [P, T, HH, T])
        S1 = sb("S1", [P, T, HH])
        lg = sb("lg", [P, 3, E])
        rt = sb("rt", [P, 5, 3, E])
        rs = sb("rs", [P, 3, 3])
        c3 = sb("c3", [P, 2, 3, E], BF16)
        c3T = sb("c3T", [3 * E, NAB], BF16)
        cc = sb("cc", [P, E // 2])
        junk = sb("junk", [P, 2 * INNER], BF16)
        wsum = sb("wsum", [P, 5])
        wsc = sb("wsc", [P, 5])
        winv = sb("winv", [P, 5])
        wf = sb("wf", [P, 2])
        fx = sb("fx", [P, 8, 3])
        hmx = sb("hmx", [P, 3])
        stats = sb("stats", [P, NLN, 6])
        mv = sb("mv", [P, NLN, 2])
        veps = sb("veps", [P, NLN])
        rstd = sb("rstd", [P, NLN])
        nhalf = sb("nhalf", [P, 1])
        magic = sb("magic", [P, 2])

        ld_cst, ld_sel, ld_fc, ld_fr = (sem(n) for n in ("ld_cst", "ld_sel", "ld_fc", "ld_fr"))
        ld_x = [sem(f"ld_x{i}") for i in range(7)]
        ld_cw = [sem(f"ld_cw{i}") for i in range(2)]
        ld_tq, ld_tkv, ld_tp, ld_tg = (sem(n) for n in ("ld_tq", "ld_tkv", "ld_tp", "ld_tg"))
        ld_at0, ld_rt, ld_at1 = sem("ld_at0"), sem("ld_rt"), sem("ld_at1")
        ld_gu = [sem(f"ld_gu{i}") for i in range(3)]
        ld_dn = sem("ld_dn")
        ld_ff = sem("ld_ff")
        chain = sem("chain")
        pchain = sem("pchain")
        var_ready, rstd_ready = sem("var_ready"), sem("rstd_ready")
        consts_ready = sem("consts_ready")
        xh_ready = sem("xh_ready")
        norm_ready = sem("norm_ready")
        red_added = sem("red_added")
        pe_step = {k: sem("pe_" + k) for k in
                   ("conv", "T", "kv", "K", "V", "clsT", "gq", "qT", "q", "aggT", "proj", "loT", "mod",
                    "lnloT", "gv", "gs", "pT", "fold", "cls", "sumA")}
        ev = {k: sem("ev_" + k) for k in
              ("conv", "T", "kv", "clsT", "gq", "qT", "q", "aggT", "proj", "loT", "mod", "lnloT",
               "gs", "pgv", "pT", "fold", "cls", "sumA")}
        local_exp, local_arg = sem("local_exp"), sem("local_arg")
        scored = sem("scored")
        agg_ready = sem("agg_ready")
        g_ready = sem("g_ready")
        gexp, garg = sem("gexp"), sem("garg")
        gp_ready = sem("gp_ready")
        abs_done = sem("abs_done")
        intA = sem("intA")
        scaledB, intB = sem("scaledB"), sem("intB")
        xn_ready = sem("xn_ready")
        xnT_done, xT_ready = sem("xnT_done"), sem("xT_ready")
        qkv_done, qkv_ready = sem("qkv_done"), sem("qkv_ready")
        at_arg, at_exp = sem("at_arg"), sem("at_exp")
        rot_ready, rot_used = sem("rot_ready"), sem("rot_used")
        probs_ready = sem("probs_ready")
        y_ready, yT_done, yT_ready, ao_done = sem("y_ready"), sem("yT_done"), sem("yT_ready"), sem("ao_done")
        h_ready = sem("h_ready")
        rt_done, rt_arg, rt_exp, c3_ready, c3T_done, c3T_ready = (
            sem(n) for n in ("rt_done", "rt_arg", "rt_exp", "c3_ready", "c3T_done", "c3T_ready"))
        coef_done = sem("coef_done")
        acc_done = sem("acc_done")
        gu_done, th_ready, gu_used, act_ready, dn_done = (
            sem(n) for n in ("gu_done", "th_ready", "gu_used", "act_ready", "dn_done"))
        cgu_done, cth_ready, chid_ready, chT_done, cact_ready, cdn_done, cc_ready = (
            sem(n) for n in ("cgu_done", "cth_ready", "chid_ready", "chT_done", "cact_ready", "cdn_done", "cc_ready"))
        scB_ready = sem("scB_ready")
        xq_ready, xqT_done, xqT_ready = sem("xq_ready"), sem("xqT_done"), sem("xqT_ready")
        hs_ready, last_hs_ready = sem("hs_ready"), sem("last_hs_ready")
        fg_done, fth_ready, fg_used = sem("fg_done"), sem("fth_ready"), sem("fg_used")
        hq_ready, hqT_done, hqT_ready, fd_done = sem("hq_ready"), sem("hqT_done"), sem("hqT_ready"), sem("fd_done")
        tscale_ready = sem("tscale_ready")
        stored = sem("stored")

        STEPS = tokenizer_steps()
        block = ctx.enter_context(nc.Block())

        @block.sync
        def _(sp):
            xmain = xk.rearrange("(c p) n -> p c n", p=CP)
            cmain = cw.rearrange("(c p) n -> p c n", p=CP)

            def load_x(g):
                cols = slice(X_LOADS[g] * P, X_LOADS[g + 1] * P)
                sp.dma_start(x_sb[0:CP, :, cols], xmain[:, :, cols]).then_inc(ld_x[g], 16)

            load_x(0)
            sp.dma_start(cw_sb[:, 0:2, :], cmain[:, 0:2, :]).then_inc(ld_cw[0], 16)
            sp.dma_start(cw_sb[:, 2:CK, :], cmain[:, 2:CK, :]).then_inc(ld_cw[1], 16)
            load_x(1)
            load_x(2)
            sp.dma_start(fc[:, :, :], fcols).then_inc(ld_fc, 16)
            sp.dma_start(cst_sb[:, :], cst).then_inc(ld_cst, 16)
            load_x(3)
            sp.dma_start(tw[:, :, W_Q:W_KV], tokw[:, :, W_Q:W_KV]).then_inc(ld_tq, 16)
            sp.dma_start(tw[:, :, W_KV:W_P], tokw[:, :, W_KV:W_P]).then_inc(ld_tkv, 16)
            load_x(4)
            sp.dma_start(at0w_sb[:, :, :, :], at0w).then_inc(ld_at0, 16)
            sp.dma_start(at0p_sb[:, :, :], at0p).then_inc(ld_at0, 16)
            load_x(5)
            sp.dma_start(fr[:, :, :], bc(frows, 0, P)).then_inc(ld_fr, 16)
            load_x(6)
            sp.dma_start(tw[:, :, W_GQ:W_END], tokw[:, :, W_GQ:W_END]).then_inc(ld_tg, 16)
            sp.dma_start(tw[:, :, W_P:W_GQ], tokw[:, :, W_P:W_GQ]).then_inc(ld_tp, 16)
            sp.dma_start(router_sb[:, :, :], router).then_inc(ld_rt, 16)
            sp.dma_start(sel[:, :, :], sel_in).then_inc(ld_sel, 16)
            sp.dma_start(gu_sb[:, 8:10], moe_gu[:, 8:10]).then_inc(ld_gu[0], 16)
            sp.dma_start(gu_sb[:, 0:4], moe_gu[:, 0:4]).then_inc(ld_gu[1], 16)
            sp.dma_start(gu_sb[:, 4:8], moe_gu[:, 4:8]).then_inc(ld_gu[2], 16)
            sp.wait_ge(pe_step["conv"], NT)
            sp.dma_start(dn_sb[:, :, :], moe_d).then_inc(ld_dn, 16)
            for i, w in enumerate((ffg, ffu, ffd)):
                sp.dma_start(ffw_sb[:, i, :], w).then_inc(ld_ff, 16)
            sp.dma_start(at1w_sb[:, :, :, :], at1w).then_inc(ld_at1, 16)
            sp.dma_start(at1p_sb[:, :, :], at1p).then_inc(ld_at1, 16)
            for s in (0, 2, 1, 3, 4):
                j, half = BLK[s] // 2, BLK[s] % 2
                sp.wait_ge(h_ready, 9 + j + 1)
                sp.dma_start(out[:, s, :], h[half * NB:(half + 1) * NB, j, :]).then_inc(stored, 16)
            sp.wait_ge(stored, 16 * T)

        @block.tensor
        def _(te):
            def mm(o, l, r, c, n):
                return te.matmul(o, l, r, start=(c == 0), stop=(c == n - 1))

            def keep_warm(b, n):
                for _ in range(n):
                    te.matmul(bank[b][:, 0:P], ones[:, :], ones[:, :], start=True, stop=True)

            def turn(o, src, np_):
                for c in range(KC):
                    last = te.transpose(o[:, c, 0:np_], src[0:np_, c * P:(c + 1) * P], ident[0:np_, 0:np_])
                return last

            def chunks(b, n=P):
                return bank[b][:, 0:KC * P].rearrange("p (c n) -> p c n", c=KC)

            def conv(i):
                if i in X_LOADS:
                    te.wait_ge(ld_x[X_LOADS.index(i)], 16)
                if i >= 2:
                    te.wait_ge(ev["conv"], i - 1)
                cols = slice(i * P, (i + 1) * P)
                for c in range(CK):
                    if i == 0 and c in (0, 2):
                        te.wait_ge(ld_cw[c // 2], 16)
                    last = mm(bank[i % 2][:, 0:C], x_sb[0:CP, c, cols], cw_sb[:, c, :], c, CK)
                last.then_inc(pe_step["conv"], 1)

            def tile_T(i):
                te.wait_ge(norm_ready, i + 1)
                if i >= 2:
                    te.wait_ge(ev["T"], i - 1)
                if i == 0:
                    te.wait_ge(ld_cst, 16)
                turn(chunks(2 + i % 2), pe[:, i, :], P).then_inc(pe_step["T"], 1)

            def key_value(u, i, c0, c1):
                if u == 0:
                    te.wait_ge(ld_tkv, 16)
                te.wait_ge(ev["T"], i + 1)
                if u >= 2:
                    te.wait_ge(ev["kv"], u - 1)
                for c in range(KC):
                    last = mm(bank[4 + u % 2][:, 0:c1 - c0], lnT[:, i % NPATCH, c, :], tw[:, c, W_KV + c0:W_KV + c1], c, KC)
                return last

            def tile_kv(i):
                key_value(i, i, 0, 2 * C).then_inc(pe_step["kv"], 1)

            def tile_k(i):
                key_value(i, i, 0, C).then_inc(pe_step["K"], 1)

            def tile_v(i):
                key_value(i + NPATCH, i, C, 2 * C).then_inc(pe_step["V"], 1)

            def cls_T(_):
                te.wait_ge(ld_cst, 16)
                te.wait_ge(xh_ready, 2)
                te.wait_ge(ev["qT"], 1)
                turn(chunks(6), xh[:, 2, :], P).then_inc(pe_step["clsT"], 1)

            def cls_q(_):
                te.wait_ge(ld_tg, 16)
                te.wait_ge(ev["clsT"], 1)
                te.wait_ge(ev["q"], 1)
                for c in range(KC):
                    last = mm(bank[7][:, 0:C], clsT[:, c, :], tw[:, c, W_GQ:W_GKV], c, KC)
                last.then_inc(pe_step["gq"], 1)

            def q_T(w):
                te.wait_ge(xh_ready, 1 + 2 * w)
                if w:
                    te.wait_ge(ev["aggT"], 1)
                turn(chunks(6), xh[:, w, :], P).then_inc(pe_step["qT"], 1)

            def q_mm(w):
                if w == 0:
                    te.wait_ge(ld_tq, 16)
                te.wait_ge(ev["proj"] if w else ev["sumA"], 1)
                te.wait_ge(ev["qT"], w + 1)
                for c in range(KC):
                    last = mm(bank[7][:, 0:C], qlnT[:, c, :], tw[:, c, W_Q:W_KV], c, KC)
                last.then_inc(pe_step["q"], 1)

            def sum_a(_):
                te.wait_ge(abs_done, 2)
                te.wait_ge(consts_ready, 5)
                mm(bank[7][:, 0:2], ones[:, :], wsum[:, 0:2], 0, 1).then_inc(pe_step["sumA"], 1)

            def agg_T(w):
                te.wait_ge(agg_ready, w + 1)
                te.wait_ge(ev["lnloT"] if w else ev["clsT"], 1)
                turn(chunks(6), agg[:, :], P).then_inc(pe_step["aggT"], 1)

            def proj(w):
                if w == 0:
                    te.wait_ge(ld_tp, 16)
                te.wait_ge(ev["mod"] if w else ev["gq"], 1)
                te.wait_ge(ev["aggT"], w + 1)
                for c in range(KC):
                    last = mm(bank[7][:, 0:C], aggT[:, c, :], tw[:, c, W_P:W_M], c, KC)
                last.then_inc(pe_step["proj"], 1)

            def lo_T(w):
                te.wait_ge(ev["proj"], w + 1)
                te.wait_ge(ev["aggT"] if w else ev["qT"], 2)
                turn(chunks(6), lo[:, w, :], P).then_inc(pe_step["loT"], 1)

            def mod(w):
                te.wait_ge(ev["loT"], w + 1)
                te.wait_ge(ev["proj"] if w else ev["q"], 2)
                for c in range(KC):
                    last = mm(bank[7][:, 0:C], loT[:, c, :], tw[:, c, W_M:W_GQ], c, KC)
                last.then_inc(pe_step["mod"], 1)

            def lnlo_T(w):
                te.wait_ge(xh_ready, 4 + w)
                te.wait_ge(ev["loT"], w + 1)
                turn(chunks(6), xh[:, w, :], P).then_inc(pe_step["lnloT"], 1)

            def g_scores(_):
                te.wait_ge(g_ready, 1)
                te.wait_ge(ev["lnloT"], 2)
                te.wait_ge(ev["conv"], NT)
                for c in range(KC):
                    last = mm(bank[1][0:LH, 0:2 * P], G[:, c, :], lnloT[:, c, :, :], c, KC)
                last.then_inc(pe_step["gs"], 1)

            def g_v(_):
                te.wait_ge(ev["kv"], 3 * NPATCH)
                for w in range(2):
                    for c in range(KC):
                        last = mm(bank[4][:, w * C:(w + 1) * C], lnloT[:, c, w, :],
                                  tw[:, c, W_GKV + C:W_GP], c, KC)
                last.then_inc(pe_step["gv"], 1)

            def p_T(_):
                te.wait_ge(gp_ready, 1)
                te.wait_ge(qkv_ready, 1)
                gs = gsc[:, :, :].rearrange("h (w a) b -> h w (a b)", w=2)
                for w in range(2):
                    last = te.transpose(bank[3][:, w * LH:(w + 1) * LH], gs[:, w, :], ident[0:LH, 0:LH])
                last.then_inc(pe_step["pT"], 1)

            def fold_halves(_):
                te.wait_ge(ev["pgv"], 1)
                for c in range(KC):
                    for w in range(2):
                        last = mm(bank[5][:, c * NB:(c + 1) * NB], pgv[:, w, c * P:(c + 1) * P], fold, w, 2)
                last.then_inc(pe_step["fold"], 1)

            def cls_out(_):
                te.wait_ge(ev["fold"], 1)
                for c in range(KC):
                    last = mm(bank[5][0:NB, C:2 * C], gfold[:, c, :], tw[:, c, W_GP:W_END], c, KC)
                last.then_inc(pe_step["cls"], 1)

            def tokens_T(n, j):
                te.wait_ge(xn_ready, XN[n, j] + 1)
                turn(chunks(XT_BANK[n][j]), xn[:, j, :], ROWS[j]).then_inc(xnT_done, 1)

            def token_qkv(layer, s, w):
                te.wait_ge(xT_ready, XN[("at0", "at1")[layer], BLK[s] // 2] + 1)
                rows = slice(BLK[s] * NB, (BLK[s] + 1) * NB)
                for hh in range(2):
                    for c in range(KC):
                        last = mm(bank[QKV_BANK[layer][s]][hh * NB:(hh + 1) * NB, 0:3 * P], xT[:, c, rows],
                                  w[:, c, hh, :], c, KC)
                last.then_inc(qkv_done, 1)

            def first_T(j):
                if j == 0:
                    te.wait_ge(ev["conv"], NT)
                else:
                    te.wait_ge(xT_ready, 1 if j == 1 else XN["moe", 0] + 1)
                tokens_T("at0", j)

            def first_qkv(s):
                if s == 0:
                    te.wait_ge(intA, 2)
                    te.wait_ge(ev["T"], NT)
                if s == 1:
                    te.wait_ge(ev["mod"], 2)
                if s == 3:
                    te.wait_ge(ev["lnloT"], 2)
                if s == 4:
                    te.wait_ge(qkv_ready, 2)
                token_qkv(0, s, at0w_sb)

            def y_T(layer, g):
                ts = (2 * g, 2 * g + 1)[0:1 if g == 2 else 2]
                te.wait_ge(y_ready, T * layer + ts[-1] + 1)
                if g == 2:
                    te.wait_ge(yT_ready, 3 * layer + 1)
                for i, t in enumerate(ts):
                    last = te.transpose(bank[YT_BANK[layer][g]][:, i * P:(i + 1) * P], y[:, t, :], ident)
                last.then_inc(yT_done, 1)

            def project(layer, j, wp):
                te.wait_ge(yT_ready, 3 * layer + (2 if j < 2 else 3))
                for c in range(KC):
                    last = mm(bank[AO_BANK[layer][j]][0:ROWS[j], 0:C], yT[:, c, j * P:j * P + ROWS[j]],
                              wp[:, c, :], c, KC)
                last.then_inc(ao_done, 1)

            run = {"conv": conv, "T": tile_T, "kv": tile_kv, "K": tile_k, "V": tile_v, "clsT": cls_T, "gq": cls_q,
                   "qT": q_T, "q": q_mm, "sumA": sum_a, "aggT": agg_T, "proj": proj, "loT": lo_T, "mod": mod,
                   "lnloT": lnlo_T, "gs": g_scores, "gv": g_v, "pT": p_T, "fold": fold_halves, "cls": cls_out,
                   "xT": first_T, "qkv": first_qkv, "yT": lambda g: y_T(0, g), "ao": lambda j: project(0, j, at0p_sb)}
            te.wait_ge(consts_ready, 5)
            keep_warm(2, 8)
            for kind, i in STEPS:
                if kind in run:
                    run[kind](i)
                if kind == "gv":
                    keep_warm(0, 8)
                    te.wait_ge(at_exp, 1)
                    keep_warm(0, 11)
                if kind == "yT":
                    keep_warm(2, 9 if i == 0 else 2)

            def route_logits(part):
                if part == 0:
                    te.wait_ge(ld_rt, 16)
                    for j in range(2):
                        for c in range(KC):
                            last = mm(bank[3][:, j * E:(j + 1) * E], xT[:, c, j * P:(j + 1) * P], router_sb[:, c, :], c, KC)
                else:
                    te.wait_ge(xT_ready, XN["moe", 2] + 1)
                    for e in range(2):
                        for c in range(KC):
                            last = mm(bank[2][e * NB:(e + 1) * NB, 0:E], xT[:, c, NAB:NTOK], router_sb[:, c, :], c, KC)
                last.then_inc(rt_done, 1)

            def coef_T():
                te.wait_ge(c3_ready, 1)
                bankb = bank[3][0:3 * E, 0:P].bitcast(BF16)
                for j in range(2):
                    last = te.transpose(bankb[:, j * P:(j + 1) * P], c3[:, j, :, :].rearrange("p a e -> p (a e)"), identb[:, :])
                last.then_inc(c3T_done, 1)

            def gate_up(i):
                m = MOE_ORDER[i]
                if i == 0:
                    te.wait_ge(ld_gu[0], 16)
                    te.wait_ge(xT_ready, XN["moe", 1] + 1)
                if i == 1:
                    te.wait_ge(ev["cls"], 1)
                if i == 2:
                    te.wait_ge(ld_gu[1], 16)
                if i == 6:
                    te.wait_ge(ld_gu[2], 16)
                if i < 2:
                    te.wait_ge(h_ready, 2)
                else:
                    te.wait_ge(gu_used, i - 1)
                for gu in range(2):
                    for c in range(KC):
                        last = mm(bank[4 + 2 * gu + i % 2][:, 0:NAB], gu_sb[:, m, gu, c, :], xT[:, c, 0:NAB], c, KC)
                last.then_inc(gu_done, 1)

            def coef_rows(i):
                m = MOE_ORDER[i]
                if i == 2:
                    te.wait_ge(c3T_ready, 1)
                else:
                    te.wait_ge(act_ready, i)
                last = mm(bank[3][:, 0:NAB], sel[:, m, :], c3T[:, 0:NAB], 0, 1)
                if i == 2:
                    te.wait_ge(abs_done, 5)
                    last = mm(bank[3][:, 384:387], ones[:, :], wsum[:, 2:5], 0, 1)
                last.then_inc(coef_done, 1)

            def down(i):
                m = MOE_ORDER[i]
                if i == 0:
                    te.wait_ge(ld_dn, 16)
                te.wait_ge(act_ready, i + 1)
                for j in range(2):
                    last = mm(bank[j][:, 0:C], act_m[:, i % 2, j * P:(j + 1) * P], dn_sb[:, m, :], i, NM)
                    if i == NM - 1:
                        last.then_inc(acc_done, 1)
                if i < NM - 1:
                    last.then_inc(dn_done, 1)

            def class_gate_up(q):
                te.wait_ge(gu_used, NM - 1 + q) if q < 2 else te.wait_ge(cact_ready, q - 1)
                for e in range(2):
                    for c in range(KC):
                        last = mm(bank[4 + q % 2][e * NB:(e + 1) * NB, 0:2 * P], xT[:, c, NAB:NTOK],
                                  gu_sb[:, MOE_ORDER[2 * q + e], :, c, :], c, KC)
                last.then_inc(cgu_done, 1)

            def class_T(q):
                te.wait_ge(chid_ready, q + 1)
                te.transpose(bank[4 + q % 2][:, 2 * P:3 * P], act_a[:, q % 2, NAB:NAB + P], ident).then_inc(chT_done, 1)

            def class_down(q):
                te.wait_ge(cact_ready, q + 1)
                for e in range(2):
                    i = 2 * q + e
                    last = mm(bank[2][0:NB, 0:C], act_m[:, q % 2, NAB + e * NB:NAB + (e + 1) * NB],
                              dn_sb[:, MOE_ORDER[i], :], i, NM)
                last.then_inc(acc_done if q == NM // 2 - 1 else cdn_done, 1)

            tokens_T("moe", 0)
            tokens_T("moe", 1)
            gate_up(0)
            route_logits(0)
            first_T(2)
            gate_up(1)
            first_qkv(4)
            gate_up(2)
            down(0)
            gate_up(3)
            down(1)
            te.wait_ge(ld_sel, 16)
            te.wait_ge(consts_ready, 5)
            coef_T()
            coef_rows(2)
            for i in range(4, NM):
                gate_up(i)
                if i == 6:
                    project(0, 2, at0p_sb)
                if i == 8:
                    route_logits(1)
                coef_rows(i - 1)
                down(i - 2)
                if i == 5:
                    y_T(0, 2)
                if i == 7:
                    tokens_T("moe", 2)
            class_gate_up(0)
            coef_rows(NM - 1)
            down(NM - 2)
            class_gate_up(1)
            down(NM - 1)
            class_T(0)
            class_T(1)
            class_down(0)
            class_gate_up(2)
            class_down(1)
            class_gate_up(3)
            te.wait_ge(ld_at1, 32)
            te.wait_ge(h_ready, 4)
            tokens_T("at1", 0)
            class_T(2)
            te.wait_ge(h_ready, 5)
            tokens_T("at1", 1)
            class_T(3)
            token_qkv(1, 0, at1w_sb)
            token_qkv(1, 1, at1w_sb)
            class_down(2)
            class_gate_up(4)
            class_down(3)
            token_qkv(1, 2, at1w_sb)
            class_T(4)
            token_qkv(1, 3, at1w_sb)
            class_down(4)
            keep_warm(3, 18)
            te.wait_ge(at_arg, 3)
            keep_warm(3, 2)
            tokens_T("at1", 2)
            token_qkv(1, 4, at1w_sb)
            keep_warm(3, 3)
            y_T(1, 0)
            keep_warm(3, 4)
            y_T(1, 1)
            project(1, 0, at1p_sb)
            project(1, 1, at1p_sb)
            keep_warm(3, 6)
            te.wait_ge(h_ready, 8)
            keep_warm(3, 10)

            def grid_T(j):
                te.wait_ge(xq_ready, j + 1)
                if j == 2:
                    te.wait_ge(xqT_ready, 2)
                turn(chunks(min(6 + j, 7)), xn[:, j, :], ROWS[j]).then_inc(xqT_done, 1)

            def ff_up(k):
                j, half = k // 2, k % 2
                te.wait_ge(xqT_ready, j + 1)
                if k >= 2:
                    te.wait_ge(fg_used, k - 1)
                for gu, wq in enumerate((gateq, upq)):
                    for c in range(KC):
                        last = mm(bank[2 * gu + k % 2][0:ROWS[j], :], xqT[:, c, j * P:j * P + ROWS[j]],
                                  wq[:, c, half * 512:(half + 1) * 512], c, KC)
                last.then_inc(fg_done, 1)

            def ff_down(j):
                r = ROWS[j]
                for half in range(2):
                    if j < 2:
                        te.wait_ge(hs_ready, 2 * j + half + 1)
                    else:
                        te.wait_ge(last_hs_ready, half + 1)
                    if j == 0 and half:
                        te.wait_ge(h_ready, 9)
                    if j:
                        te.wait_ge(hqT_ready, 2 * j - 1 + half)
                    for c in range(NI // 2):
                        k = half * NI // 2 + c
                        last = te.transpose(bank[4 + half][:, c * P:c * P + r], hm[0:r, j % 2, k * P:(k + 1) * P],
                                            ident[0:r, 0:r])
                    last.then_inc(hqT_done, 1)
                if j == 1:
                    te.wait_ge(xqT_ready, 3)
                if j == 2:
                    te.wait_ge(h_ready, 10)
                for c in range(NI):
                    if c % (NI // 2) == 0:
                        te.wait_ge(hqT_ready, 2 * j + 1 + c // (NI // 2))
                    last = mm(bank[6 + j % 2][0:r, 0:C], hqT[:, c, 0:r], downq[:, c, :], c, NI)
                last.then_inc(fd_done, 1)

            te.wait_ge(intB, 6)
            grid_T(0)
            ff_up(0)
            ff_up(1)
            grid_T(1)
            y_T(1, 2)
            project(1, 2, at1p_sb)
            ff_up(2)
            ff_up(3)
            ff_down(0)
            grid_T(2)
            ff_up(4)
            ff_up(5)
            ff_down(1)
            ff_down(2)

        @block.scalar
        def _(ac):
            def copy(o, i):
                return ac.activation(o, i, ACT.Copy)

            def chunks(b):
                return bank[b][:, 0:KC * P].rearrange("p (c n) -> p c n", c=KC)

            def affine(o, b, g):
                for c in range(KC):
                    last = ac.activation(o(c), chunks(b)[:, c, :], ACT.Identity,
                                         bias=fc[:, g + 1, c:c + 1], scale=fc[:, g, c:c + 1])
                return last

            def conv(i):
                ac.wait_ge(pe_step["conv"], i + 1)
                copy(pe[:, i, :], bank[i % 2][:, 0:C]).then_inc(ev["conv"], 1)

            def tile_T(i):
                ac.wait_ge(pe_step["T"], i + 1)
                if i == 0:
                    ac.wait_ge(ld_fc, 16)
                if i >= NPATCH:
                    ac.wait_ge(pe_step["kv"], i - NPATCH + 1)
                affine(lambda c: lnT[:, i % NPATCH, c, :], 2 + i % 2, G_LKV).then_inc(ev["T"], 1)

            def tile_kv(i):
                ac.wait_ge(pe_step["kv"], i + 1)
                if i >= 6:
                    ac.wait_ge(scored, i // 3 - 1)
                k, v = i % 6, 6 + i
                copy(kvb[:, k:v + 1:v - k, :], bank[4 + i % 2][:, :].rearrange("p (a n) -> p a n", a=2)
                     ).then_inc(ev["kv"], 1)

            def tile_k(i):
                ac.wait_ge(pe_step["K"], i - NPATCH + 1)
                ac.wait_ge(scored, i // 3 - 1)
                copy(kvb[:, i % 6, :], bank[4 + i % 2][:, 0:C]).then_inc(ev["kv"], 1)

            def tile_v(i):
                ac.wait_ge(pe_step["V"], i - NPATCH + 1)
                ac.wait_ge(agg_ready, 1)
                copy(kvb[:, 6 + i - NPATCH, :], bank[4 + (i + NPATCH) % 2][:, 0:C]).then_inc(ev["kv"], 1)

            def cls_T(_):
                ac.wait_ge(pe_step["clsT"], 1)
                affine(lambda c: clsT[:, c, :], 6, G_GQ).then_inc(ev["clsT"], 1)

            def cls_q(_):
                ac.wait_ge(pe_step["gq"], 1)
                copy(gq[:, :], bank[7][:, 0:C]).then_inc(ev["gq"], 1)

            def q_T(w):
                if w == 0:
                    ac.wait_ge(ld_fc, 16)
                ac.wait_ge(pe_step["qT"], w + 1)
                if w:
                    ac.wait_ge(pe_step["q"], w)
                affine(lambda c: qlnT[:, c, :], 6, G_LQ).then_inc(ev["qT"], 1)

            def q_mm(w):
                ac.wait_ge(pe_step["q"], w + 1)
                ac.activation(q_sb[:, w, :], bank[7][:, 0:C], ACT.Copy, scale=float(C) ** -0.5).then_inc(ev["q"], 1)

            def exp_local(w):
                ac.wait_ge(local_arg, w + 1)
                ac.activation(sc[:, :, :], sc[:, :, :], ACT.Exp).then_inc(local_exp, 1)

            def agg_T(w):
                ac.wait_ge(pe_step["aggT"], w + 1)
                copy(aggT[:, :, :], chunks(6)).then_inc(ev["aggT"], 1)

            def lo_T(w):
                ac.wait_ge(pe_step["loT"], w + 1)
                copy(loT[:, :, :], chunks(6)).then_inc(ev["loT"], 1)

            def lnlo_T(w):
                ac.wait_ge(pe_step["lnloT"], w + 1)
                affine(lambda c: lnloT[:, c, w, :], 6, G_GKV).then_inc(ev["lnloT"], 1)

            def abs_sums(lots, first):
                for n, (i, src) in enumerate(lots):
                    if first + n:
                        ac.wait_ge(abs_done, first + n)
                    ac.activation(junk[:, 0:src.shape[1]], src, ACT.Abs, accum_out=wsum[:, i:i + 1]).then_inc(abs_done, 1)

            def abs_b(k):
                ac.wait_ge(ld_ff, 48)
                abs_sums([(2 + k, ffw_sb[:, k, :])], 2 + k)

            def abs_a(_):
                ac.wait_ge(ld_at0, 32)
                abs_sums([(0, at0w_flat), (1, at0p_flat)], 0)

            def exp_global(_):
                ac.wait_ge(garg, 1)
                ac.activation(gsc[:, :, :], gsc[:, :, :], ACT.Exp, scale=float(C) ** -0.5).then_inc(gexp, 1)

            def fold_halves(_):
                ac.wait_ge(pe_step["fold"], 1)
                copy(gfold[:, :, :], bank[5][:, 0:KC * NB].rearrange("p (c n) -> p c n", c=KC)).then_inc(ev["fold"], 1)

            def tokens_T(n, j):
                ac.wait_ge(xnT_done, XN[n, j] + 1)
                r = ROWS[j]
                copy(xT[:, :, j * P:j * P + r], chunks(XT_BANK[n][j])[:, :, 0:r]).then_inc(xT_ready, 1)

            def token_qkv(layer, n, s):
                ac.wait_ge(qkv_done, T * layer + n + 1)
                copy(qkv[:, s, :], bank[QKV_BANK[layer][s]][:, 0:3 * P]).then_inc(qkv_ready, 1)

            def exp_scores(layer, k):
                part = S[:, 0:4, :, :] if k == 0 else S[:, 4, :, :]
                ac.wait_ge(at_arg, 2 * layer + k + 1)
                ac.activation(part, part, ACT.Exp, scale=wf[:, 0:1] if layer == 0 else HD ** -0.5).then_inc(at_exp, 1)

            def y_T(layer, g):
                ac.wait_ge(yT_done, 3 * layer + g + 1)
                if g == 2:
                    o = yT[:, :, 4 * NB:5 * NB]
                    i = bank[YT_BANK[layer][g]][:, 0:P].rearrange("p (a b) -> p a b", a=2)
                else:
                    o = yT[:, :, 0:4 * NB].rearrange("p a (u v b) -> p u v a b", u=2, v=2)[:, :, g, :, :]
                    i = bank[YT_BANK[layer][g]][:, 0:2 * P].rearrange("p (t a b) -> p t a b", t=2, a=2)
                copy(o, i).then_inc(yT_ready, 1)

            run = {"conv": conv, "T": tile_T, "kv": tile_kv, "K": tile_k, "V": tile_v, "clsT": cls_T, "gq": cls_q,
                   "qT": q_T, "q": q_mm, "abs0": abs_a, "absB": abs_b, "aggT": agg_T, "loT": lo_T,
                   "lnloT": lnlo_T, "gexp": exp_global, "exp": exp_local, "fold": fold_halves, "exp4": lambda _: exp_scores(0, 0),
                   "xT": lambda j: tokens_T("at0", j),
                   "yT": lambda g: y_T(0, g),
                   "qkv": lambda s: token_qkv(0, FIRST_QKV.index(s), s)}
            for kind, i in STEPS:
                if kind in run:
                    run[kind](i)

            tokens_T("moe", 0)
            tokens_T("moe", 1)

            def route_exp(part):
                t = ((0, 2), (2, 3))[part]
                ac.wait_ge(rt_arg, part + 1)
                ac.activation(lg[:, t[0]:t[1], :], lg[:, t[0]:t[1], :], ACT.Exp).then_inc(rt_exp, 1)

            def coef_T():
                ac.wait_ge(c3T_done, 1)
                copy(c3T[:, :], bank[3][0:3 * E, 0:P].bitcast(BF16)).then_inc(c3T_ready, 1)

            def gate_tanh(i):
                ac.wait_ge(gu_done, i + 1)
                if i >= 2:
                    ac.wait_ge(gu_used, i - 1)
                ac.activation(th[:, i % 2, 0:NAB], bank[4 + i % 2][:, 0:NAB], ACT.Tanh, scale=0.5).then_inc(th_ready, 1)

            def class_tanh(q):
                ac.wait_ge(cgu_done, q + 1)
                ac.activation(th[:, q % 2, NAB:NAB + P], bank[4 + q % 2][:, 0:P], ACT.Tanh, scale=0.5
                              ).then_inc(cth_ready, 1)

            def class_T(q):
                ac.wait_ge(chT_done, q + 1)
                if q >= 2:
                    ac.wait_ge(cdn_done, q - 1)
                copy(act_m[:, q % 2, NAB:NAB + P], bank[4 + q % 2][:, 2 * P:3 * P]).then_inc(cact_ready, 1)

            gate_tanh(0)
            route_exp(0)
            tokens_T("at0", 2)
            gate_tanh(1)
            token_qkv(0, 4, 4)
            abs_b(2)
            gate_tanh(2)
            gate_tanh(3)
            coef_T()
            exp_scores(0, 1)
            for i in range(4, NM):
                gate_tanh(i)
                if i == 8:
                    route_exp(1)
                if i == 4:
                    ac.wait_ge(scB_ready, 1)
                k, part = (i - 4) // 2, slice((i % 2) * INNER, (i % 2 + 1) * INNER)
                ac.activation(ffw_sb[:, k, part], ffw_sb[:, k, part], ACT.Copy,
                              scale=winv[:, 2 + k:3 + k]).then_inc(scaledB, 1)
                if i == 5:
                    y_T(0, 2)
                if i == 7:
                    tokens_T("moe", 2)
            class_tanh(0)
            class_tanh(1)
            class_T(0)
            class_T(1)
            class_tanh(2)
            class_tanh(3)
            tokens_T("at1", 0)
            class_T(2)
            tokens_T("at1", 1)
            class_T(3)
            token_qkv(1, 0, 0)
            token_qkv(1, 1, 1)
            class_tanh(4)
            token_qkv(1, 2, 2)
            class_T(4)
            token_qkv(1, 3, 3)
            exp_scores(1, 0)
            tokens_T("at1", 2)
            token_qkv(1, 4, 4)
            y_T(1, 0)
            y_T(1, 1)
            exp_scores(1, 1)
            ac.activation(junk[:, 0:1], magic[:, 0:1], ACT.Silu).then_inc(abs_done, 1)

            def grid_T(j):
                ac.wait_ge(xqT_done, j + 1)
                ac.activation(xqT[:, :, j * P:j * P + ROWS[j]], chunks(min(6 + j, 7))[:, :, 0:ROWS[j]], ACT.Identity,
                              bias=magic[:, 1:2]).then_inc(xqT_ready, 1)

            def ff_tanh(k):
                j = k // 2
                ac.wait_ge(fg_done, k + 1)
                ac.wait_ge(tscale_ready, j + 1)
                if k >= 2:
                    ac.wait_ge(fg_used, k - 1)
                r = ROWS[j]
                ac.activation(th[0:r, k % 2, :], bank[k % 2][0:r, :], ACT.Silu,
                              scale=fx[0:r, 3, j:j + 1]).then_inc(fth_ready, 1)

            def ff_grid(j):
                r = ROWS[j]
                ac.wait_ge(hq_ready, j + 1)
                for half in range(2):
                    o = hm[0:r, j % 2, half * 512:(half + 1) * 512]
                    ac.activation(o, o, ACT.Identity, bias=magic[0:r, 0:1], scale=fx[0:r, 6, j:j + 1]).then_inc(hs_ready, 1)

            def ff_T(j):
                r = ROWS[j]
                for half in range(2):
                    ac.wait_ge(hqT_done, 2 * j + half + 1)
                    if j:
                        ac.wait_ge(fd_done, j)
                    ac.activation(hqT[:, half * NI // 2:(half + 1) * NI // 2, 0:r],
                                  bank[4 + half][:, :].rearrange("p (c n) -> p c n", c=NI // 2)[:, :, 0:r],
                                  ACT.Identity, bias=magic[:, 1:2]).then_inc(hqT_ready, 1)

            grid_T(0)
            ff_tanh(0)
            ff_tanh(1)
            grid_T(1)
            y_T(1, 2)
            ff_tanh(2)
            ff_grid(0)
            ff_tanh(3)
            ff_T(0)
            grid_T(2)
            ff_tanh(4)
            ff_tanh(5)
            ff_grid(1)
            ff_T(1)
            ff_T(2)

        @block.gpsimd
        def _(po):
            links = [0]

            def link(ins):
                links[0] += 1
                ins.then_inc(pchain, 1)
                po.wait_ge(pchain, links[0])

            po.memset(nhalf[:, :], -0.5).then_inc(consts_ready, 1)
            po.memset(ones[:, :], 1.0).then_inc(consts_ready, 1)
            po.memset(magic[:, 0:1], MAGIC).then_inc(consts_ready, 1)
            po.memset(magic[:, 1:2], -MAGIC).then_inc(consts_ready, 1)
            po.memset(S[:, :, :, :], NEG).then_inc(consts_ready, 1)
            po.wait_ge(consts_ready, 5)

            def root(key):
                r = ROWS[key[1]] if key[0] in ("at0", "moe", "at1", "ffn") else P
                i = LN[key]
                po.wait_ge(var_ready, i + 1)
                link(po.tensor_scalar(veps[0:r, i:i + 1], mv[0:r, i, 1:2], EPS, None, ALU.add))
                po.tensor_tensor(rstd[0:r, i:i + 1], veps[0:r, i:i + 1], nhalf[0:r, :], ALU.pow).then_inc(rstd_ready, 1)

            def add_patch(i):
                w, t = i // NPATCH, i % NPATCH
                if t == 0:
                    return
                po.wait_ge(ev["conv"], i + 1)
                if t > 1:
                    po.wait_ge(red_added, 8 * w + t - 1)
                po.tensor_tensor(red[:, w, :], pe[:, i, :], pe[:, i - 1, :] if t == 1 else red[:, w, :],
                                 ALU.add).then_inc(red_added, 1)

            def class_values(layer):
                po.wait_ge(probs_ready, layer + 1)
                v = qkv[:, :, 2 * P:3 * P].rearrange("p s (h d) -> p s h d", d=HD)
                pr = bc(S[:, T - 1, :, :].rearrange("p h s -> p s h"), 3, HD)
                link(po.tensor_tensor(aprod[:, :, :].rearrange("p s (h d) -> p s h d", d=HD), v, pr, ALU.mult))
                for s in range(1, T):
                    last = po.tensor_tensor(y[:, T - 1, :], aprod[:, 0, :] if s == 1 else y[:, T - 1, :], aprod[:, s, :],
                                            ALU.add)
                    if s < T - 1:
                        link(last)
                last.then_inc(y_ready, 1)

            for key in LN_ORDER:
                if key == ("at1", 0):
                    break
                if key == ("moe", 2):
                    class_values(0)
                if key[0] == "tile" and key[1] < NT - 2:
                    add_patch(key[1])
                if key in (("tile", NT - 3), ("tile", NT - 2)):
                    add_patch(key[1] + 1)
                root(key)
            for u in range(POOL_INTS):
                k, part = u // 2, slice((u % 2) * INNER, (u % 2 + 1) * INNER)
                po.wait_ge(scaledB, u + 1)
                w = ffw_sb[:, k, part]
                link(po.tensor_scalar(w, w, MAGIC, MAGIC + 1.0, ALU.add, ALU.min))
                po.tensor_scalar(ffq_sb[:, k, part], w, MAGIC - 1.0, MAGIC, ALU.max, ALU.subtract).then_inc(intB, 1)
            for j in range(2):
                root(("at1", j))

            def swap_halves(s):
                half = HD // 2
                v = qkv[:, s, 0:2 * P].rearrange("p (g d) -> p g d", d=HD)
                sin = cst_sb[:, C_SIN + HD * (s - 1):C_SIN + HD * s]
                if s > 2:
                    po.wait_ge(rot_used, s - 2)
                po.wait_ge(qkv_ready, T + s + 1)
                po.tensor_tensor(rot[:, s % 2, :, 0:half], v[:, :, half:HD], bc(sin[:, 0:half], 1, 2 * HH),
                                 ALU.mult).then_inc(rot_ready, 1)
                po.tensor_tensor(rot[:, s % 2, :, half:HD], v[:, :, 0:half], bc(sin[:, half:HD], 1, 2 * HH),
                                 ALU.mult).then_inc(rot_ready, 1)

            for s in range(1, T):
                if s == T - 1:
                    root(("at1", 2))
                swap_halves(s)
            for j in range(2):
                root(("ffn", j))
            class_values(1)
            root(("ffn", 2))

        @block.vector
        def _(ve):
            links = [0]

            def link(ins):
                links[0] += 1
                ins.then_inc(chain, 1)
                ve.wait_ge(chain, links[0])

            def chunks(b):
                return bank[b][:, 0:KC * P].rearrange("p (c n) -> p c n", c=KC)

            def ln_stats(key, src, r=P):
                i = LN[key]
                link(ve.bn_stats(stats[0:r, i, :], src))
                ve.bn_aggr(mv[0:r, i, :], stats[0:r, i, :]).then_inc(var_ready, 1)

            def ln_norm(key, dst, src, r=P):
                i = LN[key]
                ve.wait_ge(rstd_ready, i + 1)
                return ve.tensor_scalar(dst, src, mv[0:r, i, 0:1], rstd[0:r, i:i + 1], ALU.subtract, ALU.mult)

            def class_row():
                ve.wait_ge(ld_fr, 16)
                ln_stats(("cls", 0), fr[:, R_CLS, :])
                ve.tensor_tensor(clsb[:, :], fr[0:NB, R_CLS, :], fr[0:NB, R_GAP, :], ALU.add)
                ln_norm(("cls", 0), xh[:, 2, :], fr[:, R_CLS, :]).then_inc(xh_ready, 1)

            def stats_tile(i):
                ve.wait_ge(ev["conv"], i + 1)
                ln_stats(("tile", i), pe[:, i, :])

            def norm_tile(i):
                w, t = i // NPATCH, i % NPATCH
                ve.wait_ge(red_added, 8 * w + max(t, 1))
                ln_norm(("tile", i), pe[:, i, :], pe[:, i, :]).then_inc(norm_ready, 1)

            def query_stats(w):
                ve.wait_ge(red_added, 8 * w + 8)
                link(ve.tensor_scalar(red[:, w, :], red[:, w, :], 1.0 / NPATCH, None, ALU.mult))
                ln_stats(("q", w), red[:, w, :])

            def query_norm(w):
                ln_norm(("q", w), xh[:, w, :], red[:, w, :]).then_inc(xh_ready, 1)

            def class_query():
                ve.wait_ge(ev["gq"], 1)
                link(ve.tensor_tensor(gprod[:, :, :], tw[:, :, W_GKV:W_GKV + C], bc(gq[:, :], 1, KC), ALU.mult))
                ve.tensor_reduce(G[:, :, :], gprod[:, :, :].rearrange("p c (h d) -> p c h d", d=LD), AX.X,
                                 ALU.add).then_inc(g_ready, 1)

            def window_scores(g):
                w, t0 = g // 3, 3 * (g % 3)
                ve.wait_ge(ev["kv"], 3 * g + 3)
                ve.wait_ge(ev["q"], w + 1)
                k0 = 3 * (g % 2)
                link(ve.tensor_tensor(prod[:, t0:t0 + 3, :], kvb[:, k0:k0 + 3, :], bc(q_sb[:, w, :], 1, 3), ALU.mult
                                      ))
                ve.tensor_reduce(sc[:, t0:t0 + 3, :], prod[:, t0:t0 + 3, :].rearrange("p t (h d) -> p t h d", d=LD),
                                 AX.X, ALU.add).then_inc(scored, 1)
                ve.wait_ge(scored, g + 1)

            def window_softmax(w):
                m, z = msum[:, 0, :], msum[:, 1, :]
                by_head = sc[:, :, :].rearrange("p t h -> p h t")
                link(ve.tensor_reduce(m, by_head, AX.X, ALU.max))
                ve.tensor_tensor(sc[:, :, :], sc[:, :, :], bc(m, 1, NPATCH), ALU.subtract).then_inc(local_arg, 1)
                ve.wait_ge(local_exp, w + 1)
                link(ve.tensor_reduce(z, by_head, AX.X, ALU.add))
                link(ve.reciprocal(z, z))
                link(ve.tensor_tensor(sc[:, :, :], sc[:, :, :], bc(z, 1, NPATCH), ALU.mult))

            def weigh(t0, t1):
                return ve.tensor_tensor(prod[:, t0:t1, :].rearrange("p t (h d) -> p t h d", d=LD),
                                        kvb[:, 6 + t0:6 + t1, :].rearrange("p t (h d) -> p t h d", d=LD),
                                        bc(sc[:, t0:t1, :], 3, LD), ALU.mult)

            def window_values_first():
                ve.tensor_reduce(agg[:, :], prod[:, 0:NPATCH, :].rearrange("p t f -> p f t"), AX.X, ALU.add
                                 ).then_inc(agg_ready, 1)
                ve.wait_ge(agg_ready, 1)

            def window_values_second():
                ve.wait_ge(ev["kv"], 2 * NPATCH + 3)
                weigh(0, 3)
                ve.wait_ge(ev["kv"], 2 * NPATCH + 6)
                link(weigh(3, 6))
                link(ve.tensor_reduce(prod[:, NPATCH, :], prod[:, 0:6, :].rearrange("p t f -> p f t"), AX.X, ALU.add))
                ve.wait_ge(ev["kv"], 3 * NPATCH)
                link(weigh(6, NPATCH))
                ve.wait_ge(pe_step["aggT"], 1)
                ve.tensor_reduce(agg[:, :], prod[:, 6:NPATCH + 1, :].rearrange("p t f -> p f t"), AX.X, ALU.add
                                 ).then_inc(agg_ready, 1)

            def local_add(w):
                link(ve.tensor_tensor(red[:, w, :], red[:, w, :], fr[:, R_LAP, :], ALU.add))
                ve.wait_ge(pe_step["proj"], w + 1)
                ve.tensor_tensor(lo[:, w, :], bank[7][:, 0:C], red[:, w, :], ALU.add).then_inc(ev["proj"], 1)
                ve.wait_ge(ev["proj"], w + 1)
                ln_stats(("lo", w), lo[:, w, :])

            def local_norm(w):
                ve.wait_ge(pe_step["qT"], w + 1)
                ln_norm(("lo", w), xh[:, w, :], lo[:, w, :]).then_inc(xh_ready, 1)

            def trunk_rows(w):
                ve.wait_ge(pe_step["mod"], w + 1)
                ve.tensor_tensor(h[:, w, :], bank[7][:, 0:C], fr[:, R_MOD, :], ALU.add).then_inc(ev["mod"], 1)
                ve.wait_ge(ev["mod"], w + 1)
                ln_stats(("at0", w), h[:, w, :])

            def trunk_norm(w):
                if w == 0:
                    ve.wait_ge(pe_step["T"], NT)
                ln_norm(("at0", w), xn[:, w, :], h[:, w, :]).then_inc(xn_ready, 1)

            def scales_a():
                ve.wait_ge(pe_step["sumA"], 1)
                for i, w in enumerate((at0w_sb.shape, at0p_sb.shape)):
                    n = float(np.prod(w))
                    last = ve.tensor_scalar(wsc[:, i:i + 1], bank[7][:, i:i + 1], 1.0 / n, 1e-8, ALU.mult, ALU.max)
                link(last)
                link(ve.reciprocal(winv[:, 0:2], wsc[:, 0:2]))
                link(ve.tensor_scalar(wf[:, 0:1], wsc[:, 0:1], wsc[:, 0:1], HD ** -0.5, ALU.mult, ALU.mult))
                ve.tensor_tensor(wf[:, 1:2], wsc[:, 0:1], wsc[:, 1:2], ALU.mult).then_inc(ev["sumA"], 1)

            def clipped_integers(o, w, top):
                link(ve.tensor_scalar(w, w, MAGIC, MAGIC + top, ALU.add, ALU.min))
                return ve.tensor_scalar(o, w, MAGIC - top, MAGIC, ALU.max, ALU.subtract)

            def integers_a():
                for i, w in enumerate((at0w_flat, at0p_flat)):
                    link(ve.tensor_scalar(w, w, winv[:, i:i + 1], MAGIC, ALU.mult, ALU.add))
                    link(ve.tensor_scalar(w, w, MAGIC - 2.0, MAGIC + 2.0, ALU.max, ALU.min))
                    ve.tensor_scalar(w, w, MAGIC, None, ALU.subtract).then_inc(intA, 1)

            for i in range(NT):
                stats_tile(i)
                if i >= 2:
                    norm_tile(i - 2)
                if i == 8:
                    query_stats(0)
                    query_norm(0)
                if i == 10:
                    scales_a()
                if i == 11:
                    integers_a()
                if i == 12:
                    window_scores(0)
                    window_scores(1)
                if i == 13:
                    class_row()
                    window_scores(2)
                    window_softmax(0)
                    link(weigh(0, NPATCH))
                if i == 14:
                    window_values_first()
            norm_tile(NT - 2)
            query_stats(1)
            norm_tile(NT - 1)
            query_norm(1)
            local_add(0)
            local_norm(0)
            window_scores(3)
            window_scores(4)
            trunk_rows(0)
            window_scores(5)
            trunk_norm(0)
            window_softmax(1)
            window_values_second()
            class_query()
            local_add(1)
            local_norm(1)
            trunk_rows(1)
            trunk_norm(1)

            def rotate(s):
                v = qkv[:, s, 0:2 * P].rearrange("p (g d) -> p g d", d=HD)
                cos = cst_sb[:, C_COS + HD * (s - 1):C_COS + HD * s]
                ve.wait_ge(rot_ready, 2 * s)
                link(ve.tensor_tensor(v, v, bc(cos, 1, 2 * HH), ALU.mult))
                ve.tensor_tensor(v, v, rot[:, s % 2, :, :], ALU.add).then_inc(rot_used, 1)
                ve.wait_ge(rot_used, s)

            def score(layer, n, t):
                ve.wait_ge(qkv_ready, T * layer + n)
                if layer == 1 and t:
                    rotate(t)
                link(ve.tensor_tensor(aprod[:, 0:t + 1, :], qkv[:, 0:t + 1, P:2 * P],
                                      bc(qkv[:, t, 0:P], 1, t + 1), ALU.mult))
                link(ve.tensor_reduce(S[:, t, :, 0:t + 1].rearrange("p h s -> p s h"),
                                      aprod[:, 0:t + 1, :].rearrange("p s (h d) -> p s h d", d=HD), AX.X, ALU.add))

            def softmax_part(k):
                t0, t1 = ((0, 4), (4, 5))[k]
                return (S[:, t0:t1, :, :].rearrange("p t h s -> p (t h) s"),
                        S1[:, t0:t1, :].rearrange("p t h -> p (t h)"))

            def softmax_shift(k):
                rows, m = softmax_part(k)
                link(ve.tensor_reduce(m, rows, AX.X, ALU.max))
                ve.tensor_tensor(rows, rows, bc(m, 2, T), ALU.subtract).then_inc(at_arg, 1)

            def softmax_divide(layer, k):
                rows, m = softmax_part(k)
                ve.wait_ge(at_exp, 2 * layer + k + 1)
                link(ve.tensor_reduce(m, rows, AX.X, ALU.add))
                link(ve.reciprocal(m, m))
                return ve.tensor_tensor(rows, rows, bc(m, 2, T), ALU.mult)

            def values(layer, t):
                v = qkv[:, 0:t + 1, 2 * P:3 * P].rearrange("p s (h d) -> p s h d", d=HD)
                pr = bc(S[:, t, :, 0:t + 1].rearrange("p h s -> p s h"), 3, HD)
                link(ve.tensor_tensor(aprod[:, 0:t + 1, :].rearrange("p s (h d) -> p s h d", d=HD), v, pr, ALU.mult))
                ve.tensor_reduce(y[:, t, :], aprod[:, 0:t + 1, :].rearrange("p s f -> p f s"), AX.X, ALU.add
                                 ).then_inc(y_ready, 1)
                ve.wait_ge(y_ready, T * layer + t + 1)

            def add_attention(layer, j):
                r = ROWS[j]
                ve.wait_ge(ao_done, 3 * layer + j + 1)
                ve.scalar_tensor_tensor(h[0:r, j, :], bank[AO_BANK[layer][j]][0:r, 0:C],
                                        wf[0:r, 1:2] if layer == 0 else 1.0,
                                        h[0:r, j, :], ALU.mult, ALU.add).then_inc(h_ready, 1)
                ve.wait_ge(h_ready, 6 * layer + j + 1)
                ln_stats(("ffn" if layer else "moe", j), h[0:r, j, :], r)

            by_image = gsc[:, :, :].rearrange("h s b -> h b s")
            ve.wait_ge(consts_ready, 5)
            ve.wait_ge(ld_cst, 16)
            ve.wait_ge(pe_step["gs"], 1)
            link(ve.tensor_copy(gsc[:, :, :], bank[1][0:LH, 0:2 * P].rearrange("h (s b) -> h s b", s=4)))
            link(ve.tensor_reduce(gsm[:, 0, :], by_image, AX.X, ALU.max))
            ve.tensor_tensor(gsc[:, :, :], gsc[:, :, :], bc(gsm[:, 0, :], 1, 4), ALU.subtract).then_inc(garg, 1)
            score(0, 1, 0)
            link(ve.tensor_copy(identb[:, :], ident))
            score(0, 3, 1)
            score(0, 3, 2)
            score(0, 4, 3)
            softmax_shift(0)
            ve.wait_ge(gexp, 1)
            link(ve.tensor_reduce(gsm[:, 1, :], by_image, AX.X, ALU.add))
            link(softmax_divide(0, 0))
            for t in range(4):
                values(0, t)
            link(ve.reciprocal(gsm[:, 2, :], gsm[:, 1, :]))
            ve.tensor_tensor(gsc[:, :, :], gsc[:, :, :], bc(gsm[:, 2, :], 1, 4), ALU.mult).then_inc(gp_ready, 1)
            ve.wait_ge(pe_step["pT"], 1)
            ve.tensor_copy(gpt[:, :, :], bank[3][:, 0:2 * LH].rearrange("p (w h) -> p w h", w=2)).then_inc(ev["pT"], 1)
            ve.wait_ge(ev["pT"], 1)
            ve.wait_ge(pe_step["gv"], 1)
            ve.tensor_tensor(pgv[:, :, :].rearrange("p w (h d) -> p w h d", d=LD),
                             bank[4][:, :].rearrange("p (w h d) -> p w h d", w=2, d=LD),
                             bc(gpt[:, :, :], 3, LD), ALU.mult).then_inc(ev["pgv"], 1)
            add_attention(0, 0)
            add_attention(0, 1)

            def expert_norm(j):
                r = ROWS[j]
                ve.wait_ge(xnT_done, XN["at0", j] + 1)
                ln_norm(("moe", j), xn[0:r, j, :], h[0:r, j, :], r).then_inc(xn_ready, 1)

            def route(part):
                j0, j1 = ((0, 2), (2, 3))[part]
                n = j1 - j0
                idx = bc(cst_sb[:, C_IDX:C_IDX + E], 1, n)
                lgp = lg[:, j0:j1, :]
                prob, left, is_max, rank, pick = (rt[:, i, j0:j1] for i in range(5))
                m, z, best = (rs[:, i, j0:j1] for i in range(3))

                def shift():
                    ve.wait_ge(rt_done, part + 1)
                    if part:
                        link(ve.tensor_copy(lg[:, 2, :], bank[2][:, 0:E]))
                    else:
                        link(ve.tensor_copy(lgp, bank[3][:, 0:2 * E].rearrange("p (j e) -> p j e", j=2)))
                    link(ve.tensor_reduce(m, lgp, AX.X, ALU.max))
                    ve.tensor_tensor(lgp, lgp, bc(m, 2, E), ALU.subtract).then_inc(rt_arg, 1)

                def probabilities():
                    ve.wait_ge(rt_exp, part + 1)
                    link(ve.tensor_reduce(z, lgp, AX.X, ALU.add))
                    link(ve.reciprocal(z, z))
                    link(ve.tensor_tensor(prob, lgp, bc(z, 2, E), ALU.mult))

                def choose(k):
                    src = left if k else prob
                    link(ve.tensor_reduce(m, src, AX.X, ALU.max))
                    link(ve.tensor_tensor(is_max, src, bc(m, 2, E), ALU.is_ge))
                    link(ve.tensor_tensor(rank, is_max, idx, ALU.mult))
                    link(ve.tensor_reduce(best, rank, AX.X, ALU.max))
                    if k == 0:
                        link(ve.tensor_tensor(pick, idx, bc(best, 2, E), ALU.is_equal))
                        link(ve.scalar_tensor_tensor(left, pick, -2.0, prob, ALU.mult, ALU.add))
                    else:
                        link(ve.tensor_tensor(rank, idx, bc(best, 2, E), ALU.is_equal))
                        link(ve.tensor_tensor(pick, pick, rank, ALU.add))
                        link(ve.tensor_tensor(prob, prob, pick, ALU.mult))

                def split():
                    for k in range(3):
                        o = c3[:, j0:j1, k, :]
                        if k < 2:
                            link(ve.tensor_copy(o, prob))
                            link(ve.tensor_tensor(prob, prob, o, ALU.subtract))
                        else:
                            ve.tensor_copy(o, prob).then_inc(c3_ready, 1)

                def halves():
                    for e in range(2):
                        rows_ = slice(e * NB, (e + 1) * NB)
                        last = ve.tensor_scalar(cc[rows_, :], prob[rows_, 0, :].rearrange("p (k e) -> p e k", e=2)[:, e, :],
                                                0.5, None, ALU.mult)
                    last.then_inc(cc_ready, 1)

                return shift, probabilities, choose, halves if part else split

            def expert(i):
                a = act_a[:, i % 2, 0:NAB]
                ve.wait_ge(th_ready, i + 1)
                link(ve.scalar_tensor_tensor(a, th[:, i % 2, 0:NAB], 1.0, bank[4 + i % 2][:, 0:NAB], ALU.add, ALU.mult))
                ve.scalar_tensor_tensor(a, a, 0.5, bank[6 + i % 2][:, 0:NAB], ALU.mult, ALU.mult).then_inc(gu_used, 1)
                ve.wait_ge(gu_used, i + 1)
                if i >= 2:
                    ve.wait_ge(dn_done, i - 1)
                    if i == 2:
                        score(0, 5, 4)
                        softmax_shift(1)
                    ve.wait_ge(coef_done, i - 1)
                    if i == 2:
                        link(ve.tensor_scalar(wsc[:, 2:5], bank[3][:, 384:387], 1.0 / (C * INNER), 1e-5,
                                              ALU.mult, ALU.max))
                        ve.reciprocal(winv[:, 2:5], wsc[:, 2:5]).then_inc(scB_ready, 1)
                    ve.tensor_tensor(act_m[:, i % 2, 0:NAB], a, bank[3][:, 0:NAB], ALU.mult).then_inc(act_ready, 1)
                else:
                    ve.tensor_copy(act_m[:, i % 2, 0:NAB], a).then_inc(act_ready, 1)

            def class_expert(q):
                a, b = act_a[:, q % 2, NAB:NAB + P], bank[4 + q % 2]
                ve.wait_ge(cth_ready, q + 1)
                if q >= 2:
                    ve.wait_ge(chT_done, q - 1)
                link(ve.scalar_tensor_tensor(a, th[:, q % 2, NAB:NAB + P], 1.0, b[:, 0:P], ALU.add, ALU.mult))
                ve.scalar_tensor_tensor(a, a, cc[:, q - 1:q] if q else 0.5, b[:, P:2 * P], ALU.mult, ALU.mult
                                        ).then_inc(chid_ready, 1)

            def clear_scores():
                ve.wait_ge(y_ready, T)
                link(ve.memset(S[:, :, :, :], NEG))

            def integers_b(u):
                k, part = u // 2, slice((u % 2) * INNER, (u % 2 + 1) * INNER)
                ve.wait_ge(scaledB, u + 1)
                clipped_integers(ffq_sb[:, k, part], ffw_sb[:, k, part], 1.0).then_inc(intB, 1)

            def add_experts(j):
                r = ROWS[j]
                ve.wait_ge(acc_done, j + 1)
                ve.tensor_tensor(h[0:r, j, :], bank[j][0:r, 0:C], h[0:r, j, :], ALU.add).then_inc(h_ready, 1)
                ve.wait_ge(h_ready, 3 + j + 1)
                ln_stats(("at1", j), h[0:r, j, :], r)

            def attention_norm(j):
                r = ROWS[j]
                ln_norm(("at1", j), xn[0:r, j, :], h[0:r, j, :], r).then_inc(xn_ready, 1)

            expert_norm(0)
            expert_norm(1)
            ve.wait_ge(pe_step["cls"], 1)
            ve.tensor_tensor(h[0:NB, 2, :], bank[5][0:NB, C:2 * C], clsb[:, :], ALU.add).then_inc(ev["cls"], 1)
            ve.wait_ge(ev["cls"], 1)
            ln_stats(("at0", 2), h[0:NB, 2, :], NB)
            ln_norm(("at0", 2), xn[0:NB, 2, :], h[0:NB, 2, :], NB).then_inc(xn_ready, 1)
            expert(0)
            shift, probabilities, choose, split = route(0)
            shift()
            expert(1)
            probabilities()
            choose(0)
            choose(1)
            split()
            shift, probabilities, choose, halves = route(1)
            beside = {2: [lambda: softmax_divide(0, 1).then_inc(probs_ready, 1)],
                      5: [lambda: add_attention(0, 2)], 6: [lambda: expert_norm(2), clear_scores],
                      7: [shift], 8: [probabilities, lambda: choose(0)], 9: [lambda: choose(1), halves]}
            for i in range(2, NM):
                expert(i)
                for part in beside.get(i, []):
                    part()
            class_expert(0)
            ve.wait_ge(cc_ready, 1)
            class_expert(1)
            add_experts(0)
            add_experts(1)
            attention_norm(0)
            attention_norm(1)
            class_expert(2)
            class_expert(3)
            integers_b(1)
            integers_b(2)
            score(1, 1, 0)
            integers_b(3)
            score(1, 2, 1)
            class_expert(4)
            integers_b(4)
            integers_b(5)
            score(1, 3, 2)
            add_experts(2)
            score(1, 4, 3)
            softmax_shift(0)
            attention_norm(2)
            link(softmax_divide(1, 0))
            for t in range(4):
                values(1, t)
            score(1, 5, 4)
            softmax_shift(1)
            ve.memset(fx[:, 0, :], 1.0)
            add_attention(1, 0)
            add_attention(1, 1)
            softmax_divide(1, 1).then_inc(probs_ready, 1)

            amax, sx, unit, gscale, least, hsize, sh, fo = (fx[:, i] for i in range(8))

            def grid_tokens(j0, j1):
                cols = slice(j0, j1)
                for j in range(j0, j1):
                    r = ROWS[j]
                    ln_norm(("ffn", j), xn[0:r, j, :], h[0:r, j, :], r).then_inc(xn_ready, 1)
                for j in range(j0, j1):
                    r = ROWS[j]
                    ve.wait_ge(xn_ready, 9 + j + 1)
                    last = ve.tensor_reduce(amax[0:r, j:j + 1], xn[0:r, j, :], AX.X, ALU.max, apply_absolute_value=True)
                link(last)
                link(ve.tensor_scalar(amax[:, cols], amax[:, cols], 1.0 / 127.0, 1e-5 / 127.0, ALU.mult, ALU.max))
                link(ve.reciprocal(sx[:, cols], amax[:, cols]))
                for j in range(j0, j1):
                    r = ROWS[j]
                    ve.tensor_scalar(xn[0:r, j, :], xn[0:r, j, :], sx[0:r, j:j + 1], MAGIC, ALU.mult, ALU.add
                                     ).then_inc(xq_ready, 1)
                for j in range(j0, j1):
                    ve.tensor_scalar(gscale[:, j:j + 1], amax[:, j:j + 1], wsc[:, 2:3], None, ALU.mult
                                     ).then_inc(tscale_ready, 1)
                    last = ve.tensor_scalar(unit[:, j:j + 1], amax[:, j:j + 1], wsc[:, 3:4], None, ALU.mult)
                return last

            def least_sizes(j0, j1, units):
                cols = slice(j0, j1)
                link(units)
                link(ve.reciprocal(least[:, cols], unit[:, cols]))
                link(ve.tensor_scalar(least[:, cols], least[:, cols], 1e-5 / 127.0, None, ALU.mult))

            def ff_act(k):
                j, half = k // 2, k % 2
                r = ROWS[j]
                ve.wait_ge(fth_ready, k + 1)
                if j == 2:
                    ve.wait_ge(hqT_done, 2)
                o = hm[0:r, j % 2, half * 512:(half + 1) * 512]
                ve.tensor_tensor(o, th[0:r, k % 2, :], bank[2 + k % 2][0:r, :], ALU.mult).then_inc(fg_used, 1)

            def ff_scale(j):
                r = ROWS[j]
                col = slice(j, j + 1)
                ve.wait_ge(fg_used, 2 * j + 2)
                link(ve.tensor_reduce(hmx[0:r, col], hm[0:r, j % 2, :], AX.X, ALU.max, apply_absolute_value=True))
                link(ve.tensor_scalar(hsize[0:r, col], hmx[0:r, col], 1.0 / 127.0, least[0:r, col], ALU.mult, ALU.max))
                if j < 2:
                    ve.reciprocal(sh[0:r, col], hsize[0:r, col]).then_inc(hq_ready, 1)
                else:
                    link(ve.reciprocal(sh[0:r, col], hsize[0:r, col]))
                    for half in range(2):
                        o = hm[0:r, 0, half * 512:(half + 1) * 512]
                        ve.tensor_scalar(o, o, sh[0:r, col], MAGIC, ALU.mult, ALU.add).then_inc(last_hs_ready, 1)
                link(ve.tensor_scalar(fo[0:r, col], hsize[0:r, col], unit[0:r, col], wsc[0:r, 4:5], ALU.mult, ALU.mult))

            def ff_out(j):
                r = ROWS[j]
                ve.wait_ge(fd_done, j + 1)
                ve.scalar_tensor_tensor(h[0:r, j, :], bank[6 + j % 2][0:r, 0:C], fo[0:r, j:j + 1], h[0:r, j, :],
                                        ALU.mult, ALU.add).then_inc(h_ready, 1)

            grid_tokens(0, 1)
            least_sizes(0, 2, grid_tokens(1, 2))
            ff_act(0)
            ff_act(1)
            ff_scale(0)
            add_attention(1, 2)
            ff_act(2)
            least_sizes(2, 3, grid_tokens(2, 3))
            ff_act(3)
            ff_scale(1)
            ff_out(0)
            ff_act(4)
            ff_act(5)
            ff_scale(2)
            ff_out(1)
            ff_out(2)


def kernel(**inputs):
    import ml_dtypes
    import concourse.bacc as _bacc
    from concourse.bass_utils import run_bass_kernel_spmd as _run

    a = {k: np.asarray(v) for k, v in inputs.items()}

    def rows(w):
        return w.reshape(w.shape[0] // P, P, w.shape[1]).transpose(1, 0, 2)

    xk = a["x"].reshape(NB, 3, 2, 3, 14, 2, 3, 14).transpose(1, 4, 7, 5, 3, 6, 2, 0).reshape(CONV_K, NT * P)
    cw = a["L0_tok_conv_w"].reshape(C, CONV_K).T
    xk, cw = (np.concatenate([m, np.zeros((CK * CP - CONV_K, m.shape[1]), m.dtype)]) for m in (xk, cw))
    t = lambda n: a["L0_tok_" + n]
    tokw = rows(np.concatenate([t("la_wq"), t("la_wkv"), t("la_proj_w"), t("mod_w"), t("ga_wq"), t("ga_wkv"),
                                t("ga_proj_w")], axis=1))
    fcols = np.stack([t(n) for n in ("la_ln_q_g", "la_ln_q_b", "la_ln_kv_g", "la_ln_kv_b", "ga_ln_q_g", "ga_ln_q_b",
                                     "ga_ln_kv_g", "ga_ln_kv_b")]).reshape(8, KC, P).transpose(2, 0, 1)
    frows = np.stack([t("la_proj_b"), t("ga_proj_b"), t("mod_b"), t("class_emb")])

    def halves(w):
        return rows(w.T.reshape(C, 3, 2, P).transpose(0, 2, 1, 3).reshape(C, 6 * P)).reshape(P, KC, 2, 3 * P)

    at1 = np.concatenate([a["L1_attn_Wq"], a["L1_attn_Wk"], a["L1_attn_Wv"]])
    eg, eu = (a["L0_ffn_experts_" + n].transpose(1, 0, 2) for n in ("gate", "up"))
    sg, su = (a["L0_ffn_shared_" + n].reshape(C, 2, P) for n in ("gate", "up"))
    gu = np.stack([np.concatenate([eg, sg], axis=1), np.concatenate([eu, su], axis=1)], axis=2)
    moe_gu = gu.reshape(KC, P, NM, 2, P).transpose(1, 2, 3, 0, 4)
    moe_d = np.concatenate([a["L0_ffn_experts_down"], a["L0_ffn_shared_down"].reshape(2, P, C)]).transpose(1, 0, 2)

    cst = np.zeros((P, C_END), np.float32)
    cst[:, C_ID:C_ID + P] = np.eye(P)
    cst[:, C_FOLD:C_FOLD + NB] = np.tile(np.eye(NB), (2, 1))
    cst[:, C_IDX:C_IDX + E] = np.arange(E, 0, -1)
    freq = (1.0 / np.float32(10000.0) ** (np.arange(0, HD, 2, dtype=np.float32) / HD)).astype(np.float32)
    ang = np.arange(1, T, dtype=np.float32)[:, None] * freq[None, :]
    cst[:, C_COS:C_SIN] = np.concatenate([np.cos(ang), np.cos(ang)], axis=1).reshape(1, -1)
    cst[:, C_SIN:C_END] = np.concatenate([-np.sin(ang), np.sin(ang)], axis=1).reshape(1, -1)
    sel = np.zeros((3 * E, E, P), ml_dtypes.bfloat16)
    for k in range(3 * E):
        sel[k, k % E, :] = 1

    ins = {"xk": xk, "cw": cw, "cst": cst, "sel": sel, "fcols": fcols, "frows": frows, "tokw": tokw,
           "at0w": halves(a["L0_attn_w_attn"]), "at0p": rows(a["L0_attn_w_proj"].T), "router": rows(a["L0_ffn_router"]),
           "moe_gu": moe_gu, "moe_d": moe_d, "at1w": halves(at1), "at1p": rows(a["L1_attn_Wo"].T),
           "ffg": rows(a["L1_ffn_w_gate"].T).reshape(P, -1), "ffu": rows(a["L1_ffn_w_up"].T).reshape(P, -1),
           "ffd": rows(a["L1_ffn_w_down"].T).reshape(P, -1)}
    nc = _bacc.Bacc("TRN2", target_bir_lowering=False, num_devices=1)
    arrays, args = {}, []
    for name, v in ins.items():
        v = np.ascontiguousarray(v)
        arrays[f"in_{name}"] = v
        args.append(nc.dram_tensor(f"in_{name}", v.shape, mybir.dt.from_np(v.dtype), kind="ExternalInput").ap())
    out = nc.dram_tensor("out_0", (NB, T, C), F32, kind="ExternalOutput").ap()
    vit_tower(nc, *args, out)
    r = _run(nc, [arrays], core_ids=[0])
    return r.results[0]["out_0"]
```
